# Optimizing a Trainium2 kernel written in Bass

```python
import numpy as np
import jax
import jax.numpy as jnp

def _softmax(x, axis=-1):
    return jax.nn.softmax(x, axis=axis)

def _gelu(x):
    return jax.nn.gelu(x, approximate=True)

def _silu(x):
    return jax.nn.silu(x)

def _sigmoid(x):
    return jax.nn.sigmoid(x)

def _layernorm(x, axis=-1, eps=1e-05):
    m = jnp.mean(x, axis=axis, keepdims=True)
    v = jnp.var(x, axis=axis, keepdims=True)
    return (x - m) / jnp.sqrt(v + eps)

def _scatter_add(tgt, idx, src, axis=0):
    return tgt.at[idx].add(src)

def _segment_sum(src, seg, n):
    return jax.ops.segment_sum(src, seg, n)
kernel_name = 'mk_adaln_d2_jaxref_r8_c6f0e7'

def setup_inputs(seed: int=0):
    np.random.seed(seed)
    _w = jnp.asarray

    def _L0_attn_setup():
        import jax, jax.numpy as jnp
        import numpy as np
        import math
        EMBED_DIM = 128
        NDIM = 2
        SCALE = math.sqrt(1.0 / NDIM)

        def _ema_kernel(delta, alpha, beta, gamma, length):
            p = jax.nn.sigmoid(delta)
            a = jax.nn.sigmoid(alpha)
            q = 1.0 - p * a
            t = jnp.arange(length, dtype=q.dtype)
            vander = t[None, None, :] * jnp.log(q)
            kernel = p * beta * jnp.exp(vander)
            return jnp.einsum('dnl,dn->dl', kernel, gamma * SCALE)
        key = jax.random.key(seed)
        ks = jax.random.split(key, 6)
        B, S, D, N = (4, 1024, EMBED_DIM, NDIM)
        x = jax.random.normal(ks[0], (B, S, D), dtype=jnp.float32)
        delta = 0.2 * jax.random.normal(ks[1], (D, N, 1), dtype=jnp.float32)
        alpha = 0.2 * jax.random.normal(ks[2], (D, N, 1), dtype=jnp.float32)
        val = jnp.where(jnp.arange(N) % 2 == 1, -1.0, 1.0).reshape(N, 1).astype(jnp.float32)
        beta = 0.02 * jax.random.normal(ks[3], (D, N, 1), dtype=jnp.float32) + val
        gamma = jax.random.normal(ks[4], (D, N), dtype=jnp.float32)
        omega = jax.random.normal(ks[5], (D,), dtype=jnp.float32)
        return {'x': x, 'delta': delta, 'alpha': alpha, 'beta': beta, 'gamma': gamma, 'omega': omega}
    _L0_attn_in = _L0_attn_setup()

    def _L0_ffn_setup():
        import jax, jax.numpy as jnp
        import numpy as np
        EPS = 1e-05
        HEADS = 8
        DIM_KEY = 128
        K = 16
        NUM_KEYS = 32
        key = jax.random.key(seed)
        ks = jax.random.split(key, 5)
        B, T, D = (1, 128, 128)
        x = jax.random.normal(ks[0], (B, T, D), dtype=jnp.float32)
        norm_w = jnp.ones((D,), dtype=jnp.float32)
        wq = jax.random.normal(ks[1], (D, DIM_KEY * HEADS * 2), dtype=jnp.float32) * 0.02
        keys = jax.random.normal(ks[2], (HEADS, NUM_KEYS, 2, DIM_KEY), dtype=jnp.float32) * 0.02
        expert_down = jax.random.normal(ks[3], (NUM_KEYS * NUM_KEYS, D), dtype=jnp.float32) * 0.02
        expert_up = jax.random.normal(ks[4], (NUM_KEYS * NUM_KEYS, D), dtype=jnp.float32) * 0.02
        return {'x': x, 'norm_w': norm_w, 'wq': wq, 'keys': keys, 'expert_down': expert_down, 'expert_up': expert_up}
    _L0_ffn_in = _L0_ffn_setup()
    _L0_c = _w((lambda *s: np.random.randn(*s).astype(np.float32) * 0.05)(1, 128))
    _L0_wmod = _w((lambda *s: np.random.randn(*s).astype(np.float32) * 0.05)(128, 6 * 128) * 128 ** (-0.5))

    def _L1_attn_setup():
        import jax, jax.numpy as jnp
        import numpy as np
        N_EMBD = 128
        BLOCK_SIZE = 256
        ATTN_SPAN = 32
        LN_EPS = 1e-05

        def _band_mask(T, span, dtype):
            ones = jnp.ones((T, T), dtype=dtype)
            return jnp.tril(ones, 0) * (1.0 - jnp.tril(ones, -span))

        def _layer_norm(h, w, b):
            mu = jnp.mean(h, axis=-1, keepdims=True)
            var = jnp.var(h, axis=-1, keepdims=True)
            return (h - mu) * jax.lax.rsqrt(var + LN_EPS) * w + b
        key = jax.random.key(seed)
        k_x, k_w, k_b, k_lw = jax.random.split(key, 4)
        B, T, C = (4, BLOCK_SIZE, N_EMBD)
        x = jax.random.normal(k_x, (B, T, C), dtype=jnp.float32)
        lim = 1.0 / np.sqrt(C)
        W_qkv = jax.random.uniform(k_w, (C, 3 * C), minval=-lim, maxval=lim, dtype=jnp.float32)
        b_qkv = jax.random.uniform(k_b, (3 * C,), minval=-lim, maxval=lim, dtype=jnp.float32)
        ln_w = jnp.ones((C,), dtype=jnp.float32)
        ln_b = jnp.zeros((C,), dtype=jnp.float32)
        return {'x': x, 'W_qkv': W_qkv, 'b_qkv': b_qkv, 'ln_w': ln_w, 'ln_b': ln_b}
    _L1_attn_in = _L1_attn_setup()

    def _L1_ffn_setup():
        import jax, jax.numpy as jnp
        import numpy as np
        DIM = 128
        DEPTH = 2
        HEADS = 8
        DIM_HEAD = 64
        WINDOW = 64
        INNER = HEADS * DIM_HEAD
        HID = int(DIM * 4 * 2 / 3)
        B, N = (2, 1024)
        QK_SCALE = 8.0

        def shift_token(t):
            t1, t2 = jnp.split(t, 2, axis=-1)
            t2 = jnp.pad(t2, ((0, 0), (1, 0), (0, 0)))[:, :-1]
            return jnp.concatenate([t1, t2], axis=-1)

        def l2norm(t):
            return t / jnp.clip(jnp.linalg.norm(t, axis=-1, keepdims=True), 1e-12)

        def rotate_half(x):
            x1, x2 = jnp.split(x, 2, axis=-1)
            return jnp.concatenate([-x2, x1], axis=-1)

        def rotary_xpos(q, k):
            n = q.shape[-2]
            half_idx = jnp.arange(0, DIM_HEAD, 2, dtype=jnp.float32)
            inv_freq = 1.0 / 10000.0 ** (half_idx / DIM_HEAD)
            t = jnp.arange(n, dtype=jnp.float32)
            freqs = t[:, None] * inv_freq[None, :]
            freqs = jnp.concatenate([freqs, freqs], axis=-1)
            base = (half_idx + 0.4 * DIM_HEAD) / (1.4 * DIM_HEAD)
            power = (t - n // 2) / float(WINDOW // 2)
            scale = base[None, :] ** power[:, None]
            scale = jnp.concatenate([scale, scale], axis=-1)
            cos, sin = (jnp.cos(freqs), jnp.sin(freqs))
            q = q * cos * scale + rotate_half(q) * sin * scale
            k = k * cos / scale + rotate_half(k) * sin / scale
            return (q, k)

        def local_attention(q, k, v):
            b, h, n, d = q.shape
            w = n // WINDOW
            bq = q.reshape(b, h, w, WINDOW, d) * QK_SCALE
            bk = k.reshape(b, h, w, WINDOW, d)
            bv = v.reshape(b, h, w, WINDOW, d)

            def look_around(t):
                p = jnp.pad(t, ((0, 0), (0, 0), (1, 0), (0, 0), (0, 0)))
                return jnp.concatenate([p[:, :, :w], p[:, :, 1:]], axis=3)
            bk, bv = (look_around(bk), look_around(bv))
            bt = jnp.arange(n).reshape(w, WINDOW)
            btp = jnp.pad(bt, ((1, 0), (0, 0)), constant_values=-1)
            btk = jnp.concatenate([btp[:w], btp[1:]], axis=1)
            sim = jnp.einsum('bhwid,bhwjd->bhwij', bq, bk)
            i = bt[:, :, None]
            j = btk[:, None, :]
            mask = (i < j) | (i > j + WINDOW) | (j == -1)
            sim = jnp.where(mask, -jnp.finfo(sim.dtype).max, sim)
            attn = jax.nn.softmax(sim, axis=-1)
            out = jnp.einsum('bhwij,bhwjd->bhwid', attn, bv)
            return out.reshape(b, h, n, d)

        def _layer(x, wqkv, qs, ksc, wo, lg, lb, w1, b1, w2, b2):
            b, n, _ = x.shape
            h = shift_token(x)
            qkv = h @ wqkv
            q, k, v = jnp.split(qkv, 3, axis=-1)
            to_heads = lambda t: t.reshape(b, n, HEADS, DIM_HEAD).transpose(0, 2, 1, 3)
            q, k, v = (to_heads(q), to_heads(k), to_heads(v))
            q = l2norm(q) * qs
            k = l2norm(k) * ksc
            q, k = rotary_xpos(q, k)
            o = local_attention(q, k, v)
            o = o.transpose(0, 2, 1, 3).reshape(b, n, INNER)
            x = x + o @ wo
            h = shift_token(x)
            mu = h.mean(-1, keepdims=True)
            var = h.var(-1, keepdims=True)
            h = (h - mu) / jnp.sqrt(var + 1e-05) * lg + lb
            h = h @ w1 + b1
            a, g = jnp.split(h, 2, axis=-1)
            h = a * jax.nn.gelu(g, approximate=False)
            x = x + h @ w2 + b2
            return x
        key = jax.random.key(seed)
        ks = jax.random.split(key, 6)
        return {'x': jax.random.normal(ks[0], (B, N, DIM), jnp.float32), 'wqkv': jax.random.normal(ks[1], (DEPTH, DIM, 3 * INNER), jnp.float32) * 0.02, 'q_scale': jnp.ones((DEPTH, DIM_HEAD), jnp.float32), 'k_scale': jnp.ones((DEPTH, DIM_HEAD), jnp.float32), 'wo': jax.random.normal(ks[2], (DEPTH, INNER, DIM), jnp.float32) * 0.02, 'ln_g': jnp.ones((DEPTH, DIM), jnp.float32), 'ln_b': jnp.zeros((DEPTH, DIM), jnp.float32), 'w1': jax.random.normal(ks[3], (DEPTH, DIM, 2 * HID), jnp.float32) * 0.02, 'b1': jnp.zeros((DEPTH, 2 * HID), jnp.float32), 'w2': jax.random.normal(ks[4], (DEPTH, HID, DIM), jnp.float32) * 0.02, 'b2': jnp.zeros((DEPTH, DIM), jnp.float32)}
    _L1_ffn_in = _L1_ffn_setup()
    _L1_c = _w((lambda *s: np.random.randn(*s).astype(np.float32) * 0.05)(1, 128))
    _L1_wmod = _w((lambda *s: np.random.randn(*s).astype(np.float32) * 0.05)(128, 6 * 128) * 128 ** (-0.5))
    _d = {'L0_attn_x': _L0_attn_in['x'], 'L0_attn_delta': _L0_attn_in['delta'], 'L0_attn_alpha': _L0_attn_in['alpha'], 'L0_attn_beta': _L0_attn_in['beta'], 'L0_attn_gamma': _L0_attn_in['gamma'], 'L0_attn_omega': _L0_attn_in['omega'], 'L0_ffn_norm_w': _L0_ffn_in['norm_w'], 'L0_ffn_wq': _L0_ffn_in['wq'], 'L0_ffn_keys': _L0_ffn_in['keys'], 'L0_ffn_expert_down': _L0_ffn_in['expert_down'], 'L0_ffn_expert_up': _L0_ffn_in['expert_up'], 'L0_c': _L0_c, 'L0_wmod': _L0_wmod, 'L1_attn_W_qkv': _L1_attn_in['W_qkv'], 'L1_attn_b_qkv': _L1_attn_in['b_qkv'], 'L1_attn_ln_w': _L1_attn_in['ln_w'], 'L1_attn_ln_b': _L1_attn_in['ln_b'], 'L1_ffn_wqkv': _L1_ffn_in['wqkv'], 'L1_ffn_q_scale': _L1_ffn_in['q_scale'], 'L1_ffn_k_scale': _L1_ffn_in['k_scale'], 'L1_ffn_wo': _L1_ffn_in['wo'], 'L1_ffn_ln_g': _L1_ffn_in['ln_g'], 'L1_ffn_ln_b': _L1_ffn_in['ln_b'], 'L1_ffn_w1': _L1_ffn_in['w1'], 'L1_ffn_b1': _L1_ffn_in['b1'], 'L1_ffn_w2': _L1_ffn_in['w2'], 'L1_ffn_b2': _L1_ffn_in['b2'], 'L1_c': _L1_c, 'L1_wmod': _L1_wmod}
    _x0 = _d['L0_attn_x']
    _d['L0_attn_x'] = jax.random.normal(jax.random.fold_in(jax.random.key(seed), 1), (1, 2048, 128), dtype=_x0.dtype)
    del _x0
    return _d

def reference(L0_attn_x, L0_attn_delta, L0_attn_alpha, L0_attn_beta, L0_attn_gamma, L0_attn_omega, L0_ffn_norm_w, L0_ffn_wq, L0_ffn_keys, L0_ffn_expert_down, L0_ffn_expert_up, L0_c, L0_wmod, L1_attn_W_qkv, L1_attn_b_qkv, L1_attn_ln_w, L1_attn_ln_b, L1_ffn_wqkv, L1_ffn_q_scale, L1_ffn_k_scale, L1_ffn_wo, L1_ffn_ln_g, L1_ffn_ln_b, L1_ffn_w1, L1_ffn_b1, L1_ffn_w2, L1_ffn_b2, L1_c, L1_wmod):

    def _L0_attn_ref(x, delta, alpha, beta, gamma, omega):
        import jax, jax.numpy as jnp
        import numpy as np
        import math
        EMBED_DIM = 128
        NDIM = 2
        SCALE = math.sqrt(1.0 / NDIM)

        def _ema_kernel(delta, alpha, beta, gamma, length):
            p = jax.nn.sigmoid(delta)
            a = jax.nn.sigmoid(alpha)
            q = 1.0 - p * a
            t = jnp.arange(length, dtype=q.dtype)
            vander = t[None, None, :] * jnp.log(q)
            kernel = p * beta * jnp.exp(vander)
            return jnp.einsum('dnl,dn->dl', kernel, gamma * SCALE)
        B, S, D = x.shape
        residual = x * omega
        xt = jnp.transpose(x, (0, 2, 1))
        k = _ema_kernel(delta, alpha, beta, gamma, S)
        n = 2 * S
        k_f = jnp.fft.rfft(k.astype(jnp.float32), n=n)
        x_f = jnp.fft.rfft(xt.astype(jnp.float32), n=n)
        out = jnp.fft.irfft(x_f * k_f, n=n)[..., :S]
        out = out.astype(x.dtype)
        return jax.nn.silu(jnp.transpose(out, (0, 2, 1)) + residual)

    def _L0_ffn_ref(x, norm_w, wq, keys, expert_down, expert_up):
        import jax, jax.numpy as jnp
        import numpy as np
        EPS = 1e-05
        HEADS = 8
        DIM_KEY = 128
        K = 16
        NUM_KEYS = 32
        B, T, D = x.shape
        inv = jax.lax.rsqrt(jnp.mean(x * x, axis=-1, keepdims=True) + EPS)
        x_norm = x * inv * norm_w
        q = (x_norm @ wq).reshape(B, T, HEADS, 2, DIM_KEY)
        sim = jnp.einsum('bthpd,hkpd->pbthk', q, keys)
        s1, i1 = jax.lax.top_k(sim[0], K)
        s2, i2 = jax.lax.top_k(sim[1], K)
        all_idx = (i1[..., :, None] * NUM_KEYS + i2[..., None, :]).reshape(B, T, HEADS, K * K)
        all_scores = (s1[..., :, None] + s2[..., None, :]).reshape(B, T, HEADS, K * K)
        final_scores, pk = jax.lax.top_k(all_scores, K)
        final_idx = jnp.take_along_axis(all_idx, pk, axis=-1)
        wd = expert_down[final_idx]
        wu = expert_up[final_idx]
        hidden = jnp.einsum('btd,bthkd->bthk', x_norm, wd)
        hidden = jax.nn.gelu(hidden, approximate=False)
        hidden = hidden * jax.nn.relu(final_scores)
        out = jnp.einsum('bthk,bthkd->btd', hidden, wu)
        return out

    def _L1_attn_ref(x, W_qkv, b_qkv, ln_w, ln_b):
        import jax, jax.numpy as jnp
        import numpy as np
        N_EMBD = 128
        BLOCK_SIZE = 256
        ATTN_SPAN = 32
        LN_EPS = 1e-05

        def _band_mask(T, span, dtype):
            ones = jnp.ones((T, T), dtype=dtype)
            return jnp.tril(ones, 0) * (1.0 - jnp.tril(ones, -span))

        def _layer_norm(h, w, b):
            mu = jnp.mean(h, axis=-1, keepdims=True)
            var = jnp.var(h, axis=-1, keepdims=True)
            return (h - mu) * jax.lax.rsqrt(var + LN_EPS) * w + b
        B, T, C = x.shape
        qkv = x @ W_qkv + b_qkv
        q, k, v = jnp.split(qkv, 3, axis=-1)
        scale = np.sqrt(C * ATTN_SPAN).astype(np.float32)
        scores = jnp.einsum('bid,bjd->bij', q, k) / scale
        scores = scores * _band_mask(T, ATTN_SPAN, x.dtype)[None, :, :]
        out = jnp.einsum('bij,bjd->bid', scores, v)
        return _layer_norm(out, ln_w, ln_b)

    def _L1_ffn_ref(x, wqkv, q_scale, k_scale, wo, ln_g, ln_b, w1, b1, w2, b2):
        import jax, jax.numpy as jnp
        import numpy as np
        DIM = 128
        DEPTH = 2
        HEADS = 8
        DIM_HEAD = 64
        WINDOW = 64
        INNER = HEADS * DIM_HEAD
        HID = int(DIM * 4 * 2 / 3)
        B, N = (2, 1024)
        QK_SCALE = 8.0

        def shift_token(t):
            t1, t2 = jnp.split(t, 2, axis=-1)
            t2 = jnp.pad(t2, ((0, 0), (1, 0), (0, 0)))[:, :-1]
            return jnp.concatenate([t1, t2], axis=-1)

        def l2norm(t):
            return t / jnp.clip(jnp.linalg.norm(t, axis=-1, keepdims=True), 1e-12)

        def rotate_half(x):
            x1, x2 = jnp.split(x, 2, axis=-1)
            return jnp.concatenate([-x2, x1], axis=-1)

        def rotary_xpos(q, k):
            n = q.shape[-2]
            half_idx = jnp.arange(0, DIM_HEAD, 2, dtype=jnp.float32)
            inv_freq = 1.0 / 10000.0 ** (half_idx / DIM_HEAD)
            t = jnp.arange(n, dtype=jnp.float32)
            freqs = t[:, None] * inv_freq[None, :]
            freqs = jnp.concatenate([freqs, freqs], axis=-1)
            base = (half_idx + 0.4 * DIM_HEAD) / (1.4 * DIM_HEAD)
            power = (t - n // 2) / float(WINDOW // 2)
            scale = base[None, :] ** power[:, None]
            scale = jnp.concatenate([scale, scale], axis=-1)
            cos, sin = (jnp.cos(freqs), jnp.sin(freqs))
            q = q * cos * scale + rotate_half(q) * sin * scale
            k = k * cos / scale + rotate_half(k) * sin / scale
            return (q, k)

        def local_attention(q, k, v):
            b, h, n, d = q.shape
            w = n // WINDOW
            bq = q.reshape(b, h, w, WINDOW, d) * QK_SCALE
            bk = k.reshape(b, h, w, WINDOW, d)
            bv = v.reshape(b, h, w, WINDOW, d)

            def look_around(t):
                p = jnp.pad(t, ((0, 0), (0, 0), (1, 0), (0, 0), (0, 0)))
                return jnp.concatenate([p[:, :, :w], p[:, :, 1:]], axis=3)
            bk, bv = (look_around(bk), look_around(bv))
            bt = jnp.arange(n).reshape(w, WINDOW)
            btp = jnp.pad(bt, ((1, 0), (0, 0)), constant_values=-1)
            btk = jnp.concatenate([btp[:w], btp[1:]], axis=1)
            sim = jnp.einsum('bhwid,bhwjd->bhwij', bq, bk)
            i = bt[:, :, None]
            j = btk[:, None, :]
            mask = (i < j) | (i > j + WINDOW) | (j == -1)
            sim = jnp.where(mask, -jnp.finfo(sim.dtype).max, sim)
            attn = jax.nn.softmax(sim, axis=-1)
            out = jnp.einsum('bhwij,bhwjd->bhwid', attn, bv)
            return out.reshape(b, h, n, d)

        def _layer(x, wqkv, qs, ksc, wo, lg, lb, w1, b1, w2, b2):
            b, n, _ = x.shape
            h = shift_token(x)
            qkv = h @ wqkv
            q, k, v = jnp.split(qkv, 3, axis=-1)
            to_heads = lambda t: t.reshape(b, n, HEADS, DIM_HEAD).transpose(0, 2, 1, 3)
            q, k, v = (to_heads(q), to_heads(k), to_heads(v))
            q = l2norm(q) * qs
            k = l2norm(k) * ksc
            q, k = rotary_xpos(q, k)
            o = local_attention(q, k, v)
            o = o.transpose(0, 2, 1, 3).reshape(b, n, INNER)
            x = x + o @ wo
            h = shift_token(x)
            mu = h.mean(-1, keepdims=True)
            var = h.var(-1, keepdims=True)
            h = (h - mu) / jnp.sqrt(var + 1e-05) * lg + lb
            h = h @ w1 + b1
            a, g = jnp.split(h, 2, axis=-1)
            h = a * jax.nn.gelu(g, approximate=False)
            x = x + h @ w2 + b2
            return x
        for l in range(DEPTH):
            x = _layer(x, wqkv[l], q_scale[l], k_scale[l], wo[l], ln_g[l], ln_b[l], w1[l], b1[l], w2[l], b2[l])
        return x
    x = L0_attn_x
    mod = (_silu(L0_c) @ L0_wmod).reshape(L0_c.shape[0], 6, 1, -1)
    sa, ca, ga, sb, cb, gb = (mod[:, 0], mod[:, 1], mod[:, 2], mod[:, 3], mod[:, 4], mod[:, 5])
    ga = (2 * (ga >= 0) - 1) * jnp.maximum(jnp.abs(ga), 0.25)
    gb = (2 * (gb >= 0) - 1) * jnp.maximum(jnp.abs(gb), 0.25)
    h = _layernorm(x, axis=-1) * (1 + ca) + sa
    x = x + ga * _L0_attn_ref(h, L0_attn_delta, L0_attn_alpha, L0_attn_beta, L0_attn_gamma, L0_attn_omega)
    h = _layernorm(x, axis=-1) * (1 + cb) + sb
    x = x + gb * _L0_ffn_ref(h, L0_ffn_norm_w, L0_ffn_wq, L0_ffn_keys, L0_ffn_expert_down, L0_ffn_expert_up)
    mod = (_silu(L1_c) @ L1_wmod).reshape(L1_c.shape[0], 6, 1, -1)
    sa, ca, ga, sb, cb, gb = (mod[:, 0], mod[:, 1], mod[:, 2], mod[:, 3], mod[:, 4], mod[:, 5])
    ga = (2 * (ga >= 0) - 1) * jnp.maximum(jnp.abs(ga), 0.25)
    gb = (2 * (gb >= 0) - 1) * jnp.maximum(jnp.abs(gb), 0.25)
    h = _layernorm(x, axis=-1) * (1 + ca) + sa
    x = x + ga * _L1_attn_ref(h, L1_attn_W_qkv, L1_attn_b_qkv, L1_attn_ln_w, L1_attn_ln_b)
    h = _layernorm(x, axis=-1) * (1 + cb) + sb
    x = x + gb * _L1_ffn_ref(h, L1_ffn_wqkv, L1_ffn_q_scale, L1_ffn_k_scale, L1_ffn_wo, L1_ffn_ln_g, L1_ffn_ln_b, L1_ffn_w1, L1_ffn_b1, L1_ffn_w2, L1_ffn_b2)
    return x

_drawn_inputs = setup_inputs


def setup_inputs(seed=0):
    import zlib

    import numpy as np

    out = dict(_drawn_inputs(seed))
    spreads = {'L0_ffn_norm_w': (1.0, 0.6),
     'L1_attn_ln_w': (1.0, 0.6),
     'L1_attn_ln_b': (0.0, 0.923),
     'L1_ffn_q_scale': (1.0, 0.6),
     'L1_ffn_k_scale': (1.0, 0.6),
     'L1_ffn_ln_g': (1.0, 0.6),
     'L1_ffn_ln_b': (0.0, 0.8),
     'L1_ffn_b1': (0.0, 0.8),
     'L1_ffn_b2': (0.0, 0.8)}
    factors = {'L0_attn_delta': 5.511,
     'L0_attn_alpha': 6.829,
     'L0_attn_beta': 8.0,
     'L0_ffn_wq': 8.0,
     'L0_ffn_keys': 8.0,
     'L0_ffn_expert_down': 8.0,
     'L0_ffn_expert_up': 8.0,
     'L1_ffn_wqkv': 7.646,
     'L1_ffn_wo': 7.644,
     'L1_ffn_w1': 8.0,
     'L1_ffn_w2': 8.0,
     'L1_attn_b_qkv': 6.996}
    for name, (base, spread) in spreads.items():
        noise = np.random.default_rng([zlib.crc32(name.encode()), seed]).standard_normal(out[name].shape)
        drawn = base * np.exp(spread * noise) if base else spread * noise
        out[name] = jnp.asarray(drawn.astype(out[name].dtype))
    for name, factor in factors.items():
        out[name] = (out[name] * factor).astype(out[name].dtype)
    return out
```

```python
from contextlib import ExitStack

import numpy as np

import concourse.bass as bass
from concourse import mybir
from concourse.alu_op_type import AluOpType as ALU

ACT = mybir.ActivationFunctionType
AX_X = mybir.AxisListType.X
F32 = mybir.dt.float32
BF16 = mybir.dt.bfloat16

P = 128
T = 2048
D = 128
TILE = 128
NT = T // TILE
CH = 512
NC = T // CH
CT = CH // TILE
EPS = 1e-5
EH, NK, TOPK = 8, 32, 16
NE = NK * NK
EB = NE // P
CAND = sum(TOPK // (i + 1) for i in range(TOPK))
SPAN = 32
LAYERS, H, DH, WIN = 2, 8, 64, 64
INNER = H * DH
QK_SCALE = 8.0
KEYS = WIN + TILE
HID = D * 4 * 2 // 3
HB = [(0, P), (P, P), (2 * P, HID - 2 * P)]
MASKED = -1e37
LOWEST = -3.0e38


def build(nc, x, delta, alpha, beta, gamma, omega, norm_w, wq, keys, e_down, e_up, c0, wmod0,
          w_qkv, b_qkv, ln_w, ln_b, wqkv, q_scale, k_scale, wo, ln_g, ln_bb, w1, b1, w2, b2,
          c1, wmod1, rotary, out):
    with ExitStack() as ctx:
        def sb(name, shape, dt=F32):
            return ctx.enter_context(nc.sbuf_tensor(name, shape, dt))

        def sem(name):
            return ctx.enter_context(nc.semaphore(name))

        PS = ctx.enter_context(nc.psum_tensor("PS", [P, 8 * CH], F32))

        def bank(b, n=CH):
            return PS[:, b * CH:b * CH + n]

        arena = sb("arena", [P, 9 * NE])

        def carve(start, *shape):
            n = int(np.prod(shape))
            v = arena[:, start:start + n]
            return v.rearrange("p (a b) -> p a b", a=shape[0]) if len(shape) == 2 else v

        x_tok = sb("x_tok", [P, NT, D])
        XT = sb("XT", [P, T])
        HT = sb("HT", [P, T])
        ZA = sb("ZA", [P, 1 + T])
        ZB = sb("ZB", [P, 1 + T])
        ident = sb("ident", [P, P])
        ident_bf = sb("ident_bf", [P, P], BF16)
        center = sb("center", [P, P])
        mean = sb("mean", [P, P])
        cols = sb("cols", [P, 64])
        mod_raw = sb("mod_raw", [P, 12])
        mod = sb("mod", [P, 12])
        sgn = sb("sgn", [P, 12])
        silc = sb("silc", [P, 2])
        sig = sb("sig", [P, 4])
        ema = sb("ema", [P, 8])
        eps_c = sb("eps_c", [P, 1])

        wmod_s = sb("wmod_s", [P, 2, 6 * D])
        rotL = sb("rotL", [P, NT, 4 * DH])
        flat = rotL[:, :, :].rearrange("p a b -> p (a b)")
        wq_s = flat[:, 0:2 * EH * D]
        keys_s = carve(6 * NE, 4, D)
        wqT = flat[:, 2 * EH * D:4 * EH * D].rearrange("p (a b) -> p a b", a=2 * EH)
        keysT = carve(6 * NE + 4 * D, 4 * P)
        fold = sb("fold", [P, 2 * EH * NK])
        down_s = carve(7 * NE, EB, D)
        downT = sb("downT", [P, NE])
        up_s = sb("up_s", [P, EB, D])
        wqkv1_s = sb("wqkv1_s", [P, 3 * D])
        bv_b = sb("bv_b", [P, D])
        wqkv_s = sb("wqkv_s", [P, LAYERS, 3 * INNER])
        wo_s = sb("wo_s", [P, LAYERS, INNER // P, D])
        w1_s = sb("w1_s", [P, LAYERS, 2 * HID])
        w2_s = sb("w2_s", [P, LAYERS, 3, D])
        b1_s = sb("b1_s", [P, LAYERS, 6])
        rot_s = sb("rot_s", [P, NT, 4 * DH])
        rscale = sb("rscale", [P, LAYERS, 4 * DH])
        band = sb("band", [P, P + SPAN])
        mask_bf = sb("mask_bf", [P, KEYS], BF16)
        mask0_bf = sb("mask0_bf", [P, KEYS], BF16)

        sq_s = sb("sq_s", [P, CH])
        lnv = sb("lnv", [P, CH])
        rstd = sb("rstd", [P, CH])
        nrm = sb("nrm", [P, CH])
        h2 = sb("h2", [P, CH])

        ld_x, ld_small, ld_w0, ld_w1 = sem("ld_x"), sem("ld_small"), sem("ld_w0"), sem("ld_w1")
        passed = sem("passed")
        const_ready, stored = sem("const_ready"), sem("stored")
        pool_step, dve_step, act_step = sem("pool_step"), sem("dve_step"), sem("act_step")

        CD, CA, CB, CG, CO, CN, CBQ, CBK, CLW, CLB, CC = 0, 2, 4, 6, 8, 9, 10, 11, 12, 13, 14
        CLG, CLBB, CB2 = 16, 18, 20
        small = [
            (cols[:, CD:CD + 2], delta.rearrange("p n a -> p (n a)")),
            (cols[:, CA:CA + 2], alpha.rearrange("p n a -> p (n a)")),
            (cols[:, CB:CB + 2], beta.rearrange("p n a -> p (n a)")),
            (cols[:, CG:CG + 2], gamma),
            (cols[:, CO:CO + 1], omega.rearrange("(p a) -> p a", a=1)),
            (cols[:, CN:CN + 1], norm_w.rearrange("(p a) -> p a", a=1)),
            (cols[:, CBQ:CBQ + 2], b_qkv[0:2 * D].rearrange("(n p) -> p n", p=P)),
            (cols[:, CLW:CLW + 1], ln_w.rearrange("(p a) -> p a", a=1)),
            (cols[:, CLB:CLB + 1], ln_b.rearrange("(p a) -> p a", a=1)),
            (cols[:, CC:CC + 1], c0.rearrange("a p -> p a")),
            (cols[:, CC + 1:CC + 2], c1.rearrange("a p -> p a")),
            (cols[:, CLG:CLG + 2], ln_g.rearrange("l p -> p l")),
            (cols[:, CLBB:CLBB + 2], ln_bb.rearrange("l p -> p l")),
            (cols[:, CB2:CB2 + 2], b2.rearrange("l p -> p l")),
            (bv_b[:, :], b_qkv[2 * D:3 * D].rearrange("(a d) -> a d", a=1).to_broadcast([P, D])),
        ]
        tail = HB[2][1]
        for l in range(LAYERS):
            for g in range(2):
                o = g * HID
                small.append((b1_s[:, l, 3 * g:3 * g + 2], b1[l, o:o + 2 * P].rearrange("(n p) -> p n", p=P)))
                small.append((b1_s[0:tail, l, 3 * g + 2:3 * g + 3],
                              b1[l, o + 2 * P:o + HID].rearrange("(p a) -> p a", a=1)))
            for j, s in enumerate((q_scale, k_scale)):
                row = s[l:l + 1, :]
                small.append((rscale[:, l, j * DH:(j + 1) * DH], row.to_broadcast([P, DH])))
                o = (2 + j) * DH
                small.append((rscale[:, l, o:o + DH // 2], row[:, DH // 2:].to_broadcast([P, DH // 2])))
                small.append((rscale[:, l, o + DH // 2:o + DH], row[:, 0:DH // 2].to_broadcast([P, DH // 2])))
        N_SMALL = 16 * len(small)

        mod_ready, mod_done, sig_ready = sem("mod_ready"), sem("mod_done"), sem("sig_ready")
        silc_ready = sem("silc_ready")
        xT_ps, xT_done = sem("xT_ps"), sem("xT_done")
        tr_ps, tr_done = sem("tr_ps"), sem("tr_done")
        fold_ps, fold_done = sem("fold_ps"), sem("fold_done")
        ema_ready = sem("ema_ready")
        rot_ready = sem("rot_ready")
        cen_ready, sq_ready, var_ready = sem("cen_ready"), sem("sq_ready"), sem("var_ready")
        r_ready_a = sem("ln_norms_ready")
        rstd_ready, nrm_ready, nrm_used = sem("rstd_ready"), sem("nrm_ready"), sem("nrm_used")
        y_ready, silu_ready, x1_done = sem("y_ready"), sem("silu_ready"), sem("x1_done")
        h2_ready, h2sq_ready, ms_ready, rms_ready, xn_done = (
            sem("h2_ready"), sem("h2sq_ready"), sem("ms_ready"), sem("rms_ready"), sem("xn_done"))
        xn_ready, sim_ps, sim_ready = sem("xn_ready"), sem("sim_ps"), sem("sim_ready")
        hid_ps, gelu_ready, sum_ready, sum_free = (
            sem("hid_ps"), sem("gelu_ready"), sem("sum_ready"), sem("sum_free"))
        weight_ready, weightT_ps, hidw_ready, eout_ps, x2_done = (
            sem("weight_ready"), sem("weightT_ps"), sem("hidw_ready"), sem("eout_ps"), sem("x2_done"))
        hc_ready, qkv_ps, qk_ready, v_ready, score_ps, score_ready, ctx_ps, ctx_done = (
            sem("hc_ready"), sem("qkv_ps"), sem("qk_ready"), sem("v_ready"), sem("score_ps"),
            sem("score_ready"), sem("ctx_ps"), sem("ctx_done"))
        ln_out, x3_done, z0_done = sem("ln_out"), sem("x3_done"), sem("z0_done")
        hs_ready, qkv2_ps, v2_ready, sq2_ready, ss_ready, r_ready = (
            sem("hs_ready"), sem("qkv2_ps"), sem("v2_ready"), sem("sq2_ready"), sem("ss_ready"),
            sem("r_ready"))
        rot1_ready, rot2_ready, qkT_ps, qT_ready, kT_ready, sim2_ps, max_ready, p_ready, p2_ready = (
            sem("rot1_ready"), sem("rot2_ready"), sem("qkT_ps"), sem("qT_ready"), sem("kT_ready"),
            sem("sim2_ps"), sem("max_ready"), sem("p_ready"), sem("p2_ready"))
        pT_ps, pT_ready, pTw_ready, pv_ps, o_ready, oT_ps, oT_ready, wo_ps, zb_done = (
            sem("pT_ps"), sem("pT_ready"), sem("pTw_ready"), sem("pv_ps"), sem("o_ready"),
            sem("oT_ps"), sem("oT_ready"), sem("wo_ps"), sem("zb_done"))
        zs_ready, hn_ready, up_ps, gate_ready, hh_ready, down_ps, za_done = (
            sem("zs_ready"), sem("hn_ready"), sem("up_ps"), sem("gate_ready"), sem("hh_ready"),
            sem("down_ps"), sem("za_done"))
        fin_ready, finT_ps, fin_out = sem("fin_ready"), sem("finT_ps"), sem("fin_out")

        scan1, scan2, ysum, silu_s = (carve(i * CH, CH) for i in range(4))

        xn = sb("xn", [P, 2, TILE])
        sims = sb("sims", [P, 2, 2 * EH * NK])
        rest = sb("rest", [P, 2 * EH, NK])
        srt = sb("srt", [P, 2 * EH, TOPK])
        cand = sb("cand", [P, EH, CAND])
        cand2 = sb("cand2", [P, EH, CAND])
        top = sb("top", [P, EH, TOPK])
        thr = sb("thr", [P, EH])
        sums, kept, wts, gelu_s = (carve(2 * i * NE, 2, NE) for i in range(4))
        hidw = carve(8 * NE, NE)

        hc = sb("hc", [P, 2, TILE])
        q1 = sb("q1", [P, TILE])
        k1 = sb("k1", [P, 2, TILE])
        v1 = sb("v1", [P, 2, D])
        sc = sb("sc", [P, TILE + SPAN])

        sq2 = carve(0 * NE, 2 * INNER)
        ss = sb("ss", [P, 2 * H])
        lnss = sb("lnss", [P, 2 * H])
        rr = sb("rr", [P, 2 * H])
        ra = carve(1 * NE, 2 * INNER)
        rb = carve(2 * NE, 2 * INNER)
        qT = sb("qT", [P, H // 2, TILE])
        kT = sb("kT", [P, 2, H // 2, TILE])
        v2 = sb("v2", [P, 2, INNER])
        mx = sb("mx", [P, H])
        nmx = sb("nmx", [P, H])
        pr = sb("pr", [P, WIN + H * KEYS])
        rsum = sb("rsum", [P, H])
        rinv = sb("rinv", [P, H])
        pT = carve(3 * NE, H, TILE)
        pTw = carve(4 * NE, H, TILE)
        o_s = carve(5 * NE, INNER)
        oT = carve(5 * NE + INNER, INNER // P, TILE)

        zs = carve(3 * NE, CH)
        hn = carve(3 * NE + CH, CH)
        gate = carve(0, 3, CH)
        hh = carve(3 * CH, 3, CH)
        fin = carve(4 * NE, CH)

        def skewed(eng, base, front, back):
            front(base, 0, 0, first=True)
            with eng.Fori(0, NT // 2 - 1) as p:
                for u in range(2):
                    front(2 * p + (base + 1 + u), 1 - u, (2 * p + (1 + u)) * TILE)
                    back(2 * p + (base + u), u, (2 * p + u) * TILE)
            front(base + NT - 1, 1, (NT - 1) * TILE)
            back(base + NT - 2, 0, (NT - 2) * TILE)
            back(base + NT - 1, 1, (NT - 1) * TILE)

        def pairs(eng, base, tile, first=0):
            with eng.Fori(first // 2, NT // 2) as p:
                for u in range(2):
                    tile(2 * p + (base + u), u, (2 * p + u) * TILE)

        def plain(eng):
            eng.sem_inc(passed, 1)

        def cols_at(buf, off, n, rows=slice(0, P)):
            return buf[rows, bass.ds(off, n)]

        def place(h):
            return (h % 2) * (H // 2) + h // 2

        def scores_of(h):
            o = (place(h) // 2) * CH + (place(h) % 2) * KEYS
            return PS[:, o:o + KEYS]

        block = ctx.enter_context(nc.Block())

        @block.sync
        def _(sp):
            sp.dma_start(x_tok[:, :, :], x[0].rearrange("(n p) d -> p n d", p=P)).then_inc(ld_x, 16)
            sp.dma_start(wmod_s[:, 0, :], wmod0).then_inc(ld_w0, 16)
            sp.dma_start(wmod_s[:, 1, :], wmod1).then_inc(ld_w0, 16)
            sp.dma_start(wq_s[:, :], wq).then_inc(ld_w0, 16)
            sp.dma_start(keys_s[:, :, :],
                         keys.rearrange("h k p d -> (h k p) d").rearrange("(n r) d -> r n d", r=P)).then_inc(ld_w0, 16)
            sp.dma_start(down_s[:, :, :], e_down.rearrange("(n r) d -> r n d", r=P)).then_inc(ld_w0, 16)
            sp.dma_start(up_s[:, :, :], e_up.rearrange("(n r) d -> r n d", r=P)).then_inc(ld_w0, 16)
            sp.dma_start(wqkv1_s[:, :], w_qkv).then_inc(ld_w1, 16)
            sp.dma_start(rot_s[:, :, :], rotary.rearrange("(n p) c -> p n c", p=P)).then_inc(ld_w1, 16)
            sp.dma_start(wqkv_s[:, :, :], wqkv.rearrange("l p n -> p l n")).then_inc(ld_w1, 16)
            for l in range(LAYERS):
                sp.dma_start(wo_s[:, l, :, :], wo[l].rearrange("(n p) d -> p n d", p=P)).then_inc(ld_w1, 16)
                sp.dma_start(w2_s[:, l, 0:2, :], w2[l, 0:2 * P, :].rearrange("(n p) d -> p n d", p=P)).then_inc(ld_w1, 16)
                sp.dma_start(w2_s[0:tail, l, 2, :], w2[l, 2 * P:HID, :]).then_inc(ld_w1, 16)
            sp.dma_start(w1_s[:, :, :], w1.rearrange("l p n -> p l n")).then_inc(ld_w1, 16)
            o_v = out[0].rearrange("(n p) d -> p n d", p=P)
            for c in range(NC):
                sp.wait_ge(fin_out, c + 1)
                sp.dma_start(o_v[:, c * CT:(c + 1) * CT, :], x_tok[:, c * CT:(c + 1) * CT, :]).then_inc(stored, 16)
            sp.wait_ge(stored, 16 * NC)
        N_W0 = 16 * 6
        N_W1 = 16 * (4 + 3 * LAYERS)

        @block.gpsimd
        def _(pool):
            n = [0]

            def step(ins):
                n[0] += 1
                ins.then_inc(pool_step, 1)
                pool.wait_ge(pool_step, n[0])

            nc.gpsimd.memset(ident[:, :], 0.0)
            nc.gpsimd.memset(center[:, :], -1.0 / D)
            nc.gpsimd.memset(mean[:, :], 1.0 / D)
            nc.gpsimd.memset(eps_c[:, :], EPS)
            nc.gpsimd.memset(band[:, :], 1.0)
            nc.gpsimd.memset(mask_bf[:, :], 0.0)
            nc.gpsimd.memset(ema[:, :], 0.0)
            nc.gpsimd.memset(k1[:, :, :], 0.0)
            nc.gpsimd.memset(v1[:, :, :], 0.0)
            nc.gpsimd.memset(kT[:, 1, :, :], 0.0)
            nc.gpsimd.memset(v2[:, 1, :], 0.0)
            nc.gpsimd.memset(ZA[:, 0:1], 0.0)
            nc.gpsimd.memset(ZB[:, 0:1], 0.0)
            step(nc.gpsimd.memset(pr[:, 0:WIN], 0.0))
            step(nc.gpsimd.affine_select(out=ident[:, :], in_=ident[:, :], compare_op=ALU.not_equal, fill=1.0,
                                         base=0, pattern=[[-1, P]], channel_multiplier=1))
            own = band[:, 0:P]
            step(nc.gpsimd.affine_select(out=own, in_=own, compare_op=ALU.is_ge, fill=0.0,
                                         base=0, pattern=[[1, P]], channel_multiplier=-1))
            step(nc.gpsimd.affine_select(out=own, in_=own, compare_op=ALU.is_ge, fill=0.0,
                                         base=SPAN - 1, pattern=[[-1, P]], channel_multiplier=1))
            prev = band[:, P:P + SPAN]
            step(nc.gpsimd.affine_select(out=prev, in_=prev, compare_op=ALU.is_ge, fill=0.0,
                                         base=SPAN - 1 - P, pattern=[[-1, SPAN]], channel_multiplier=1))
            step(nc.gpsimd.affine_select(out=mask_bf[:, :], in_=mask_bf[:, :], compare_op=ALU.is_ge, fill=MASKED,
                                         base=WIN, pattern=[[-1, KEYS]], channel_multiplier=1))
            step(nc.gpsimd.affine_select(out=mask_bf[:, :], in_=mask_bf[:, :], compare_op=ALU.is_ge, fill=MASKED,
                                         base=0, pattern=[[1, KEYS]], channel_multiplier=-1))
            step(nc.gpsimd.affine_select(out=mask0_bf[:, :], in_=mask_bf[:, :], compare_op=ALU.is_ge, fill=MASKED,
                                         base=-WIN, pattern=[[1, KEYS]], channel_multiplier=0))
            step(nc.gpsimd.tensor_copy(ident_bf[:, :], ident[:, :]))
            nc.gpsimd.tensor_tensor(center[:, :], center[:, :], ident[:, :], ALU.add).then_inc(const_ready, 1)

            def rotary_table(l):
                ins = nc.gpsimd.tensor_tensor(rotL[:, :, :], rot_s[:, :, :],
                                              rscale[:, l:l + 1, :].to_broadcast([P, NT, 4 * DH]), ALU.mult)
                ins.then_inc(rot_ready, 1)

            pool.wait_ge(ld_small, N_SMALL)
            pool.wait_ge(ld_w1, N_W1)
            pool.wait_ge(fold_ps, 1)
            rotary_table(0)

            def pair_sums(t, u):
                pool.wait_ge(sim_ready, t + 1)
                for h in range(EH):
                    pool.wait_ge(sum_free, t * EH + (h + 1))
                    a = sims[:, u, h * NK:(h + 1) * NK].unsqueeze(2).to_broadcast([P, NK, NK])
                    b = sims[:, u, (EH + h) * NK:(EH + h + 1) * NK].unsqueeze(1).to_broadcast([P, NK, NK])
                    nc.gpsimd.tensor_tensor(sums[:, h % 2, :].rearrange("p (a b) -> p a b", a=NK), a, b,
                                            ALU.add).then_inc(sum_ready, 1)

            with pool.Fori(0, NT // 2) as p:
                for u in range(2):
                    pair_sums(2 * p + u, u)

            for l in range(LAYERS):
                if l:
                    pool.wait_ge(rot1_ready, NT * l)
                    pool.wait_ge(zb_done, NT * l)
                    rotary_table(l)
                base = NT * l
                with pool.Fori(base, base + NT) as t:
                    pool.wait_ge(rot1_ready, t + 1)
                    nc.gpsimd.tensor_tensor(ra[:, :], ra[:, :], rb[:, :], ALU.add).then_inc(pool_step, 1)
                    pool.wait_ge(pool_step, t + (n[0] + 1))
                    pool.wait_ge(r_ready, t + 1)
                    v = ra[:, :].rearrange("p (g d) -> p g d", d=DH)
                    nc.gpsimd.tensor_tensor(v, v, rr[:, :].unsqueeze(2).to_broadcast([P, 2 * H, DH]),
                                            ALU.mult).then_inc(rot2_ready, 1)

        @block.scalar
        def _(act):
            for dst, src in small:
                act.dma_start(dst, src, allow_slow_non_contiguous=True).then_inc(ld_small, 16)
            act.wait_ge(ld_small, N_SMALL)
            nc.scalar.activation(silc[:, :], cols[:, CC:CC + 2], ACT.Silu).then_inc(silc_ready, 1)
            nc.scalar.activation(sig[:, :], cols[:, CD:CD + 4], ACT.Sigmoid).then_inc(sig_ready, 1)
            for c in range(NC):
                act.wait_ge(xT_ps, c + 1)
                nc.scalar.copy(XT[:, c * CH:(c + 1) * CH], bank(c)).then_inc(xT_done, 1)
            for g in range(4):
                act.wait_ge(tr_ps, g + 1)
                nc.scalar.copy(wqT[:, 4 * g:4 * g + 4, :], bank(4 + g % 2).rearrange("p (a b) -> p a b", a=4)).then_inc(tr_done, 1)
            act.wait_ge(tr_ps, 5)
            nc.scalar.copy(keysT[:, :], bank(4)).then_inc(tr_done, 1)
            for g in range(2):
                act.wait_ge(tr_ps, 6 + g)
                nc.scalar.copy(downT[:, g * CH:(g + 1) * CH], bank(4 + (5 + g) % 2)).then_inc(tr_done, 1)
            act.wait_ge(fold_ps, 1)
            nc.scalar.copy(fold[:, :], bank(6)).then_inc(fold_done, 1)
            act.wait_ge(const_ready, 1)
            n = [0]

            def norm(c):
                act.wait_ge(cen_ready, c + 1)
                nc.scalar.activation(sq_s[:, :], bank(0), ACT.Square).then_inc(sq_ready, 1)
                act.wait_ge(var_ready, c + 1)
                nc.scalar.activation(lnv[:, :], bank(1), ACT.Ln, bias=eps_c[:, 0:1]).then_inc(act_step, 1)
                act.wait_ge(act_step, c + 1)
                act.wait_ge(nrm_ready, c)
                nc.scalar.activation(rstd[:, :], lnv[:, :], ACT.Exp, scale=-0.5).then_inc(rstd_ready, 1)

            def norm_affine(c, dst, scale, bias):
                act.wait_ge(nrm_ready, c + 1)
                return nc.scalar.activation(dst, nrm[:, :], ACT.Identity, scale=scale, bias=bias)

            act.wait_ge(mod_done, 1)
            with act.Fori(0, NC) as c:
                norm(c)
                norm_affine(c, cols_at(HT, c * CH, CH), mod[:, 1:2], mod[:, 0:1]).then_inc(nrm_used, 1)
            with act.Fori(0, NC) as c:
                act.wait_ge(y_ready, c + 1)
                act.wait_ge(x1_done, c)
                nc.scalar.activation(silu_s[:, :], ysum[:, :], ACT.Silu).then_inc(silu_ready, 1)
            with act.Fori(0, NC) as c:
                norm(c + NC)
                norm_affine(c + NC, h2[:, :], mod[:, 4:5], mod[:, 3:4]).then_inc(h2_ready, 1)
                act.wait_ge(h2_ready, c + 1)
                nc.scalar.activation(sq_s[:, :], h2[:, :], ACT.Square).then_inc(h2sq_ready, 1)
                act.wait_ge(ms_ready, c + 1)
                nc.scalar.activation(lnv[:, :], bank(2), ACT.Ln, bias=eps_c[:, 0:1]).then_inc(rms_ready, 1)
                act.wait_ge(rms_ready, 2 * c + 1)
                nc.scalar.activation(rstd[:, :], lnv[:, :], ACT.Exp, scale=-0.5).then_inc(rms_ready, 1)
                act.wait_ge(xn_done, c + 1)
            def front0(t, u, off, first=False):
                act.wait_ge(xn_done, NC)
                nc.scalar.copy(xn[:, u, :], cols_at(HT, off, TILE)).then_inc(xn_ready, 1)
                act.wait_ge(sim_ps, t + 1)
                nc.scalar.copy(sims[:, u, :], bank(u)).then_inc(sim_ready, 1)
                act.wait_ge(hid_ps, t + 1)
                nc.scalar.activation(gelu_s[:, u, :], PS[:, 2 * CH:4 * CH], ACT.Gelu).then_inc(gelu_ready, 1)

            skewed(act, 0, front0, lambda t, u, off: None)

            with act.Fori(0, NC) as c:
                norm(c + 2 * NC)
                norm_affine(c + 2 * NC, cols_at(HT, c * CH, CH), mod[:, 7:8], mod[:, 6:7]).then_inc(nrm_used, 1)

            def front1(t, u, off, first=False):
                nc.scalar.copy(hc[:, u, :], cols_at(HT, off, TILE)).then_inc(hc_ready, 1)
                act.wait_ge(qkv_ps, t + 1)
                nc.scalar.activation(q1[:, :], bank(u)[:, 0:TILE], ACT.Identity, bias=cols[:, CBQ:CBQ + 1])
                nc.scalar.activation(k1[:, u, :], bank(u)[:, TILE:2 * TILE], ACT.Identity,
                                     bias=cols[:, CBK:CBK + 1]).then_inc(qk_ready, 1)

            def back1(t, u, off):
                act.wait_ge(ctx_ps, t + 1)
                plain(act)
                nc.scalar.copy(cols_at(HT, off, TILE), bank(4 + u, TILE)).then_inc(ctx_done, 1)

            skewed(act, 0, front1, back1)
            with act.Fori(0, NC) as c:
                norm(c + 3 * NC)
                norm_affine(c + 3 * NC, h2[:, :], cols[:, CLW:CLW + 1], cols[:, CLB:CLB + 1]).then_inc(ln_out, 1)
                act.wait_ge(x3_done, c + 1)
            with act.Fori(0, NC) as c:
                norm(c + 4 * NC)
                norm_affine(c + 4 * NC, cols_at(ZA, c * CH + 1, CH), mod[:, 10:11], mod[:, 9:10]).then_inc(z0_done, 1)

            for l in range(LAYERS):
                if l:
                    act.wait_ge(za_done, NC * l)
                else:
                    act.wait_ge(z0_done, NC)

                def front2(t, u, off, first=False):
                    nc.scalar.copy(hc[0:DH, u, :], cols_at(ZA, off + 1, TILE, slice(0, DH)))
                    nc.scalar.copy(hc[DH:P, u, :], cols_at(ZA, off, TILE, slice(DH, P))).then_inc(hs_ready, 1)
                    act.wait_ge(qkv2_ps, t + 1)
                    nc.scalar.activation(sq2[:, :], PS[:, 4 * CH:6 * CH], ACT.Square).then_inc(sq2_ready, 1)
                    nc.scalar.copy(v2[:, u, :], bank(6)).then_inc(v2_ready, 1)
                    act.wait_ge(ss_ready, t + 1)
                    nc.scalar.activation(lnss[:, :], ss[:, :], ACT.Ln).then_inc(r_ready_a, 1)
                    act.wait_ge(r_ready_a, t + 1)
                    nc.scalar.activation(rr[:, :], lnss[:, :], ACT.Exp, scale=-0.5).then_inc(r_ready, 1)

                def mid2(t, u, off):
                    act.wait_ge(qkT_ps, t + 1)
                    nc.scalar.copy(kT[:, u, :, :], bank(5).rearrange("p (a b) -> p a b", a=H // 2)).then_inc(kT_ready, 1)
                    act.wait_ge(max_ready, t + 1)
                    for h in range(H):
                        ins = nc.scalar.activation(pr[:, WIN + h * KEYS:WIN + (h + 1) * KEYS], scores_of(h), ACT.Exp,
                                                   scale=QK_SCALE, bias=nmx[:, place(h):place(h) + 1], accum_out=rsum[:, h:h + 1])
                    ins.then_inc(p_ready, 1)

                def back2(t, u, off):
                    act.wait_ge(pT_ps, t + 1)
                    nc.scalar.copy(pT[:, :, :], PS[:, 0:2 * CH].rearrange("p (a b) -> p a b", a=H)).then_inc(pT_ready, 1)
                    act.wait_ge(oT_ps, t + 1)
                    nc.scalar.copy(oT[:, :, :], bank(7).rearrange("p (a b) -> p a b", a=INNER // P)).then_inc(oT_ready, 1)

                base = NT * l
                def tile2(t, u, off):
                    front2(t, u, off)
                    mid2(t, u, off)
                    back2(t, u, off)

                pairs(act, base, tile2)

                with act.Fori(NC * l, NC * (l + 1)) as c:
                    off = (c - NC * l) * CH
                    k = c + 5 * NC
                    act.wait_ge(zb_done, NT * (l + 1))
                    act.wait_ge(cen_ready, k)
                    nc.scalar.copy(zs[0:DH, :], cols_at(ZB, off + 1, CH, slice(0, DH)))
                    nc.scalar.copy(zs[DH:P, :], cols_at(ZB, off, CH, slice(DH, P))).then_inc(zs_ready, 1)
                    norm(k)
                    norm_affine(k, hn[:, :], cols[:, CLG + l:CLG + l + 1], cols[:, CLBB + l:CLBB + l + 1]).then_inc(hn_ready, 1)
                    for b, (o, m) in enumerate(HB):
                        act.wait_ge(up_ps, c * 3 + (b + 1))
                        nc.scalar.activation(gate[0:m, b, :], PS[0:m, (5 + b % 2) * CH:(6 + b % 2) * CH], ACT.Gelu,
                                             bias=b1_s[0:m, l, 3 + b:4 + b]).then_inc(gate_ready, 1)

            with act.Fori(0, NC) as c:
                act.wait_ge(finT_ps, c + 1)
                plain(act)
                nc.scalar.copy(x_tok[:, bass.ds(c * CT, CT), :], bank(0).rearrange("p (a b) -> p a b", a=CT)).then_inc(fin_out, 1)

        @block.tensor
        def _(pe):
            def mm(o, w, m, start=True, stop=True):
                return nc.tensor.matmul(o, w, m, start=start, stop=stop)

            pe.wait_ge(const_ready, 1)
            pe.wait_ge(ld_w0, N_W0)
            pe.wait_ge(silc_ready, 1)
            for l in range(2):
                for j in range(6):
                    ins = mm(bank(7)[:, 6 * l + j:6 * l + j + 1], wmod_s[:, l, j * D:(j + 1) * D], silc[:, l:l + 1])
            ins.then_inc(mod_ready, 1)
            pe.wait_ge(ld_x, 16)
            for c in range(NC):
                for j in range(CT):
                    ins = nc.tensor.transpose(bank(c)[:, j * TILE:(j + 1) * TILE], x_tok[:, c * CT + j, :], ident[:, :])
                ins.then_inc(xT_ps, 1)
            for g in range(7):
                if g >= 2:
                    pe.wait_ge(tr_done, g - 1)
                for j in range(4):
                    src = (wq_s[:, (4 * g + j) * D:(4 * g + j + 1) * D] if g < 4 else
                           keys_s[:, j, :] if g == 4 else down_s[:, 4 * (g - 5) + j, :])
                    ins = nc.tensor.transpose(bank(4 + g % 2)[:, j * P:(j + 1) * P], src, ident[:, :])
                ins.then_inc(tr_ps, 1)
            pe.wait_ge(tr_done, 5)
            kv = keysT[:, :].rearrange("p (h k a) -> p h a k", h=EH, a=2)
            for a in range(2):
                for h in range(EH):
                    o = (a * EH + h) * NK
                    ins = mm(bank(6)[:, o:o + NK], wqT[:, 2 * h + a, :], kv[:, h, a, :])
            ins.then_inc(fold_ps, 1)
            pe.wait_ge(xT_done, NC)

            def norm(c, src, ready=None):
                pe.wait_ge(nrm_ready, c)
                mm(bank(0), center[:, :], src).then_inc(cen_ready, 1)
                pe.wait_ge(sq_ready, c + 1)
                mm(bank(1), mean[:, :], sq_s[:, :]).then_inc(var_ready, 1)

            with pe.Fori(0, NC) as c:
                norm(c, cols_at(XT, c * CH, CH))
            with pe.Fori(0, NC) as c:
                pe.wait_ge(x1_done, NC)
                norm(c + NC, cols_at(XT, c * CH, CH))
                pe.wait_ge(h2sq_ready, c + 1)
                mm(bank(2), mean[:, :], sq_s[:, :]).then_inc(ms_ready, 1)
            pe.wait_ge(fold_done, 1)
            pe.wait_ge(tr_done, 7)
            pe.wait_ge(xn_done, NC)

            def front0(t, u, off, first=False):
                pe.wait_ge(xn_ready, t + 1)
                mm(bank(u), xn[:, u, :], fold[:, :]).then_inc(sim_ps, 1)
                pe.wait_ge(gelu_ready, t)
                for e in range(EB):
                    ins = mm(PS[:, 2 * CH + e * P:2 * CH + (e + 1) * P], downT[:, e * P:(e + 1) * P], xn[:, u, :])
                ins.then_inc(hid_ps, 1)

            def back0(t, u, off):
                pe.wait_ge(weight_ready, t + 1)
                for e in range(EB):
                    ins = nc.tensor.transpose(PS[:, 4 * CH + e * P:4 * CH + (e + 1) * P],
                                              wts[:, u, e * P:(e + 1) * P], ident[:, :])
                ins.then_inc(weightT_ps, 1)
                pe.wait_ge(hidw_ready, t + 1)
                for e in range(EB):
                    ins = mm(bank(6 + u, TILE), up_s[:, e, :], hidw[:, e * P:(e + 1) * P], e == 0, e == EB - 1)
                ins.then_inc(eout_ps, 1)

            skewed(pe, 0, front0, back0)

            with pe.Fori(0, NC) as c:
                pe.wait_ge(x2_done, NT)
                norm(c + 2 * NC, cols_at(XT, c * CH, CH))

            pe.wait_ge(ld_w1, N_W1)
            pe.wait_ge(nrm_used, 2 * NC)

            def front1(t, u, off, first=False):
                pe.wait_ge(hc_ready, t + 1)
                mm(bank(u)[:, 0:TILE], wqkv1_s[:, 0:D], hc[:, u, :])
                mm(bank(u)[:, TILE:2 * TILE], wqkv1_s[:, D:2 * D], hc[:, u, :])
                mm(bank(6 + u, TILE), hc[:, u, :], wqkv1_s[:, 2 * D:3 * D]).then_inc(qkv_ps, 1)
                pe.wait_ge(qk_ready, t + 1)
                mm(bank(2 + u)[:, 0:TILE], k1[:, u, :], q1[:, :])
                mm(bank(2 + u)[:, TILE:TILE + SPAN], k1[:, 1 - u, :], q1[:, 0:SPAN]).then_inc(score_ps, 1)

            def back1(t, u, off):
                pe.wait_ge(score_ready, t + 1)
                o = bank(4 + u, TILE)
                mm(o, v1[:, u, :], sc[:, 0:TILE])
                nc.tensor.matmul(o[:, 0:SPAN], v1[:, 1 - u, :], sc[:, TILE:TILE + SPAN], start=False, stop=True,
                                 skip_group_check=True).then_inc(ctx_ps, 1)

            def tile1(t, u, off):
                front1(t, u, off)
                back1(t, u, off)

            pairs(pe, 0, tile1)
            with pe.Fori(0, NC) as c:
                pe.wait_ge(ctx_done, NT)
                norm(c + 3 * NC, cols_at(HT, c * CH, CH))
            with pe.Fori(0, NC) as c:
                pe.wait_ge(x3_done, NC)
                norm(c + 4 * NC, cols_at(XT, c * CH, CH))

            for l in range(LAYERS):
                if l:
                    pe.wait_ge(za_done, NC * l)
                else:
                    pe.wait_ge(z0_done, NC)

                def qkv2(t, u):
                    pe.wait_ge(hs_ready, t + 1)
                    for j in range(3):
                        ins = mm(bank(4 + j), hc[:, u, :], wqkv_s[:, l, j * INNER:(j + 1) * INNER])
                    ins.then_inc(qkv2_ps, 1)

                def sims2(t, u, first=False):
                    pe.wait_ge(rot2_ready, t + 1)
                    for g in range(H):
                        ins = nc.tensor.transpose(PS[:, 4 * CH + g * P:4 * CH + (g + 1) * P], ra[:, g * P:(g + 1) * P], ident[:, :])
                    ins.then_inc(qkT_ps, 1)
                    pe.wait_ge(qT_ready, t + 1)
                    pe.wait_ge(kT_ready, t + 1)
                    for h in range(H):
                        rows = slice(DH * (h % 2), DH * (h % 2) + DH)
                        o = scores_of(h)
                        m = mask0_bf if first else mask_bf
                        nc.tensor.matmul(o, ident_bf[:, :], m[:, :], start=True, stop=True, skip_group_check=True)
                        nc.tensor.matmul(o[:, 0:WIN], qT[rows, h // 2, :], kT[rows, 1 - u, h // 2, WIN:TILE],
                                         start=False, stop=True, skip_group_check=True)
                        ins = nc.tensor.matmul(o[:, WIN:KEYS], qT[rows, h // 2, :], kT[rows, u, h // 2, :],
                                               start=False, stop=True, skip_group_check=True)
                    ins.then_inc(sim2_ps, 1)

                def back2(t, u):
                    pe.wait_ge(p_ready, t + 1)
                    for h in range(H):
                        o = WIN + h * KEYS
                        nc.tensor.transpose(PS[:, h * P:(h + 1) * P], pr[:, o + WIN:o + KEYS], ident[:, :])
                        ins = nc.tensor.transpose(PS[:, 2 * CH + h * P:2 * CH + (h + 1) * P], pr[:, o - WIN:o + WIN], ident[:, :])
                    ins.then_inc(pT_ps, 1)
                    pe.wait_ge(pT_ready, t + 1)
                    pe.wait_ge(pTw_ready, t + 1)
                    pe.wait_ge(v2_ready, t + 1)
                    for h in range(H):
                        o = bank(6)[:, h * DH:(h + 1) * DH]
                        hv = slice(h * DH, (h + 1) * DH)
                        nc.tensor.matmul(o, pT[:, h, :], v2[:, u, hv], start=True, stop=False, skip_group_check=True)
                        ins = nc.tensor.matmul(o, pTw[WIN:P, h, :], v2[WIN:P, 1 - u, hv], start=False, stop=True,
                                               skip_group_check=True)
                    ins.then_inc(pv_ps, 1)
                    pe.wait_ge(o_ready, t + 1)
                    for g in range(INNER // P):
                        ins = nc.tensor.transpose(bank(7)[:, g * P:(g + 1) * P], o_s[:, g * P:(g + 1) * P], ident[:, :])
                    ins.then_inc(oT_ps, 1)
                    pe.wait_ge(oT_ready, t + 1)
                    for g in range(INNER // P):
                        ins = mm(bank(7, TILE), wo_s[:, l, g, :], oT[:, g, :], g == 0, g == INNER // P - 1)
                    ins.then_inc(wo_ps, 1)

                base = NT * l

                def tile2(t, u, first=False):
                    pe.wait_ge(zb_done, t)
                    qkv2(t, u)
                    sims2(t, u, first)
                    back2(t, u)

                tile2(base, 0, True)
                tile2(base + 1, 1)
                pairs(pe, base, lambda t, u, off: tile2(t, u), first=2)

                with pe.Fori(NC * l, NC * (l + 1)) as c:
                    pe.wait_ge(zs_ready, c + 1)
                    norm(c + 5 * NC, zs[:, :])
                    pe.wait_ge(hn_ready, c + 1)
                    for b, (o, m) in enumerate(HB):
                        if b == 0:
                            pe.wait_ge(hh_ready, c * 3)
                        elif b == 2:
                            pe.wait_ge(hh_ready, c * 3 + 1)
                        mm(PS[0:m, (3 + b % 2) * CH:(4 + b % 2) * CH], w1_s[:, l, o:o + m], hn[:, :])
                        mm(PS[0:m, (5 + b % 2) * CH:(6 + b % 2) * CH], w1_s[:, l, HID + o:HID + o + m], hn[:, :]).then_inc(up_ps, 1)
                    pe.wait_ge(hh_ready, c * 3 + 3)
                    pe.wait_ge(za_done, c)
                    for b, (o, m) in enumerate(HB):
                        ins = mm(bank(7), w2_s[0:m, l, b, :], hh[0:m, b, :], b == 0, b == 2)
                    ins.then_inc(down_ps, 1)

            with pe.Fori(0, NC) as c:
                pe.wait_ge(fin_ready, c + 1)
                pe.wait_ge(fin_out, c)
                for j in range(CT):
                    ins = nc.tensor.transpose(bank(0)[:, j * TILE:(j + 1) * TILE], fin[:, j * TILE:(j + 1) * TILE], ident[:, :])
                ins.then_inc(finT_ps, 1)

        @block.vector
        def _(dve):
            V = nc.vector
            n = [0]

            def step(ins, k=None):
                n[0] += 1
                ins.then_inc(dve_step, 1)
                dve.wait_ge(dve_step, n[0] if k is None else k + n[0])

            dve.wait_ge(mod_ready, 1)
            step(V.tensor_copy(mod_raw[:, :], bank(7, 12)))
            step(V.tensor_copy(mod[:, :], mod_raw[:, :]))
            step(V.tensor_scalar(sgn[:, :], mod_raw[:, :], 0.0, 2.0, ALU.is_ge, ALU.mult))
            for l in range(2):
                for j in (1, 4):
                    V.tensor_scalar(mod[:, 6 * l + j:6 * l + j + 1], mod_raw[:, 6 * l + j:6 * l + j + 1], 1.0, None, ALU.add)
            step(V.tensor_scalar(sgn[:, :], sgn[:, :], -1.0, None, ALU.add))
            for l in range(2):
                for j in (2, 5):
                    o = 6 * l + j
                    step(V.tensor_scalar(mod[:, o:o + 1], mod_raw[:, o:o + 1], sgn[:, o:o + 1], 0.25, ALU.mult, ALU.max))
                    step(V.tensor_tensor(mod[:, o:o + 1], mod[:, o:o + 1], sgn[:, o:o + 1], ALU.mult))
            V.tensor_copy(sgn[:, 0:1], mod[:, 0:1]).then_inc(mod_done, 1)
            dve.wait_ge(sig_ready, 1)
            dve.wait_ge(const_ready, 1)
            step(V.tensor_tensor(ema[:, 0:2], sig[:, 0:2], sig[:, 2:4], ALU.mult))
            step(V.tensor_scalar(ema[:, 0:2], ema[:, 0:2], -1.0, 1.0, ALU.mult, ALU.add))
            step(V.tensor_tensor(ema[:, 2:4], sig[:, 0:2], cols[:, CB:CB + 2], ALU.mult))
            step(V.tensor_scalar(ema[:, 4:6], cols[:, CG:CG + 2], float(np.sqrt(0.5)), None, ALU.mult))
            step(V.tensor_tensor(ema[:, 2:4], ema[:, 2:4], ema[:, 4:6], ALU.mult))

            def norm(c):
                dve.wait_ge(rstd_ready, c + 1)
                V.tensor_tensor(nrm[:, :], bank(0), rstd[:, :], ALU.mult).then_inc(nrm_ready, 1)

            def loop(eng_range, steps, body):
                start, stop, by = eng_range
                before = n[0]
                with dve.Fori(start, stop, by) as i:
                    done = [0]

                    def link(ins):
                        done[0] += 1
                        ins.then_inc(dve_step, 1)
                        dve.wait_ge(dve_step, (i - start) * (steps // by) + (before + done[0]))

                    body(i, link)
                    assert done[0] == steps, done[0]
                n[0] = before + steps * ((stop - start) // by)

            def norm_loop(k, used=None, at=0):
                with dve.Fori(0, NC) as c:
                    if used is not None:
                        dve.wait_ge(used, c + at)
                    norm(c + k * NC)

            norm_loop(0, nrm_used)
            def ema_chunk(c, link):
                dve.wait_ge(nrm_used, c + 1)
                h = cols_at(HT, c * CH, CH)
                V.tensor_tensor_scan(scan1[:, :], ema[:, 0:1].to_broadcast([P, CH]), h, ema[:, 6:7], ALU.mult, ALU.add)
                V.tensor_tensor_scan(scan2[:, :], ema[:, 1:2].to_broadcast([P, CH]), h, ema[:, 7:8], ALU.mult, ALU.add)
                dve.wait_ge(silu_ready, c)
                link(V.tensor_scalar(ysum[:, :], h, cols[:, CO:CO + 1], None, ALU.mult))
                V.tensor_copy(ema[:, 6:7], scan1[:, CH - 1:CH])
                V.tensor_copy(ema[:, 7:8], scan2[:, CH - 1:CH])
                link(V.scalar_tensor_tensor(out=ysum[:, :], in0=scan1[:, :], scalar=ema[:, 2:3], in1=ysum[:, :],
                                            op0=ALU.mult, op1=ALU.add))
                V.scalar_tensor_tensor(out=ysum[:, :], in0=scan2[:, :], scalar=ema[:, 3:4], in1=ysum[:, :],
                                       op0=ALU.mult, op1=ALU.add).then_inc(y_ready, 1)
                dve.wait_ge(silu_ready, c + 1)
                xt = cols_at(XT, c * CH, CH)
                V.scalar_tensor_tensor(out=xt, in0=silu_s[:, :], scalar=mod[:, 2:3], in1=xt,
                                       op0=ALU.mult, op1=ALU.add).then_inc(x1_done, 1)

            loop((0, NC, 1), 2, ema_chunk)
            with dve.Fori(0, NC) as c:
                dve.wait_ge(h2_ready, c)
                norm(c + NC)
                dve.wait_ge(rms_ready, 2 * c + 2)
                V.scalar_tensor_tensor(out=cols_at(HT, c * CH, CH), in0=h2[:, :], scalar=cols[:, CN:CN + 1],
                                       in1=rstd[:, :], op0=ALU.mult, op1=ALU.mult).then_inc(xn_done, 1)

            V.tensor_copy(thr[:, 0:1], mod[:, 0:1]).then_inc(sum_free, 2)
            before = n[0]
            PER = 8 + 2 * EH - 1

            def peer_tile(t, u):
                done = [0]

                def link(ins):
                    done[0] += 1
                    ins.then_inc(dve_step, 1)
                    dve.wait_ge(dve_step, t * PER + (before + done[0]))
                    plain(dve)

                dve.wait_ge(sim_ready, t + 1)
                plain(dve)
                s = sims[:, u, :].rearrange("p (g k) -> p g k", k=NK)
                G = range(2 * EH)
                for g in G:
                    ins = V.max(srt[:, g, 0:8], s[:, g, :])
                link(ins)
                for g in G:
                    ins = V.match_replace(out=rest[:, g, :], in_to_replace=srt[:, g, 0:8], in_values=s[:, g, :],
                                          imm_value=LOWEST)
                link(ins)
                for g in G:
                    ins = V.max(srt[:, g, 8:16], rest[:, g, :])
                link(ins)
                A, B = srt[:, 0:EH, :], srt[:, EH:2 * EH, :]
                o = 0
                for i in range(5):
                    m = TOPK // (i + 1)
                    V.tensor_tensor(cand[:, :, o:o + m], A[:, :, i:i + 1].to_broadcast([P, EH, m]), B[:, :, 0:m], ALU.add)
                    o += m
                for i in range(5, 8):
                    V.tensor_tensor(cand[:, :, o:o + 2], A[:, :, i:i + 1].to_broadcast([P, EH, 2]), B[:, :, 0:2], ALU.add)
                    o += 2
                link(V.tensor_tensor(cand[:, :, o:CAND], A[:, :, 8:16], B[:, :, 0:1].to_broadcast([P, EH, 8]), ALU.add))
                for h in range(EH):
                    ins = V.max(top[:, h, 0:8], cand[:, h, :])
                link(ins)
                for h in range(EH):
                    ins = V.match_replace(out=cand2[:, h, :], in_to_replace=top[:, h, 0:8], in_values=cand[:, h, :],
                                          imm_value=LOWEST)
                link(ins)
                for h in range(EH):
                    ins = V.max(top[:, h, 8:16], cand2[:, h, :])
                link(ins)
                link(V.tensor_scalar(thr[:, :], top[:, :, TOPK - 1], 0.0, None, ALU.max))
                dve.wait_ge(weightT_ps, t)
                for h in range(EH):
                    dve.wait_ge(sum_ready, t * EH + (h + 1))
                    dst = wts[:, u, :] if h == 0 else kept[:, h % 2, :]
                    ins = V.scalar_tensor_tensor(out=dst, in0=sums[:, h % 2, :], scalar=thr[:, h:h + 1],
                                                 in1=sums[:, h % 2, :], op0=ALU.is_ge, op1=ALU.mult)
                    ins.then_inc(sum_free, 1)
                    dve.wait_ge(sum_free, t * EH + (h + 3))
                    if h:
                        ins = V.tensor_tensor(wts[:, u, :], wts[:, u, :], kept[:, h % 2, :], ALU.add)
                        if h < EH - 1:
                            link(ins)
                        else:
                            ins.then_inc(weight_ready, 1)
                for _ in range(PER - done[0]):
                    link(V.tensor_copy(sgn[:, 1:2], mod[:, 0:1]))

            def peer_back(t, u, off):
                dve.wait_ge(weightT_ps, t + 1)
                dve.wait_ge(gelu_ready, t + 1)
                dve.wait_ge(eout_ps, t)
                V.tensor_tensor(hidw[:, :], PS[:, 4 * CH:6 * CH], gelu_s[:, u, :], ALU.mult).then_inc(hidw_ready, 1)
                dve.wait_ge(eout_ps, t + 1)
                xt = cols_at(XT, off, TILE)
                V.scalar_tensor_tensor(out=xt, in0=bank(6 + u, TILE), scalar=mod[:, 5:6], in1=xt,
                                       op0=ALU.mult, op1=ALU.add).then_inc(x2_done, 1)

            skewed(dve, 0, lambda t, u, off, first=False: peer_tile(t, u), peer_back)
            n[0] = before + PER * NT

            norm_loop(2, nrm_used, NC)
            def tile1(t, u, off):
                dve.wait_ge(qkv_ps, t + 1)
                dve.wait_ge(ctx_ps, t)
                V.tensor_tensor(v1[:, u, :], bank(6 + u, TILE), bv_b[:, :], ALU.add).then_inc(v_ready, 1)
                dve.wait_ge(score_ps, t + 1)
                V.scalar_tensor_tensor(out=sc[:, :], in0=bank(2 + u, TILE + SPAN), scalar=1.0 / float(np.sqrt(D * SPAN)),
                                       in1=band[:, :], op0=ALU.mult, op1=ALU.mult).then_inc(score_ready, 1)

            pairs(dve, 0, tile1)
            with dve.Fori(0, NC) as c:
                dve.wait_ge(ln_out, c)
                norm(c + 3 * NC)
                dve.wait_ge(ln_out, c + 1)
                xt = cols_at(XT, c * CH, CH)
                V.scalar_tensor_tensor(out=xt, in0=h2[:, :], scalar=mod[:, 8:9], in1=xt,
                                       op0=ALU.mult, op1=ALU.add).then_inc(x3_done, 1)
            norm_loop(4, z0_done)

            for l in range(LAYERS):
                base = NT * l
                dve.wait_ge(rot_ready, l + 1)

                def attend(t, off, nt, link):
                    qk = PS[:, 4 * CH:6 * CH]
                    dve.wait_ge(sq2_ready, t + 1)
                    link(V.tensor_reduce(ss[:, :], sq2[:, :].rearrange("p (g d) -> p g d", d=DH), AX_X, ALU.add))
                    V.tensor_scalar(ss[:, :], ss[:, :], 1e-24, None, ALU.max).then_inc(ss_ready, 1)
                    dve.wait_ge(qkT_ps, t)
                    tab = rotL[:, bass.ds(nt, 1), :].rearrange("p a (s j d) -> p (a s) j d", s=2, j=2)
                    q4 = qk.rearrange("p (j h d) -> p j h d", j=2, h=H)
                    a4 = ra[:, :].rearrange("p (j h d) -> p j h d", j=2, h=H)
                    b4 = rb[:, :].rearrange("p (j h d) -> p j h d", j=2, h=H)
                    hd = DH // 2
                    for j in range(2):
                        V.tensor_tensor(a4[:, j], q4[:, j], tab[:, 0, j:j + 1, :].to_broadcast([P, H, DH]), ALU.mult)
                        V.tensor_tensor(b4[:, j, :, 0:hd], q4[:, j, :, hd:DH],
                                        tab[:, 1, j:j + 1, 0:hd].to_broadcast([P, H, hd]), ALU.mult)
                        ins = V.tensor_tensor(b4[:, j, :, hd:DH], q4[:, j, :, 0:hd],
                                              tab[:, 1, j:j + 1, hd:DH].to_broadcast([P, H, hd]), ALU.mult)
                    ins.then_inc(rot1_ready, 1)
                    dve.wait_ge(qkT_ps, t + 1)
                    V.tensor_copy(qT[:, :, :], bank(4).rearrange("p (a b) -> p a b", a=H // 2)).then_inc(qT_ready, 1)
                    dve.wait_ge(sim2_ps, t + 1)
                    s = PS[:, 0:4 * CH].rearrange("p (b c) -> p b c", c=CH)[:, :, 0:2 * KEYS].rearrange("p b (e k) -> p b e k", k=KEYS)
                    link(V.tensor_reduce(mx[:, :].rearrange("p (b e) -> p b e", e=2), s, AX_X, ALU.max))
                    V.tensor_scalar(nmx[:, :], mx[:, :], -QK_SCALE, None, ALU.mult).then_inc(max_ready, 1)
                    dve.wait_ge(pT_ps, t + 1)
                    V.tensor_copy(pTw[WIN:P, :, :], PS[WIN:P, 2 * CH:4 * CH].rearrange("p (a b) -> p a b", a=H)).then_inc(pTw_ready, 1)
                    link(V.reciprocal(rinv[:, :], rsum[:, :]))
                    dve.wait_ge(pv_ps, t + 1)
                    V.tensor_tensor(o_s[:, :].rearrange("p (h d) -> p h d", d=DH), bank(6).rearrange("p (h d) -> p h d", d=DH),
                                    rinv[:, :].unsqueeze(2).to_broadcast([P, H, DH]), ALU.mult).then_inc(o_ready, 1)
                    dve.wait_ge(wo_ps, t + 1)
                    V.tensor_tensor(cols_at(ZB, off + 1, TILE), bank(7, TILE), cols_at(ZA, off + 1, TILE), ALU.add).then_inc(zb_done, 1)

                loop((base, base + NT, 1), 3, lambda t, link: attend(t, (t - base) * TILE, t - base, link))

                def ffn(c, link):
                    off = (c - NC * l) * CH
                    dve.wait_ge(hn_ready, c)
                    norm(c + 5 * NC)
                    dve.wait_ge(down_ps, c)
                    for b, (o, m) in enumerate(HB):
                        dve.wait_ge(gate_ready, c * 3 + (b + 1))
                        V.scalar_tensor_tensor(out=hh[0:m, b, :], in0=PS[0:m, (3 + b % 2) * CH:(4 + b % 2) * CH],
                                               scalar=b1_s[0:m, l, b:b + 1], in1=gate[0:m, b, :],
                                               op0=ALU.add, op1=ALU.mult).then_inc(hh_ready, 1)
                    dve.wait_ge(down_ps, c + 1)
                    V.scalar_tensor_tensor(out=cols_at(ZA, off + 1, CH), in0=bank(7), scalar=cols[:, CB2 + l:CB2 + l + 1],
                                           in1=cols_at(ZB, off + 1, CH), op0=ALU.add, op1=ALU.add).then_inc(za_done, 1)

                loop((NC * l, NC * (l + 1), 1), 0, ffn)

            with dve.Fori(0, NC) as c:
                dve.wait_ge(finT_ps, c)
                V.scalar_tensor_tensor(out=fin[:, :], in0=cols_at(ZA, c * CH + 1, CH), scalar=mod[:, 11:12],
                                       in1=cols_at(XT, c * CH, CH), op0=ALU.mult, op1=ALU.add).then_inc(fin_ready, 1)


def rotary_tables():
    f = np.float32
    half = np.arange(0, DH, 2, dtype=f)
    inv_freq = (f(1.0) / np.power(f(10000.0), half / f(DH))).astype(f)
    t = np.arange(T, dtype=f)
    freqs = t[:, None] * inv_freq[None, :]
    freqs = np.concatenate([freqs, freqs], -1)
    base = (half + f(0.4 * DH)) / f(1.4 * DH)
    power = (t - f(T // 2)) / f(WIN // 2)
    scale = np.power(base[None, :], power[:, None]).astype(f)
    scale = np.concatenate([scale, scale], -1)
    cos, sin = np.cos(freqs).astype(f), np.sin(freqs).astype(f)
    sin[:, :DH // 2] *= f(-1)
    return np.ascontiguousarray(np.concatenate([cos * scale, cos / scale, sin * scale, sin / scale], -1).astype(f))


_INS = ['L0_attn_x', 'L0_attn_delta', 'L0_attn_alpha', 'L0_attn_beta', 'L0_attn_gamma', 'L0_attn_omega',
        'L0_ffn_norm_w', 'L0_ffn_wq', 'L0_ffn_keys', 'L0_ffn_expert_down', 'L0_ffn_expert_up', 'L0_c', 'L0_wmod',
        'L1_attn_W_qkv', 'L1_attn_b_qkv', 'L1_attn_ln_w', 'L1_attn_ln_b', 'L1_ffn_wqkv', 'L1_ffn_q_scale',
        'L1_ffn_k_scale', 'L1_ffn_wo', 'L1_ffn_ln_g', 'L1_ffn_ln_b', 'L1_ffn_w1', 'L1_ffn_b1', 'L1_ffn_w2',
        'L1_ffn_b2', 'L1_c', 'L1_wmod']


def kernel(**inputs):
    import concourse.bacc as bacc
    from concourse.bass_utils import run_bass_kernel_spmd

    nc = bacc.Bacc("TRN2", target_bir_lowering=False, num_devices=1)
    arrays, args = {}, []
    given = [(name, np.ascontiguousarray(inputs[name])) for name in _INS] + [("rotary", rotary_tables())]
    for name, a in given:
        arrays[f"in_{name}"] = a
        args.append(nc.dram_tensor(f"in_{name}", a.shape, mybir.dt.from_np(a.dtype), kind="ExternalInput").ap())
    args.append(nc.dram_tensor("out_0", (1, T, D), F32, kind="ExternalOutput").ap())
    build(nc, *args)
    r = run_bass_kernel_spmd(nc, [arrays], core_ids=[0])
    return r.results[0]["out_0"]
```

```python
from contextlib import ExitStack

import numpy as np

import concourse.bass as bass
from concourse import mybir
from concourse.alu_op_type import AluOpType as ALU

ACT = mybir.ActivationFunctionType
AX_X = mybir.AxisListType.X
F32 = mybir.dt.float32
BF16 = mybir.dt.bfloat16

P = 128
T = 2048
D = 128
TILE = 128
NT = T // TILE
CH = 512
NC = T // CH
CT = CH // TILE
EPS = 1e-5
EH, NK, TOPK = 8, 32, 16
NE = NK * NK
EB = NE // P
CAND = sum(TOPK // (i + 1) for i in range(TOPK))
SPAN = 32
LAYERS, H, DH, WIN = 2, 8, 64, 64
INNER = H * DH
QK_SCALE = 8.0
KEYS = WIN + TILE
HID = D * 4 * 2 // 3
HB = [(0, P), (P, P), (2 * P, HID - 2 * P)]
MASKED = -1e37
LOWEST = -3.0e38


def build(nc, x, delta, alpha, beta, gamma, omega, norm_w, wq, keys, e_down, e_up, c0, wmod0,
          w_qkv, b_qkv, ln_w, ln_b, wqkv, q_scale, k_scale, wo, ln_g, ln_bb, w1, b1, w2, b2,
          c1, wmod1, rotary, out):
    with ExitStack() as ctx:
        def sb(name, shape, dt=F32):
            return ctx.enter_context(nc.sbuf_tensor(name, shape, dt))

        def sem(name):
            return ctx.enter_context(nc.semaphore(name))

        PS = ctx.enter_context(nc.psum_tensor("PS", [P, 8 * CH], F32))

        def bank(b, n=CH):
            return PS[:, b * CH:b * CH + n]

        arena = sb("arena", [P, 9 * NE])

        def carve(start, *shape):
            n = int(np.prod(shape))
            v = arena[:, start:start + n]
            return v.rearrange("p (a b) -> p a b", a=shape[0]) if len(shape) == 2 else v

        x_tok = sb("x_tok", [P, NT, D])
        XT = sb("XT", [P, T])
        HT = sb("HT", [P, T])
        ZA = sb("ZA", [P, 1 + T])
        ZB = sb("ZB", [P, 1 + T])
        ident = sb("ident", [P, P])
        ident_bf = sb("ident_bf", [P, P], BF16)
        center = sb("center", [P, P])
        mean = sb("mean", [P, P])
        cols = sb("cols", [P, 64])
        mod_raw = sb("mod_raw", [P, 12])
        mod = sb("mod", [P, 12])
        sgn = sb("sgn", [P, 12])
        silc = sb("silc", [P, 2])
        sig = sb("sig", [P, 4])
        ema = sb("ema", [P, 8])
        eps_c = sb("eps_c", [P, 1])

        wmod_s = sb("wmod_s", [P, 2, 6 * D])
        rotL = sb("rotL", [P, NT, 4 * DH])
        flat = rotL[:, :, :].rearrange("p a b -> p (a b)")
        wq_s = flat[:, 0:2 * EH * D]
        keys_s = carve(6 * NE, 4, D)
        wqT = flat[:, 2 * EH * D:4 * EH * D].rearrange("p (a b) -> p a b", a=2 * EH)
        keysT = carve(6 * NE + 4 * D, 4 * P)
        fold = sb("fold", [P, 2 * EH * NK])
        down_s = carve(7 * NE, EB, D)
        downT = sb("downT", [P, NE])
        up_s = sb("up_s", [P, EB, D])
        wqkv1_s = sb("wqkv1_s", [P, 3 * D])
        bv_b = sb("bv_b", [P, D])
        wqkv_s = sb("wqkv_s", [P, LAYERS, 3 * INNER])
        wo_s = sb("wo_s", [P, LAYERS, INNER // P, D])
        w1_s = sb("w1_s", [P, LAYERS, 2 * HID])
        w2_s = sb("w2_s", [P, LAYERS, 3, D])
        b1_s = sb("b1_s", [P, LAYERS, 6])
        rot_s = sb("rot_s", [P, NT, 4 * DH])
        rscale = sb("rscale", [P, LAYERS, 4 * DH])
        band = sb("band", [P, P + SPAN])
        mask_bf = sb("mask_bf", [P, KEYS], BF16)
        mask0_bf = sb("mask0_bf", [P, KEYS], BF16)

        sq_s = sb("sq_s", [P, 2, CH])
        rstd = sb("rstd", [P, 2, CH])
        nrm = sb("nrm", [P, 2, CH])
        h2 = sb("h2", [P, 2, CH])

        START = 4
        counted = []

        def count(names):
            made = [sem(n) for n in names.split()]
            counted.extend(made)
            return made

        ld_x, ld_mod, ld_w0, ld_w1, ld_early, ld_late = (
            sem("ld_x"), sem("ld_mod"), sem("ld_w0"), sem("ld_w1"), sem("ld_early"), sem("ld_late"))
        passed, masks_ready = sem("passed"), sem("masks_ready")
        const_ready, stored = sem("const_ready"), sem("stored")
        pool_step, dve_step = sem("pool_step"), sem("dve_step")

        CD, CA, CB, CG, CO, CN, CBQ, CBK, CLW, CLB, CC = 0, 2, 4, 6, 8, 9, 10, 11, 12, 13, 14
        CLG, CLBB, CB2 = 16, 18, 20
        small = [
            (cols[:, CD:CD + 2], delta.rearrange("p n a -> p (n a)")),
            (cols[:, CA:CA + 2], alpha.rearrange("p n a -> p (n a)")),
            (cols[:, CB:CB + 2], beta.rearrange("p n a -> p (n a)")),
            (cols[:, CG:CG + 2], gamma),
            (cols[:, CO:CO + 1], omega.rearrange("(p a) -> p a", a=1)),
            (cols[:, CN:CN + 1], norm_w.rearrange("(p a) -> p a", a=1)),
            (cols[:, CBQ:CBQ + 2], b_qkv[0:2 * D].rearrange("(n p) -> p n", p=P)),
            (cols[:, CLW:CLW + 1], ln_w.rearrange("(p a) -> p a", a=1)),
            (cols[:, CLB:CLB + 1], ln_b.rearrange("(p a) -> p a", a=1)),
            (cols[:, CC:CC + 1], c0.rearrange("a p -> p a")),
            (cols[:, CC + 1:CC + 2], c1.rearrange("a p -> p a")),
            (cols[:, CLG:CLG + 2], ln_g.rearrange("l p -> p l")),
            (cols[:, CLBB:CLBB + 2], ln_bb.rearrange("l p -> p l")),
            (cols[:, CB2:CB2 + 2], b2.rearrange("l p -> p l")),
            (bv_b[:, :], b_qkv[2 * D:3 * D].rearrange("(a d) -> a d", a=1).to_broadcast([P, D])),
        ]
        tail = HB[2][1]
        for l in range(LAYERS):
            for g in range(2):
                o = g * HID
                small.append((b1_s[:, l, 3 * g:3 * g + 2], b1[l, o:o + 2 * P].rearrange("(n p) -> p n", p=P)))
                small.append((b1_s[0:tail, l, 3 * g + 2:3 * g + 3],
                              b1[l, o + 2 * P:o + HID].rearrange("(p a) -> p a", a=1)))
            for j, s in enumerate((q_scale, k_scale)):
                row = s[l:l + 1, :]
                small.append((rscale[:, l, j * DH:(j + 1) * DH], row.to_broadcast([P, DH])))
                o = (2 + j) * DH
                small.append((rscale[:, l, o:o + DH // 2], row[:, DH // 2:].to_broadcast([P, DH // 2])))
                small.append((rscale[:, l, o + DH // 2:o + DH], row[:, 0:DH // 2].to_broadcast([P, DH // 2])))
        EARLY = 11
        N_EARLY, N_LATE = 16 * EARLY, 16 * (len(small) - EARLY)

        mod_ready, mod_done, sig_ready, silc_ready = count("mod_ready mod_done sig_ready silc_ready")
        xT_ps, xT_done, tr_ps, tr_done = count("xT_ps xT_done tr_ps tr_done")
        fold_ps, fold_done, rot_ready = count("fold_ps fold_done rot_ready")
        cen_ready, sq_ready, var_ready, ln_ready = count("cen_ready sq_ready var_ready ln_ready")
        rstd_ready, nrm_ready, aff_ready = count("rstd_ready nrm_ready aff_ready")
        y_ready, silu_ready, x1_done = count("y_ready silu_ready x1_done")
        h2sq_ready, ms_ready, rmsln_ready, rms_ready, xn_done = count("h2sq_ready ms_ready rmsln_ready rms_ready xn_done")
        xn_ready, sim_ps, sim_ready, hid_ps, gelu_ready = count("xn_ready sim_ps sim_ready hid_ps gelu_ready")
        weightT_ps, hidw_ready, eout_ps, x2_done = count("weightT_ps hidw_ready eout_ps x2_done")
        sum_ready, kept_ready, kept_used = count("sum_ready kept_ready kept_used")
        hc_ready, qkv_ps, qk_ready, v_ready = count("hc_ready qkv_ps qk_ready v_ready")
        score_ps, score_ready, ctx_ps, ctx_done, x3_done = count("score_ps score_ready ctx_ps ctx_done x3_done")
        hs_ready, qk2_ps, v2_ps, v2_ready, sq2_ready, ss_ready = count("hs_ready qk2_ps v2_ps v2_ready sq2_ready ss_ready")
        lnss_ready, r_ready, rot1_ready, rotq_ready, rotk_ready = count("lnss_ready r_ready rot1_ready rotq_ready rotk_ready")
        ra_ready, sssum_ready, mx_ready, rinv_ready = count("ra_ready sssum_ready mx_ready rinv_ready")
        qkT_ps, qT_ready, kT_ready, sim2_ps, max_ready, p_ready = count("qkT_ps qT_ready kT_ready sim2_ps max_ready p_ready")
        pT_ps, pT_ready, pTw_ready, pv_ps, o_ready = count("pT_ps pT_ready pTw_ready pv_ps o_ready")
        oT_ps, oT_ready, wo_ps, zb_done = count("oT_ps oT_ready wo_ps zb_done")
        zs_ready, up_ps, gate_ready, hh_ready, down_ps, za_done = count("zs_ready up_ps gate_ready hh_ready down_ps za_done")
        fin_ready, finT_ps, fin_out = count("fin_ready finT_ps fin_out")

        scan1, scan2 = carve(0, CH), carve(CH, CH)
        ysum, silu_s = carve(2 * CH, 2, CH), carve(4 * CH, 2, CH)

        xn = sb("xn", [P, 2, TILE])
        sims = sb("sims", [P, 2, 2 * EH * NK])
        rest = sb("rest", [P, 2 * EH, NK])
        srt = sb("srt", [P, 2 * EH, TOPK])
        cand = sb("cand", [P, EH, CAND])
        cand2 = sb("cand2", [P, EH, CAND])
        top = sb("top", [P, EH, TOPK])
        thr = sb("thr", [P, EH])
        sums = carve(0, 4, NE)
        kept = carve(4 * NE, 2, NE)
        gelu_s = carve(6 * NE, 2, NE)
        hidw = carve(8 * NE, NE)

        hc = sb("hc", [P, 2, TILE])
        q1 = sb("q1", [P, 2, TILE])
        k1 = sb("k1", [P, 2, TILE])
        v1 = sb("v1", [P, 2, D])
        sc = sb("sc", [P, 2, TILE + SPAN])

        sq2 = carve(0 * NE, 2 * INNER)
        ss = sb("ss", [P, 2 * H])
        lnss = sb("lnss", [P, 2 * H])
        rr = sb("rr", [P, 2 * H])
        ra = carve(1 * NE, 2 * INNER)
        rb = carve(2 * NE, 2 * INNER)
        qT = sb("qT", [P, H // 2, TILE])
        kT = sb("kT", [P, 2, H // 2, TILE])
        v2 = sb("v2", [P, 2, INNER])
        mx = sb("mx", [P, H])
        nmx = sb("nmx", [P, H])
        pr = sb("pr", [P, WIN + H * KEYS])
        rsum = sb("rsum", [P, H])
        rinv = sb("rinv", [P, H])
        pT = carve(3 * NE, H, TILE)
        pTw = carve(4 * NE, H, TILE)
        o_s = carve(5 * NE, INNER)
        oT = carve(5 * NE + INNER, INNER // P, TILE)

        zs = carve(3 * NE, 2, CH)
        gate = carve(0, 3, CH)
        hh = carve(3 * CH, 3, CH)
        fin = carve(4 * NE, 2, CH)

        def turns(eng, base, ahead, step):
            looped = (NT - ahead) // 2
            with eng.Fori(0, looped) as p:
                for u in range(2):
                    step(2 * p + (base + u), u, (2 * p + u) * TILE, NT)
            for t in range(2 * looped, NT):
                step(base + t, t % 2, t * TILE, NT - 1 - t)

        def chunk_pairs(eng, k, body):
            with eng.Fori(0, NC // 2) as p:
                body(2 * p + k * NC, 2 * p)

        def plain(eng):
            eng.sem_inc(passed, 1)

        def cols_at(buf, off, n, rows=slice(0, P)):
            return buf[rows, bass.ds(off, n)]

        def place(h):
            return (h % 2) * (H // 2) + h // 2

        def scores_of(h):
            o = (place(h) // 2) * CH + (place(h) % 2) * KEYS
            return PS[:, o:o + KEYS]

        block = ctx.enter_context(nc.Block())

        @block.sync
        def _(sp):
            for s in counted:
                sp.sem_inc(s, START)
            sp.dma_start(x_tok[:, :, :], x[0].rearrange("(n p) d -> p n d", p=P)).then_inc(ld_x, 16)
            sp.dma_start(wmod_s[:, 0, :], wmod0).then_inc(ld_mod, 16)
            sp.dma_start(wmod_s[:, 1, :], wmod1).then_inc(ld_mod, 16)
            sp.dma_start(wq_s[:, :], wq).then_inc(ld_w0, 16)
            sp.dma_start(keys_s[:, :, :],
                         keys.rearrange("h k p d -> (h k p) d").rearrange("(n r) d -> r n d", r=P)).then_inc(ld_w0, 16)
            sp.dma_start(down_s[:, :, :], e_down.rearrange("(n r) d -> r n d", r=P)).then_inc(ld_w0, 16)
            sp.dma_start(up_s[:, :, :], e_up.rearrange("(n r) d -> r n d", r=P)).then_inc(ld_w0, 16)
            sp.dma_start(wqkv1_s[:, :], w_qkv).then_inc(ld_w1, 16)
            sp.dma_start(rot_s[:, :, :], rotary.rearrange("(n p) c -> p n c", p=P)).then_inc(ld_w1, 16)
            sp.dma_start(wqkv_s[:, :, :], wqkv.rearrange("l p n -> p l n")).then_inc(ld_w1, 16)
            for l in range(LAYERS):
                sp.dma_start(wo_s[:, l, :, :], wo[l].rearrange("(n p) d -> p n d", p=P)).then_inc(ld_w1, 16)
                sp.dma_start(w2_s[:, l, 0:2, :], w2[l, 0:2 * P, :].rearrange("(n p) d -> p n d", p=P)).then_inc(ld_w1, 16)
                sp.dma_start(w2_s[0:tail, l, 2, :], w2[l, 2 * P:HID, :]).then_inc(ld_w1, 16)
            sp.dma_start(w1_s[:, :, :], w1.rearrange("l p n -> p l n")).then_inc(ld_w1, 16)
            for dst, src in small[EARLY:]:
                sp.dma_start(dst, src, allow_slow_non_contiguous=True).then_inc(ld_late, 16)
            o_v = out[0].rearrange("(n p) d -> p n d", p=P)
            for c in range(NC):
                sp.wait_ge(fin_out, START + c + 1)
                sp.dma_start(o_v[:, c * CT:(c + 1) * CT, :], x_tok[:, c * CT:(c + 1) * CT, :]).then_inc(stored, 16)
            sp.wait_ge(stored, 16 * NC)
        N_W0 = 16 * 4
        N_W1 = 16 * (4 + 3 * LAYERS)

        @block.gpsimd
        def _(pool):
            n = [0]

            def step(ins):
                n[0] += 1
                ins.then_inc(pool_step, 1)
                pool.wait_ge(pool_step, n[0])

            nc.gpsimd.memset(ident[:, :], 0.0)
            nc.gpsimd.memset(center[:, :], -1.0 / D)
            nc.gpsimd.memset(mean[:, :], 1.0 / D)
            nc.gpsimd.memset(eps_c[:, :], EPS)
            step(nc.gpsimd.memset(ema[:, :], 0.0))
            step(nc.gpsimd.affine_select(out=ident[:, :], in_=ident[:, :], compare_op=ALU.not_equal, fill=1.0,
                                         base=0, pattern=[[-1, P]], channel_multiplier=1))
            nc.gpsimd.tensor_tensor(center[:, :], center[:, :], ident[:, :], ALU.add).then_inc(const_ready, 1)
            nc.gpsimd.memset(band[:, :], 1.0)
            nc.gpsimd.memset(mask_bf[:, :], 0.0)
            nc.gpsimd.memset(k1[:, :, :], 0.0)
            nc.gpsimd.memset(v1[:, :, :], 0.0)
            nc.gpsimd.memset(kT[:, 1, :, :], 0.0)
            nc.gpsimd.memset(v2[:, 1, :], 0.0)
            nc.gpsimd.memset(ZA[:, 0:1], 0.0)
            nc.gpsimd.memset(ZB[:, 0:1], 0.0)
            step(nc.gpsimd.memset(pr[:, 0:WIN], 0.0))
            own = band[:, 0:P]
            step(nc.gpsimd.affine_select(out=own, in_=own, compare_op=ALU.is_ge, fill=0.0,
                                         base=0, pattern=[[1, P]], channel_multiplier=-1))
            step(nc.gpsimd.affine_select(out=own, in_=own, compare_op=ALU.is_ge, fill=0.0,
                                         base=SPAN - 1, pattern=[[-1, P]], channel_multiplier=1))
            prev = band[:, P:P + SPAN]
            step(nc.gpsimd.affine_select(out=prev, in_=prev, compare_op=ALU.is_ge, fill=0.0,
                                         base=SPAN - 1 - P, pattern=[[-1, SPAN]], channel_multiplier=1))
            step(nc.gpsimd.affine_select(out=mask_bf[:, :], in_=mask_bf[:, :], compare_op=ALU.is_ge, fill=MASKED,
                                         base=WIN, pattern=[[-1, KEYS]], channel_multiplier=1))
            step(nc.gpsimd.affine_select(out=mask_bf[:, :], in_=mask_bf[:, :], compare_op=ALU.is_ge, fill=MASKED,
                                         base=0, pattern=[[1, KEYS]], channel_multiplier=-1))
            step(nc.gpsimd.affine_select(out=mask0_bf[:, :], in_=mask_bf[:, :], compare_op=ALU.is_ge, fill=MASKED,
                                         base=-WIN, pattern=[[1, KEYS]], channel_multiplier=0))
            nc.gpsimd.tensor_copy(ident_bf[:, :], ident[:, :]).then_inc(masks_ready, 1)

            def rotary_table(l):
                ins = nc.gpsimd.tensor_tensor(rotL[:, :, :], rot_s[:, :, :],
                                              rscale[:, l:l + 1, :].to_broadcast([P, NT, 4 * DH]), ALU.mult)
                ins.then_inc(rot_ready, 1)

            def pair_sums(t, u, off, left):
                pool.wait_ge(sim_ready, t + (START + 1))
                for h in range(EH):
                    pool.wait_ge(kept_ready, t * EH + (START + h - 3))
                    a = sims[:, u, h * NK:(h + 1) * NK].unsqueeze(2).to_broadcast([P, NK, NK])
                    b = sims[:, u, (EH + h) * NK:(EH + h + 1) * NK].unsqueeze(1).to_broadcast([P, NK, NK])
                    nc.gpsimd.tensor_tensor(sums[:, h % 4, :].rearrange("p (a b) -> p a b", a=NK), a, b,
                                            ALU.add).then_inc(sum_ready, 1)

            turns(pool, 0, 0, pair_sums)
            pool.wait_ge(ld_late, N_LATE)
            pool.wait_ge(ld_w1, N_W1)
            pool.wait_ge(fold_ps, START + 1)

            for l in range(LAYERS):
                if l:
                    pool.wait_ge(rot1_ready, START + NT * l)
                rotary_table(l)

                def scale_k(t, u, off, left):
                    pool.wait_ge(ra_ready, t + (START + 1))
                    pool.wait_ge(r_ready, t + (START + 1))
                    v = ra[:, INNER:2 * INNER].rearrange("p (g d) -> p g d", d=DH)
                    nc.gpsimd.tensor_tensor(v, v, rr[:, H:2 * H].unsqueeze(2).to_broadcast([P, H, DH]),
                                            ALU.mult).then_inc(rotk_ready, 1)

                turns(pool, NT * l, 0, scale_k)

        @block.scalar
        def _(act):
            A = nc.scalar
            for dst, src in small[0:EARLY]:
                act.dma_start(dst, src, allow_slow_non_contiguous=True).then_inc(ld_early, 16)
            for c in range(NC):
                act.wait_ge(xT_ps, START + c + 1)
                A.copy(XT[:, c * CH:(c + 1) * CH], bank(c)).then_inc(xT_done, 1)
            act.wait_ge(ld_early, N_EARLY)
            A.activation(silc[:, :], cols[:, CC:CC + 2], ACT.Silu).then_inc(silc_ready, 1)
            A.activation(sig[:, :], cols[:, CD:CD + 4], ACT.Sigmoid).then_inc(sig_ready, 1)
            act.wait_ge(const_ready, 1)

            def exp_and_ln():
                A.preload_act_table_set("natural_log_exp_and_others")

            def norm(k, dst, scale, bias, free=None):
                for u in range(2):
                    act.wait_ge(cen_ready, k + (START + u + 1))
                    A.activation(sq_s[:, u, :], bank(u), ACT.Square).then_inc(sq_ready, 1)
                for u in range(2):
                    act.wait_ge(var_ready, k + (START + u + 1))
                    act.wait_ge(nrm_ready, k + (START + u - 1))
                    A.activation(rstd[:, u, :], bank(2 + u), ACT.Ln, bias=eps_c[:, 0:1]).then_inc(ln_ready, 1)
                for u in range(2):
                    act.wait_ge(ln_ready, k + (START + u + 1))
                    A.activation(rstd[:, u, :], rstd[:, u, :], ACT.Exp, scale=-0.5).then_inc(rstd_ready, 1)
                for u in range(2):
                    if free is not None:
                        act.wait_ge(free[0], free[1] + (START + u - 1))
                    act.wait_ge(nrm_ready, k + (START + u + 1))
                    A.activation(dst(u), nrm[:, u, :], ACT.Identity, scale=scale, bias=bias).then_inc(aff_ready, 1)

            exp_and_ln()
            act.wait_ge(mod_done, START + 1)
            chunk_pairs(act, 0, lambda k, c: norm(k, lambda u: cols_at(HT, (c + u) * CH, CH), mod[:, 1:2], mod[:, 0:1]))
            for g in range(7):
                act.wait_ge(tr_ps, START + g + 1)
                dst = (wqT[:, 4 * g:4 * g + 4, :] if g < 4 else
                       (keysT[:, :] if g == 4 else downT[:, (g - 5) * CH:(g - 4) * CH]).rearrange("p (a b) -> p a b", a=4))
                A.copy(dst, bank(4 + g % 2).rearrange("p (a b) -> p a b", a=4)).then_inc(tr_done, 1)
            act.wait_ge(fold_ps, START + 1)
            A.copy(fold[:, :], bank(6)).then_inc(fold_done, 1)
            for c in range(NC):
                act.wait_ge(y_ready, START + c + 1)
                act.wait_ge(x1_done, START + c - 1)
                A.activation(silu_s[:, c % 2, :], ysum[:, c % 2, :], ACT.Silu).then_inc(silu_ready, 1)

            def rms(k, c):
                norm(k, lambda u: h2[:, u, :], mod[:, 4:5], mod[:, 3:4], (xn_done, c))
                for u in range(2):
                    act.wait_ge(aff_ready, k + (START + u + 1))
                    A.activation(sq_s[:, u, :], h2[:, u, :], ACT.Square).then_inc(h2sq_ready, 1)
                for u in range(2):
                    act.wait_ge(ms_ready, c + (START + u + 1))
                    A.activation(rstd[:, u, :], bank(4 + u), ACT.Ln, bias=eps_c[:, 0:1]).then_inc(rmsln_ready, 1)
                for u in range(2):
                    act.wait_ge(rmsln_ready, c + (START + u + 1))
                    A.activation(rstd[:, u, :], rstd[:, u, :], ACT.Exp, scale=-0.5).then_inc(rms_ready, 1)
                act.wait_ge(xn_done, c + (START + 2))

            exp_and_ln()
            chunk_pairs(act, 1, rms)

            def copy_xn(t, u, off):
                act.wait_ge(hid_ps, t + (START - 1))
                plain(act)
                A.copy(xn[:, u, :], cols_at(HT, off, TILE)).then_inc(xn_ready, 1)

            def copy_sim(t, u):
                act.wait_ge(sim_ps, t + (START + 1))
                act.wait_ge(kept_ready, t * EH + (START - EH))
                A.copy(sims[:, u, :], bank(u)).then_inc(sim_ready, 1)

            def gelu(t, u):
                act.wait_ge(hid_ps, t + (START + 1))
                act.wait_ge(hidw_ready, t + (START - 1))
                A.activation(gelu_s[:, u, :], PS[:, 2 * CH:4 * CH], ACT.Gelu).then_inc(gelu_ready, 1)

            A.copy(xn[:, 0, :], HT[:, 0:TILE]).then_inc(xn_ready, 1)
            act.wait_ge(sim_ps, START + 1)
            A.copy(sims[:, 0, :], bank(0)).then_inc(sim_ready, 1)
            A.copy(xn[:, 1, :], HT[:, TILE:2 * TILE]).then_inc(xn_ready, 1)
            gelu(0, 0)

            def peer(t, u, off, left):
                if left >= 1:
                    copy_sim(t + 1, 1 - u)
                if left >= 2:
                    copy_xn(t + 2, u, off + 2 * TILE)
                if left >= 1:
                    gelu(t + 1, 1 - u)

            turns(act, 0, 2, peer)

            exp_and_ln()
            chunk_pairs(act, 2, lambda k, c: norm(k, lambda u: cols_at(HT, (c + u) * CH, CH), mod[:, 7:8], mod[:, 6:7]))

            def copy_hc(t, u, off):
                act.wait_ge(qkv_ps, t + (START - 1))
                plain(act)
                A.copy(hc[:, u, :], cols_at(HT, off, TILE)).then_inc(hc_ready, 1)

            def bias_qk(t, u):
                act.wait_ge(qkv_ps, t + (START + 1))
                act.wait_ge(score_ps, t + START)
                A.activation(q1[:, u, :], bank(u)[:, 0:TILE], ACT.Identity, bias=cols[:, CBQ:CBQ + 1])
                A.activation(k1[:, u, :], bank(u)[:, TILE:2 * TILE], ACT.Identity,
                             bias=cols[:, CBK:CBK + 1]).then_inc(qk_ready, 1)

            act.wait_ge(aff_ready, START + 3 * NC)
            A.copy(hc[:, 0, :], HT[:, 0:TILE]).then_inc(hc_ready, 1)
            A.copy(hc[:, 1, :], HT[:, TILE:2 * TILE]).then_inc(hc_ready, 1)
            bias_qk(0, 0)

            def band_attend(t, u, off, left):
                if left >= 1:
                    bias_qk(t + 1, 1 - u)
                if left >= 2:
                    copy_hc(t + 2, u, off + 2 * TILE)
                act.wait_ge(ctx_ps, t + (START + 1))
                plain(act)
                A.copy(cols_at(HT, off, TILE), bank(4 + u, TILE)).then_inc(ctx_done, 1)

            turns(act, 0, 2, band_attend)
            chunk_pairs(act, 3, lambda k, c: norm(k, lambda u: h2[:, u, :], cols[:, CLW:CLW + 1], cols[:, CLB:CLB + 1],
                                                  (x3_done, c)))
            chunk_pairs(act, 4, lambda k, c: norm(k, lambda u: cols_at(ZA, (c + u) * CH + 1, CH), mod[:, 10:11], mod[:, 9:10]))

            for l in range(LAYERS):
                base = NT * l
                act.wait_ge(*((za_done, START + NC * l) if l else (aff_ready, START + 5 * NC)))

                def shifted(t, u, off):
                    act.wait_ge(v2_ps, t + (START - 1))
                    plain(act)
                    A.copy(hc[0:DH, u, :], cols_at(ZA, off + 1, TILE, slice(0, DH)))
                    A.copy(hc[DH:P, u, :], cols_at(ZA, off, TILE, slice(DH, P))).then_inc(hs_ready, 1)

                def squares(t):
                    act.wait_ge(rot1_ready, t + (START + 1))
                    A.activation(sq2[:, :], PS[:, 4 * CH:6 * CH], ACT.Square).then_inc(sq2_ready, 1)

                def copy_v(t, u):
                    act.wait_ge(v2_ps, t + (START + 1))
                    A.copy(v2[:, u, :], bank(6)).then_inc(v2_ready, 1)

                def inv_norms(t):
                    act.wait_ge(ss_ready, t + (START + 1))
                    A.activation(lnss[:, :], ss[:, :], ACT.Ln).then_inc(lnss_ready, 1)
                    act.wait_ge(lnss_ready, t + (START + 1))
                    act.wait_ge(rotq_ready, t + START)
                    act.wait_ge(rotk_ready, t + START)
                    A.activation(rr[:, :], lnss[:, :], ACT.Exp, scale=-0.5).then_inc(r_ready, 1)

                def copy_kT(t, u):
                    act.wait_ge(qkT_ps, t + (START + 1))
                    A.copy(kT[:, u, :, :], bank(5).rearrange("p (a b) -> p a b", a=H // 2)).then_inc(kT_ready, 1)

                def exps(t):
                    act.wait_ge(max_ready, t + (START + 1))
                    for h in range(H):
                        ins = A.activation(pr[:, WIN + h * KEYS:WIN + (h + 1) * KEYS], scores_of(h), ACT.Exp,
                                           scale=QK_SCALE, bias=nmx[:, place(h):place(h) + 1],
                                           accum_out=rsum[:, h:h + 1])
                        if h % 4 == 3:
                            ins.then_inc(p_ready, 1)

                def copy_pT(t):
                    act.wait_ge(pT_ps, t + (START + 1))
                    A.copy(pT[:, :, :], PS[:, 0:2 * CH].rearrange("p (a b) -> p a b", a=H)).then_inc(pT_ready, 1)

                def copy_oT(t):
                    act.wait_ge(oT_ps, t + (START + 1))
                    A.copy(oT[:, :, :], bank(7).rearrange("p (a b) -> p a b", a=INNER // P)).then_inc(oT_ready, 1)

                shifted(base, 0, 0)
                shifted(base + 1, 1, TILE)
                squares(base)
                inv_norms(base)
                copy_kT(base, 0)
                exps(base)
                squares(base + 1)
                copy_v(base, 0)
                inv_norms(base + 1)
                shifted(base + 2, 0, 2 * TILE)

                def attend(t, u, off, left):
                    copy_pT(t)
                    if left >= 1:
                        copy_kT(t + 1, 1 - u)
                    copy_oT(t)
                    if left >= 1:
                        exps(t + 1)
                    if left >= 2:
                        squares(t + 2)
                    if left >= 1:
                        copy_v(t + 1, 1 - u)
                    if left >= 2:
                        inv_norms(t + 2)
                    if left >= 3:
                        shifted(t + 3, 1 - u, off + 3 * TILE)

                turns(act, base, 3, attend)

                chunk_pairs(act, 5 + l, lambda k, c: norm(k, lambda u: cols_at(HT, (c + u) * CH, CH),
                                                          cols[:, CLG + l:CLG + l + 1], cols[:, CLBB + l:CLBB + l + 1]))

                with act.Fori(NC * l, NC * (l + 1)) as c:
                    for b, (o, m) in enumerate(HB):
                        act.wait_ge(up_ps, c * 3 + (START + b + 1))
                        act.wait_ge(hh_ready, c * 3 + (START + b - 2))
                        A.activation(gate[0:m, b, :], PS[0:m, (5 + b % 2) * CH:(6 + b % 2) * CH], ACT.Gelu,
                                     bias=b1_s[0:m, l, 3 + b:4 + b]).then_inc(gate_ready, 1)
                if l < LAYERS - 1:
                    exp_and_ln()

            for c in range(NC):
                act.wait_ge(finT_ps, START + c + 1)
                A.copy(x_tok[:, c * CT:(c + 1) * CT, :], bank(c % 2).rearrange("p (a b) -> p a b", a=CT)).then_inc(fin_out, 1)

        @block.tensor
        def _(pe):
            def mm(o, w, m, start=True, stop=True):
                return nc.tensor.matmul(o, w, m, start=start, stop=stop)

            def add(o, w, m, start=False):
                return nc.tensor.matmul(o, w, m, start=start, stop=True, skip_group_check=True)

            pe.wait_ge(const_ready, 1)
            pe.wait_ge(ld_x, 16)
            for c in range(NC):
                for j in range(CT):
                    ins = nc.tensor.transpose(bank(c)[:, j * TILE:(j + 1) * TILE], x_tok[:, c * CT + j, :], ident[:, :])
                ins.then_inc(xT_ps, 1)
            pe.wait_ge(ld_mod, 32)
            pe.wait_ge(silc_ready, START + 1)
            for l in range(2):
                for j in range(6):
                    ins = mm(bank(7)[:, 6 * l + j:6 * l + j + 1], wmod_s[:, l, j * D:(j + 1) * D], silc[:, l:l + 1])
            ins.then_inc(mod_ready, 1)
            pe.wait_ge(xT_done, START + NC)

            def norm(k, src, ready=None):
                for u in range(2):
                    pe.wait_ge(nrm_ready, k + (START + u - 1))
                    if ready is not None:
                        pe.wait_ge(ready[0], ready[1] + (START + u + 1))
                    mm(bank(u), center[:, :], src(u)).then_inc(cen_ready, 1)
                for u in range(2):
                    pe.wait_ge(sq_ready, k + (START + u + 1))
                    mm(bank(2 + u), mean[:, :], sq_s[:, u, :]).then_inc(var_ready, 1)

            chunk_pairs(pe, 0, lambda k, c: norm(k, lambda u: cols_at(XT, (c + u) * CH, CH)))
            pe.wait_ge(ld_w0, N_W0)
            for g in range(7):
                if g >= 2:
                    pe.wait_ge(tr_done, START + g - 1)
                for j in range(4):
                    src = (wq_s[:, (4 * g + j) * D:(4 * g + j + 1) * D] if g < 4 else
                           keys_s[:, j, :] if g == 4 else down_s[:, 4 * (g - 5) + j, :])
                    ins = nc.tensor.transpose(bank(4 + g % 2)[:, j * P:(j + 1) * P], src, ident[:, :])
                ins.then_inc(tr_ps, 1)
            pe.wait_ge(tr_done, START + 5)
            kv = keysT[:, :].rearrange("p (h k a) -> p h a k", h=EH, a=2)
            for a in range(2):
                for h in range(EH):
                    o = (a * EH + h) * NK
                    ins = mm(bank(6)[:, o:o + NK], wqT[:, 2 * h + a, :], kv[:, h, a, :])
            ins.then_inc(fold_ps, 1)
            pe.wait_ge(tr_done, START + 7)
            pe.wait_ge(x1_done, START + NC)

            def rms(k, c):
                norm(k, lambda u: cols_at(XT, (c + u) * CH, CH))
                for u in range(2):
                    pe.wait_ge(h2sq_ready, c + (START + u + 1))
                    mm(bank(4 + u), mean[:, :], sq_s[:, u, :]).then_inc(ms_ready, 1)

            chunk_pairs(pe, 1, rms)

            pe.wait_ge(fold_done, START + 1)

            def key_scores(t, u):
                pe.wait_ge(xn_ready, t + (START + 1))
                pe.wait_ge(sim_ready, t + (START - 1))
                mm(bank(u), xn[:, u, :], fold[:, :]).then_inc(sim_ps, 1)

            def hidden(t, u):
                pe.wait_ge(gelu_ready, t + START)
                for e in range(EB):
                    ins = mm(PS[:, 2 * CH + e * P:2 * CH + (e + 1) * P], downT[:, e * P:(e + 1) * P], xn[:, u, :])
                ins.then_inc(hid_ps, 1)

            def weights(t):
                for h in range(EH):
                    pe.wait_ge(kept_ready, t * EH + (START + h + 1))
                    for e in range(EB):
                        ins = add(PS[:, 4 * CH + e * P:4 * CH + (e + 1) * P], kept[:, h % 2, e * P:(e + 1) * P],
                                  ident[:, :], start=(h == 0 and e % 4 == 0))
                    ins.then_inc(kept_used, 1)
                    if h == EH - 1:
                        pe.wait_ge(kept_used, t * EH + (START + EH))
                        pe.sem_inc(weightT_ps, 1)

            def experts_out(t, u):
                pe.wait_ge(hidw_ready, t + (START + 1))
                pe.wait_ge(x2_done, t + (START - 1))
                for e in range(EB):
                    ins = mm(bank(6 + u, TILE), up_s[:, e, :], hidw[:, e * P:(e + 1) * P], e == 0, e == EB - 1)
                ins.then_inc(eout_ps, 1)

            key_scores(0, 0)
            hidden(0, 0)
            key_scores(1, 1)
            weights(0)
            hidden(1, 1)

            def peer(t, u, off, left):
                if left >= 2:
                    key_scores(t + 2, u)
                experts_out(t, u)
                if left >= 1:
                    weights(t + 1)
                if left >= 2:
                    hidden(t + 2, u)

            turns(pe, 0, 2, peer)

            pe.wait_ge(x2_done, START + NT)
            chunk_pairs(pe, 2, lambda k, c: norm(k, lambda u: cols_at(XT, (c + u) * CH, CH)))
            pe.wait_ge(ld_w1, N_W1)
            pe.wait_ge(nrm_ready, START + 3 * NC)

            def qkv(t, u):
                pe.wait_ge(hc_ready, t + (START + 1))
                pe.wait_ge(qk_ready, t + (START - 1))
                pe.wait_ge(v_ready, t + (START - 1))
                mm(bank(u)[:, 0:TILE], wqkv1_s[:, 0:D], hc[:, u, :])
                mm(bank(u)[:, TILE:2 * TILE], wqkv1_s[:, D:2 * D], hc[:, u, :])
                mm(bank(6 + u, TILE), hc[:, u, :], wqkv1_s[:, 2 * D:3 * D]).then_inc(qkv_ps, 1)

            def scores(t, u):
                pe.wait_ge(qk_ready, t + (START + 1))
                pe.wait_ge(score_ready, t + (START - 1))
                mm(bank(2 + u)[:, 0:TILE], k1[:, u, :], q1[:, u, :])
                mm(bank(2 + u)[:, TILE:TILE + SPAN], k1[:, 1 - u, :], q1[:, u, 0:SPAN]).then_inc(score_ps, 1)

            def context(t, u):
                pe.wait_ge(score_ready, t + (START + 1))
                pe.wait_ge(v_ready, t + (START + 1))
                pe.wait_ge(ctx_done, t + (START - 1))
                o = bank(4 + u, TILE)
                mm(o, v1[:, u, :], sc[:, u, 0:TILE])
                add(o[:, 0:SPAN], v1[:, 1 - u, :], sc[:, u, TILE:TILE + SPAN]).then_inc(ctx_ps, 1)

            qkv(0, 0)
            scores(0, 0)

            def band_attend(t, u, off, left):
                if left >= 1:
                    qkv(t + 1, 1 - u)
                context(t, u)
                if left >= 1:
                    scores(t + 1, 1 - u)

            turns(pe, 0, 1, band_attend)
            pe.wait_ge(ctx_done, START + NT)
            chunk_pairs(pe, 3, lambda k, c: norm(k, lambda u: cols_at(HT, (c + u) * CH, CH)))
            chunk_pairs(pe, 4, lambda k, c: norm(k, lambda u: cols_at(XT, (c + u) * CH, CH), (x3_done, c)))
            pe.wait_ge(aff_ready, START + 5 * NC)
            pe.wait_ge(masks_ready, 1)

            for l in range(LAYERS):
                base = NT * l

                def project_qk(t, u):
                    pe.wait_ge(hs_ready, t + (START + 1))
                    pe.wait_ge(qT_ready, t + START)
                    pe.wait_ge(kT_ready, t + START)
                    mm(bank(4), hc[:, u, :], wqkv_s[:, l, 0:INNER])
                    mm(bank(5), hc[:, u, :], wqkv_s[:, l, INNER:2 * INNER]).then_inc(qk2_ps, 1)

                def project_v(t, u):
                    pe.wait_ge(o_ready, t + START)
                    mm(bank(6), hc[:, u, :], wqkv_s[:, l, 2 * INNER:3 * INNER]).then_inc(v2_ps, 1)

                def turn_qk(t):
                    pe.wait_ge(rotq_ready, t + (START + 1))
                    pe.wait_ge(rotk_ready, t + (START + 1))
                    pe.wait_ge(sq2_ready, t + (START + 1))
                    for g in range(H):
                        ins = nc.tensor.transpose(PS[:, 4 * CH + g * P:4 * CH + (g + 1) * P], ra[:, g * P:(g + 1) * P], ident[:, :])
                    ins.then_inc(qkT_ps, 1)

                def masked_scores(t, u, m):
                    pe.wait_ge(pT_ready, t + START)
                    pe.wait_ge(pTw_ready, t + START)
                    for h in range(H):
                        add(scores_of(h), ident_bf[:, :], m[:, :], start=(place(h) % 2 == 0))
                    pe.wait_ge(qT_ready, t + (START + 1))
                    pe.wait_ge(kT_ready, t + (START + 1))
                    for h in range(H):
                        rows = slice(DH * (h % 2), DH * (h % 2) + DH)
                        add(scores_of(h)[:, 0:WIN], qT[rows, h // 2, :], kT[rows, 1 - u, h // 2, WIN:TILE])
                        ins = add(scores_of(h)[:, WIN:KEYS], qT[rows, h // 2, :], kT[rows, u, h // 2, :])
                    ins.then_inc(sim2_ps, 1)

                def turn_p(t):
                    for h in range(H):
                        if h % 4 == 0:
                            pe.wait_ge(p_ready, 2 * t + (START + h // 4 + 1))
                            if h == 0:
                                pe.wait_ge(p_ready, 2 * t + (START + 2))
                        o = WIN + h * KEYS
                        nc.tensor.transpose(PS[:, h * P:(h + 1) * P], pr[:, o + WIN:o + KEYS], ident[:, :])
                        ins = nc.tensor.transpose(PS[:, 2 * CH + h * P:2 * CH + (h + 1) * P], pr[:, o - WIN:o + WIN], ident[:, :])
                    ins.then_inc(pT_ps, 1)

                def weigh_v(t, u):
                    pe.wait_ge(pT_ready, t + (START + 1))
                    pe.wait_ge(pTw_ready, t + (START + 1))
                    pe.wait_ge(v2_ready, t + (START + 1))
                    for h in range(H):
                        o = bank(6)[:, h * DH:(h + 1) * DH]
                        add(o, pT[:, h, :], v2[:, u, h * DH:(h + 1) * DH], start=(h == 0))
                    for h in range(H):
                        o = bank(6)[:, h * DH:(h + 1) * DH]
                        ins = add(o, pTw[WIN:P, h, :], v2[WIN:P, 1 - u, h * DH:(h + 1) * DH])
                    ins.then_inc(pv_ps, 1)

                def turn_o(t):
                    pe.wait_ge(o_ready, t + (START + 1))
                    pe.wait_ge(zb_done, t + START)
                    for g in range(INNER // P):
                        ins = nc.tensor.transpose(bank(7)[:, g * P:(g + 1) * P], o_s[:, g * P:(g + 1) * P], ident[:, :])
                    ins.then_inc(oT_ps, 1)

                def project_o(t):
                    pe.wait_ge(oT_ready, t + (START + 1))
                    for g in range(INNER // P):
                        ins = mm(bank(7, TILE), wo_s[:, l, g, :], oT[:, g, :], g == 0, g == INNER // P - 1)
                    ins.then_inc(wo_ps, 1)

                project_qk(base, 0)
                turn_qk(base)
                masked_scores(base, 0, mask0_bf)
                project_qk(base + 1, 1)
                project_v(base, 0)

                def attend(t, u, off, left):
                    turn_p(t)
                    if left >= 1:
                        turn_qk(t + 1)
                    weigh_v(t, u)
                    if left >= 1:
                        masked_scores(t + 1, 1 - u, mask_bf)
                    turn_o(t)
                    if left >= 2:
                        project_qk(t + 2, u)
                    if left >= 1:
                        project_v(t + 1, 1 - u)
                    project_o(t)

                turns(pe, base, 2, attend)

                chunk_pairs(pe, 5 + l, lambda k, c: norm(k, lambda u: zs[:, u, :], (zs_ready, c + NC * l)))
                with pe.Fori(NC * l, NC * (l + 1)) as c:
                    pe.wait_ge(aff_ready, START + (6 + l) * NC)
                    hn = cols_at(HT, (c - NC * l) * CH, CH)
                    for b, (o, m) in enumerate(HB):
                        if b == 0:
                            pe.wait_ge(hh_ready, c * 3 + START)
                        elif b == 2:
                            pe.wait_ge(hh_ready, c * 3 + (START + 1))
                        mm(PS[0:m, (3 + b % 2) * CH:(4 + b % 2) * CH], w1_s[:, l, o:o + m], hn)
                        mm(PS[0:m, (5 + b % 2) * CH:(6 + b % 2) * CH], w1_s[:, l, HID + o:HID + o + m], hn).then_inc(up_ps, 1)
                    pe.wait_ge(hh_ready, c * 3 + (START + 3))
                    pe.wait_ge(za_done, c + START)
                    for b, (o, m) in enumerate(HB):
                        ins = mm(bank(7), w2_s[0:m, l, b, :], hh[0:m, b, :], b == 0, b == 2)
                    ins.then_inc(down_ps, 1)
                pe.wait_ge(za_done, START + NC * (l + 1))

            for c in range(NC):
                pe.wait_ge(fin_ready, START + c + 1)
                pe.wait_ge(fin_out, START + c - 1)
                for j in range(CT):
                    ins = nc.tensor.transpose(bank(c % 2)[:, j * TILE:(j + 1) * TILE], fin[:, c % 2, j * TILE:(j + 1) * TILE], ident[:, :])
                ins.then_inc(finT_ps, 1)

        @block.vector
        def _(dve):
            V = nc.vector
            n = [0]

            def step(ins):
                n[0] += 1
                ins.then_inc(dve_step, 1)
                dve.wait_ge(dve_step, n[0])

            dve.wait_ge(mod_ready, START + 1)
            step(V.tensor_copy(mod_raw[:, :], bank(7, 12)))
            step(V.tensor_copy(mod[:, :], mod_raw[:, :]))
            step(V.tensor_scalar(sgn[:, :], mod_raw[:, :], 0.0, 2.0, ALU.is_ge, ALU.mult))
            for l in range(2):
                for j in (1, 4):
                    V.tensor_scalar(mod[:, 6 * l + j:6 * l + j + 1], mod_raw[:, 6 * l + j:6 * l + j + 1], 1.0, None, ALU.add)
            step(V.tensor_scalar(sgn[:, :], sgn[:, :], -1.0, None, ALU.add))
            for op, s, b in ((ALU.mult, 1, ALU.max), (ALU.mult, 0, None)):
                for l in range(2):
                    for j in (2, 5):
                        o = 6 * l + j
                        if b is not None:
                            ins = V.tensor_scalar(mod[:, o:o + 1], mod_raw[:, o:o + 1], sgn[:, o:o + 1], 0.25, op, b)
                        else:
                            ins = V.tensor_tensor(mod[:, o:o + 1], mod[:, o:o + 1], sgn[:, o:o + 1], op)
                step(ins)
            V.tensor_copy(sgn[:, 0:1], mod[:, 0:1]).then_inc(mod_done, 1)
            dve.wait_ge(sig_ready, START + 1)
            dve.wait_ge(const_ready, 1)
            step(V.tensor_tensor(ema[:, 0:2], sig[:, 0:2], sig[:, 2:4], ALU.mult))
            V.tensor_tensor(ema[:, 2:4], sig[:, 0:2], cols[:, CB:CB + 2], ALU.mult)
            step(V.tensor_scalar(ema[:, 4:6], cols[:, CG:CG + 2], float(np.sqrt(0.5)), None, ALU.mult))
            V.tensor_scalar(ema[:, 0:2], ema[:, 0:2], -1.0, 1.0, ALU.mult, ALU.add)
            step(V.tensor_tensor(ema[:, 2:4], ema[:, 2:4], ema[:, 4:6], ALU.mult))

            def norm(k):
                for u in range(2):
                    dve.wait_ge(rstd_ready, k + (START + u + 1))
                    dve.wait_ge(aff_ready, k + (START + u - 1))
                    V.tensor_tensor(nrm[:, u, :], bank(u), rstd[:, u, :], ALU.mult).then_inc(nrm_ready, 1)

            chunk_pairs(dve, 0, lambda k, c: norm(k))

            def ema_scan(c):
                u = c % 2
                dve.wait_ge(aff_ready, START + c + 1)
                h = HT[:, c * CH:(c + 1) * CH]
                dve.wait_ge(silu_ready, START + c - 1)
                dve.wait_ge(y_ready, START + c)
                V.tensor_tensor_scan(scan1[:, :], ema[:, 0:1].to_broadcast([P, CH]), h, ema[:, 6:7], ALU.mult, ALU.add)
                V.tensor_tensor_scan(scan2[:, :], ema[:, 1:2].to_broadcast([P, CH]), h, ema[:, 7:8], ALU.mult, ALU.add)
                step(V.tensor_scalar(ysum[:, u, :], h, cols[:, CO:CO + 1], None, ALU.mult))
                V.tensor_copy(ema[:, 6:7], scan1[:, CH - 1:CH])
                V.tensor_copy(ema[:, 7:8], scan2[:, CH - 1:CH])
                step(V.scalar_tensor_tensor(out=ysum[:, u, :], in0=scan1[:, :], scalar=ema[:, 2:3], in1=ysum[:, u, :],
                                            op0=ALU.mult, op1=ALU.add))
                V.scalar_tensor_tensor(out=ysum[:, u, :], in0=scan2[:, :], scalar=ema[:, 3:4], in1=ysum[:, u, :],
                                       op0=ALU.mult, op1=ALU.add).then_inc(y_ready, 1)

            def ema_out(c):
                dve.wait_ge(silu_ready, START + c + 1)
                xt = XT[:, c * CH:(c + 1) * CH]
                V.scalar_tensor_tensor(out=xt, in0=silu_s[:, c % 2, :], scalar=mod[:, 2:3], in1=xt,
                                       op0=ALU.mult, op1=ALU.add).then_inc(x1_done, 1)

            for c in range(NC):
                ema_scan(c)
                if c:
                    ema_out(c - 1)
            ema_out(NC - 1)

            def rms(k, c):
                norm(k)
                for u in range(2):
                    dve.wait_ge(rms_ready, c + (START + u + 1))
                    V.scalar_tensor_tensor(out=cols_at(HT, (c + u) * CH, CH), in0=h2[:, u, :], scalar=cols[:, CN:CN + 1],
                                           in1=rstd[:, u, :], op0=ALU.mult, op1=ALU.mult).then_inc(xn_done, 1)

            chunk_pairs(dve, 1, rms)

            before = n[0]
            PER = 8

            def hidden_weights(t, u):
                dve.wait_ge(weightT_ps, t + (START + 1))
                dve.wait_ge(gelu_ready, t + (START + 1))
                dve.wait_ge(eout_ps, t + START)
                V.tensor_tensor(hidw[:, :], PS[:, 4 * CH:6 * CH], gelu_s[:, u, :], ALU.mult).then_inc(hidw_ready, 1)

            def residual(t, u, off):
                dve.wait_ge(eout_ps, t + (START + 1))
                xt = cols_at(XT, off, TILE)
                V.scalar_tensor_tensor(out=xt, in0=bank(6 + u, TILE), scalar=mod[:, 5:6], in1=xt,
                                       op0=ALU.mult, op1=ALU.add).then_inc(x2_done, 1)

            def peer(t, u, off, left, first=False):
                done = [0]

                def link(ins):
                    done[0] += 1
                    ins.then_inc(dve_step, 1)
                    dve.wait_ge(dve_step, t * PER + (before + done[0]))
                    if not first:
                        plain(dve)

                dve.wait_ge(sim_ready, t + (START + 1))
                if not first:
                    plain(dve)
                s = sims[:, u, :].rearrange("p (g k) -> p g k", k=NK)
                G = range(2 * EH)
                for g in G:
                    ins = V.max(srt[:, g, 0:8], s[:, g, :])
                link(ins)
                for g in G:
                    ins = V.match_replace(out=rest[:, g, :], in_to_replace=srt[:, g, 0:8], in_values=s[:, g, :],
                                          imm_value=LOWEST)
                link(ins)
                for g in G:
                    ins = V.max(srt[:, g, 8:16], rest[:, g, :])
                link(ins)
                A, B = srt[:, 0:EH, :], srt[:, EH:2 * EH, :]
                o = 0
                for i in range(5):
                    m = TOPK // (i + 1)
                    V.tensor_tensor(cand[:, :, o:o + m], A[:, :, i:i + 1].to_broadcast([P, EH, m]), B[:, :, 0:m], ALU.add)
                    o += m
                for i in range(5, 8):
                    V.tensor_tensor(cand[:, :, o:o + 2], A[:, :, i:i + 1].to_broadcast([P, EH, 2]), B[:, :, 0:2], ALU.add)
                    o += 2
                link(V.tensor_tensor(cand[:, :, o:CAND], A[:, :, 8:16], B[:, :, 0:1].to_broadcast([P, EH, 8]), ALU.add))
                for h in range(EH):
                    ins = V.max(top[:, h, 0:8], cand[:, h, :])
                link(ins)
                for h in range(EH):
                    ins = V.match_replace(out=cand2[:, h, :], in_to_replace=top[:, h, 0:8], in_values=cand[:, h, :],
                                          imm_value=LOWEST)
                link(ins)
                for h in range(EH):
                    ins = V.max(top[:, h, 8:16], cand2[:, h, :])
                link(ins)
                link(V.tensor_scalar(thr[:, :], top[:, :, TOPK - 1], 0.0, None, ALU.max))
                assert done[0] == PER
                if not first:
                    hidden_weights(t - 1, 1 - u)
                for h in range(EH):
                    dve.wait_ge(sum_ready, t * EH + (START + h + 1))
                    dve.wait_ge(kept_used, t * EH + (START + h - 1))
                    V.scalar_tensor_tensor(out=kept[:, h % 2, :], in0=sums[:, h % 4, :], scalar=thr[:, h:h + 1],
                                           in1=sums[:, h % 4, :], op0=ALU.is_ge, op1=ALU.mult).then_inc(kept_ready, 1)
                if not first:
                    residual(t - 1, 1 - u, off - TILE)

            peer(0, 0, 0, NT, first=True)
            peer(1, 1, TILE, NT)
            with dve.Fori(1, NT // 2) as p:
                for u in range(2):
                    peer(2 * p + u, u, (2 * p + u) * TILE, NT)
            hidden_weights(NT - 1, 1)
            residual(NT - 1, 1, (NT - 1) * TILE)
            n[0] = before + PER * NT

            chunk_pairs(dve, 2, lambda k, c: norm(k))
            dve.wait_ge(ld_late, N_LATE)
            dve.wait_ge(masks_ready, 1)

            def bias_v(t, u):
                dve.wait_ge(qkv_ps, t + (START + 1))
                dve.wait_ge(ctx_ps, t + START)
                V.tensor_tensor(v1[:, u, :], bank(6 + u, TILE), bv_b[:, :], ALU.add).then_inc(v_ready, 1)

            bias_v(0, 0)

            def band_attend(t, u, off, left):
                dve.wait_ge(score_ps, t + (START + 1))
                V.scalar_tensor_tensor(out=sc[:, u, :], in0=bank(2 + u, TILE + SPAN), scalar=1.0 / float(np.sqrt(D * SPAN)),
                                       in1=band[:, :], op0=ALU.mult, op1=ALU.mult).then_inc(score_ready, 1)
                if left >= 1:
                    bias_v(t + 1, 1 - u)

            turns(dve, 0, 1, band_attend)

            def norm_out(k, c):
                norm(k)
                for u in range(2):
                    dve.wait_ge(aff_ready, k + (START + u + 1))
                    xt = cols_at(XT, (c + u) * CH, CH)
                    V.scalar_tensor_tensor(out=xt, in0=h2[:, u, :], scalar=mod[:, 8:9], in1=xt,
                                           op0=ALU.mult, op1=ALU.add).then_inc(x3_done, 1)

            chunk_pairs(dve, 3, norm_out)
            chunk_pairs(dve, 4, lambda k, c: norm(k))

            for l in range(LAYERS):
                base = NT * l
                dve.wait_ge(rot_ready, START + l + 1)
                q4 = PS[:, 4 * CH:6 * CH].rearrange("p (j h d) -> p j h d", j=2, h=H)
                a4 = ra[:, :].rearrange("p (j h d) -> p j h d", j=2, h=H)
                b4 = rb[:, :].rearrange("p (j h d) -> p j h d", j=2, h=H)
                hd = DH // 2

                def rotate(t, nt):
                    dve.wait_ge(qk2_ps, t + (START + 1))
                    dve.wait_ge(qkT_ps, t + START)
                    tab = rotL[:, bass.ds(nt, 1), :].rearrange("p a (s j d) -> p (a s) j d", s=2, j=2)
                    for j in range(2):
                        V.tensor_tensor(a4[:, j], q4[:, j], tab[:, 0, j:j + 1, :].to_broadcast([P, H, DH]), ALU.mult)
                        V.tensor_tensor(b4[:, j, :, 0:hd], q4[:, j, :, hd:DH],
                                        tab[:, 1, j:j + 1, 0:hd].to_broadcast([P, H, hd]), ALU.mult)
                        ins = V.tensor_tensor(b4[:, j, :, hd:DH], q4[:, j, :, 0:hd],
                                              tab[:, 1, j:j + 1, hd:DH].to_broadcast([P, H, hd]), ALU.mult)
                    ins.then_inc(rot1_ready, 1)
                    dve.wait_ge(rot1_ready, t + (START + 1))
                    V.tensor_tensor(ra[:, :], ra[:, :], rb[:, :], ALU.add).then_inc(ra_ready, 1)

                def scale_q(t):
                    dve.wait_ge(sq2_ready, t + (START + 1))
                    V.tensor_reduce(ss[:, :], sq2[:, :].rearrange("p (g d) -> p g d", d=DH), AX_X, ALU.add).then_inc(sssum_ready, 1)
                    dve.wait_ge(sssum_ready, t + (START + 1))
                    V.tensor_scalar(ss[:, :], ss[:, :], 1e-24, None, ALU.max).then_inc(ss_ready, 1)
                    dve.wait_ge(r_ready, t + (START + 1))
                    v = ra[:, 0:INNER].rearrange("p (g d) -> p g d", d=DH)
                    V.tensor_tensor(v, v, rr[:, 0:H].unsqueeze(2).to_broadcast([P, H, DH]), ALU.mult).then_inc(rotq_ready, 1)

                def copy_qT(t):
                    dve.wait_ge(qkT_ps, t + (START + 1))
                    V.tensor_copy(qT[:, :, :], bank(4).rearrange("p (a b) -> p a b", a=H // 2)).then_inc(qT_ready, 1)

                def maxima(t):
                    dve.wait_ge(sim2_ps, t + (START + 1))
                    s = PS[:, 0:4 * CH].rearrange("p (b c) -> p b c", c=CH)[:, :, 0:2 * KEYS].rearrange("p b (e k) -> p b e k", k=KEYS)
                    V.tensor_reduce(mx[:, :].rearrange("p (b e) -> p b e", e=2), s, AX_X, ALU.max).then_inc(mx_ready, 1)
                    dve.wait_ge(mx_ready, t + (START + 1))
                    V.tensor_scalar(nmx[:, :], mx[:, :], -QK_SCALE, None, ALU.mult).then_inc(max_ready, 1)

                def copy_pTw(t):
                    dve.wait_ge(pT_ps, t + (START + 1))
                    V.tensor_copy(pTw[WIN:P, :, :], PS[WIN:P, 2 * CH:4 * CH].rearrange("p (a b) -> p a b", a=H)).then_inc(pTw_ready, 1)

                def normalise(t):
                    dve.wait_ge(p_ready, 2 * t + (START + 2))
                    V.reciprocal(rinv[:, :], rsum[:, :]).then_inc(rinv_ready, 1)
                    dve.wait_ge(rinv_ready, t + (START + 1))
                    dve.wait_ge(pv_ps, t + (START + 1))
                    V.tensor_tensor(o_s[:, :].rearrange("p (h d) -> p h d", d=DH), bank(6).rearrange("p (h d) -> p h d", d=DH),
                                    rinv[:, :].unsqueeze(2).to_broadcast([P, H, DH]), ALU.mult).then_inc(o_ready, 1)

                def residual(t, off):
                    dve.wait_ge(wo_ps, t + (START + 1))
                    V.tensor_tensor(cols_at(ZB, off + 1, TILE), bank(7, TILE), cols_at(ZA, off + 1, TILE), ALU.add).then_inc(zb_done, 1)

                rotate(base, 0)
                scale_q(base)
                copy_qT(base)
                maxima(base)
                rotate(base + 1, 1)
                scale_q(base + 1)

                def attend(t, u, off, left):
                    copy_pTw(t)
                    if left >= 1:
                        copy_qT(t + 1)
                    normalise(t)
                    if left >= 1:
                        maxima(t + 1)
                    if left >= 2:
                        rotate(t + 2, t + (2 - base))
                    residual(t, off)
                    if left >= 2:
                        scale_q(t + 2)

                turns(dve, base, 2, attend)

                def shift(k, c):
                    for u in range(2):
                        off = (c + u) * CH
                        dve.wait_ge(cen_ready, k + (START + u - 1))
                        V.tensor_copy(zs[0:DH, u, :], cols_at(ZB, off + 1, CH, slice(0, DH)))
                        V.tensor_copy(zs[DH:P, u, :], cols_at(ZB, off, CH, slice(DH, P))).then_inc(zs_ready, 1)
                    norm(k)

                chunk_pairs(dve, 5 + l, shift)

                with dve.Fori(NC * l, NC * (l + 1)) as c:
                    off = (c - NC * l) * CH
                    dve.wait_ge(down_ps, c + START)
                    for b, (o, m) in enumerate(HB):
                        dve.wait_ge(gate_ready, c * 3 + (START + b + 1))
                        V.scalar_tensor_tensor(out=hh[0:m, b, :], in0=PS[0:m, (3 + b % 2) * CH:(4 + b % 2) * CH],
                                               scalar=b1_s[0:m, l, b:b + 1], in1=gate[0:m, b, :],
                                               op0=ALU.add, op1=ALU.mult).then_inc(hh_ready, 1)
                    dve.wait_ge(down_ps, c + (START + 1))
                    V.scalar_tensor_tensor(out=cols_at(ZA, off + 1, CH), in0=bank(7), scalar=cols[:, CB2 + l:CB2 + l + 1],
                                           in1=cols_at(ZB, off + 1, CH), op0=ALU.add, op1=ALU.add).then_inc(za_done, 1)

            for c in range(NC):
                dve.wait_ge(finT_ps, START + c - 1)
                V.scalar_tensor_tensor(out=fin[:, c % 2, :], in0=ZA[:, c * CH + 1:(c + 1) * CH + 1], scalar=mod[:, 11:12],
                                       in1=XT[:, c * CH:(c + 1) * CH], op0=ALU.mult, op1=ALU.add).then_inc(fin_ready, 1)


def rotary_tables():
    f = np.float32
    half = np.arange(0, DH, 2, dtype=f)
    inv_freq = (f(1.0) / np.power(f(10000.0), half / f(DH))).astype(f)
    t = np.arange(T, dtype=f)
    freqs = t[:, None] * inv_freq[None, :]
    freqs = np.concatenate([freqs, freqs], -1)
    base = (half + f(0.4 * DH)) / f(1.4 * DH)
    power = (t - f(T // 2)) / f(WIN // 2)
    scale = np.power(base[None, :], power[:, None]).astype(f)
    scale = np.concatenate([scale, scale], -1)
    cos, sin = np.cos(freqs).astype(f), np.sin(freqs).astype(f)
    sin[:, :DH // 2] *= f(-1)
    return np.ascontiguousarray(np.concatenate([cos * scale, cos / scale, sin * scale, sin / scale], -1).astype(f))


_INS = ['L0_attn_x', 'L0_attn_delta', 'L0_attn_alpha', 'L0_attn_beta', 'L0_attn_gamma', 'L0_attn_omega',
        'L0_ffn_norm_w', 'L0_ffn_wq', 'L0_ffn_keys', 'L0_ffn_expert_down', 'L0_ffn_expert_up', 'L0_c', 'L0_wmod',
        'L1_attn_W_qkv', 'L1_attn_b_qkv', 'L1_attn_ln_w', 'L1_attn_ln_b', 'L1_ffn_wqkv', 'L1_ffn_q_scale',
        'L1_ffn_k_scale', 'L1_ffn_wo', 'L1_ffn_ln_g', 'L1_ffn_ln_b', 'L1_ffn_w1', 'L1_ffn_b1', 'L1_ffn_w2',
        'L1_ffn_b2', 'L1_c', 'L1_wmod']


def kernel(**inputs):
    import concourse.bacc as bacc
    from concourse.bass_utils import run_bass_kernel_spmd

    nc = bacc.Bacc("TRN2", target_bir_lowering=False, num_devices=1)
    arrays, args = {}, []
    given = [(name, np.ascontiguousarray(inputs[name])) for name in _INS] + [("rotary", rotary_tables())]
    for name, a in given:
        arrays[f"in_{name}"] = a
        args.append(nc.dram_tensor(f"in_{name}", a.shape, mybir.dt.from_np(a.dtype), kind="ExternalInput").ap())
    args.append(nc.dram_tensor("out_0", (1, T, D), F32, kind="ExternalOutput").ap())
    build(nc, *args)
    r = run_bass_kernel_spmd(nc, [arrays], core_ids=[0])
    return r.results[0]["out_0"]
```

```python
from contextlib import ExitStack

import numpy as np

import concourse.bass as bass
from concourse import mybir
from concourse.alu_op_type import AluOpType as ALU

ACT = mybir.ActivationFunctionType
AX_X = mybir.AxisListType.X
F32 = mybir.dt.float32
BF16 = mybir.dt.bfloat16

P = 128
T = 2048
D = 128
TILE = 128
NT = T // TILE
CH = 512
NC = T // CH
CT = CH // TILE
EPS = 1e-5
EH, NK, TOPK = 8, 32, 16
NE = NK * NK
EB = NE // P
CAND = sum(TOPK // (i + 1) for i in range(TOPK))
SPAN = 32
LAYERS, H, DH, WIN = 2, 8, 64, 64
INNER = H * DH
QK_SCALE = 8.0
KEYS = WIN + TILE
HID = D * 4 * 2 // 3
HB = [(0, P), (P, P), (2 * P, HID - 2 * P)]
MASKED = -1e37
LOWEST = -3.0e38


def build(nc, x, delta, alpha, beta, gamma, omega, norm_w, wq, keys, e_down, e_up, c0, wmod0,
          w_qkv, b_qkv, ln_w, ln_b, wqkv, q_scale, k_scale, wo, ln_g, ln_bb, w1, b1, w2, b2,
          c1, wmod1, rotary, out):
    with ExitStack() as ctx:
        def sb(name, shape, dt=F32):
            return ctx.enter_context(nc.sbuf_tensor(name, shape, dt))

        def sem(name):
            return ctx.enter_context(nc.semaphore(name))

        PS = ctx.enter_context(nc.psum_tensor("PS", [P, 8 * CH], F32))

        def bank(b, n=CH):
            return PS[:, b * CH:b * CH + n]

        arena = sb("arena", [P, 9 * NE])

        def carve(start, *shape):
            n = int(np.prod(shape))
            v = arena[:, start:start + n]
            return v.rearrange("p (a b) -> p a b", a=shape[0]) if len(shape) == 2 else v

        x_tok = sb("x_tok", [P, NT, D])
        XT = sb("XT", [P, T])
        HT = sb("HT", [P, T])
        ZA = sb("ZA", [P, 1 + T])
        ZB = sb("ZB", [P, 1 + T])
        ident = sb("ident", [P, P])
        ident_bf = sb("ident_bf", [P, P], BF16)
        center = sb("center", [P, P])
        mean = sb("mean", [P, P])
        cols = sb("cols", [P, 64])
        mod_raw = sb("mod_raw", [P, 12])
        mod = sb("mod", [P, 12])
        sgn = sb("sgn", [P, 12])
        silc = sb("silc", [P, 2])
        sig = sb("sig", [P, 4])
        ema = sb("ema", [P, 8])
        eps_c = sb("eps_c", [P, 1])

        wmod_s = sb("wmod_s", [P, 2, 6 * D])
        rotL = sb("rotL", [P, NT, 4 * DH])
        flat = rotL[:, :, :].rearrange("p a b -> p (a b)")
        wq_s = flat[:, 0:2 * EH * D]
        keys_s = carve(6 * NE, 4, D)
        wqT = flat[:, 2 * EH * D:4 * EH * D].rearrange("p (a b) -> p a b", a=2 * EH)
        keysT = carve(6 * NE + 4 * D, 4 * P)
        fold = sb("fold", [P, 2 * EH * NK])
        down_s = carve(7 * NE, EB, D)
        downT = sb("downT", [P, NE])
        up_s = sb("up_s", [P, EB, D])
        wqkv1_s = sb("wqkv1_s", [P, 3 * D])
        bv_b = sb("bv_b", [P, D])
        wqkv_s = sb("wqkv_s", [P, LAYERS, 3 * INNER])
        wo_s = sb("wo_s", [P, LAYERS, INNER // P, D])
        w1_s = sb("w1_s", [P, LAYERS, 2 * HID])
        w2_s = sb("w2_s", [P, LAYERS, 3, D])
        b1_s = sb("b1_s", [P, LAYERS, 6])
        rot_s = sb("rot_s", [P, NT, 4 * DH])
        rscale = sb("rscale", [P, LAYERS, 4 * DH])
        band = sb("band", [P, P + SPAN])
        mask_bf = sb("mask_bf", [P, KEYS + WIN], BF16)
        mask0_bf = sb("mask0_bf", [P, KEYS + WIN], BF16)

        sq_s = sb("sq_s", [P, 2, CH])
        rstd = sb("rstd", [P, 2, CH])
        nrm = sb("nrm", [P, 2, CH])
        h2 = sb("h2", [P, 2, CH])

        START = 8
        counted = []

        def count(names):
            made = [sem(n) for n in names.split()]
            counted.extend(made)
            return made

        ld_x = [sem(f"ld_x{c}") for c in range(NC)]
        ld_mod, ld_w0, ld_w1, ld_early, ld_late = (
            sem("ld_mod"), sem("ld_w0"), sem("ld_w1"), sem("ld_early"), sem("ld_late"))
        passed, masks_ready = sem("passed"), sem("masks_ready")
        const_ready, stored = sem("const_ready"), sem("stored")
        pool_step, dve_step = sem("pool_step"), sem("dve_step")

        CD, CA, CB, CG, CO, CN, CBQ, CBK, CLW, CLB, CC = 0, 2, 4, 6, 8, 9, 10, 11, 12, 13, 14
        CLG, CLBB, CB2 = 16, 18, 20
        small = [
            (cols[:, CD:CD + 2], delta.rearrange("p n a -> p (n a)")),
            (cols[:, CA:CA + 2], alpha.rearrange("p n a -> p (n a)")),
            (cols[:, CB:CB + 2], beta.rearrange("p n a -> p (n a)")),
            (cols[:, CG:CG + 2], gamma),
            (cols[:, CO:CO + 1], omega.rearrange("(p a) -> p a", a=1)),
            (cols[:, CN:CN + 1], norm_w.rearrange("(p a) -> p a", a=1)),
            (cols[:, CBQ:CBQ + 2], b_qkv[0:2 * D].rearrange("(n p) -> p n", p=P)),
            (cols[:, CLW:CLW + 1], ln_w.rearrange("(p a) -> p a", a=1)),
            (cols[:, CLB:CLB + 1], ln_b.rearrange("(p a) -> p a", a=1)),
            (cols[:, CC:CC + 1], c0.rearrange("a p -> p a")),
            (cols[:, CC + 1:CC + 2], c1.rearrange("a p -> p a")),
            (cols[:, CLG:CLG + 2], ln_g.rearrange("l p -> p l")),
            (cols[:, CLBB:CLBB + 2], ln_bb.rearrange("l p -> p l")),
            (cols[:, CB2:CB2 + 2], b2.rearrange("l p -> p l")),
            (bv_b[:, :], b_qkv[2 * D:3 * D].rearrange("(a d) -> a d", a=1).to_broadcast([P, D])),
        ]
        tail = HB[2][1]
        for l in range(LAYERS):
            for g in range(2):
                o = g * HID
                small.append((b1_s[:, l, 3 * g:3 * g + 2], b1[l, o:o + 2 * P].rearrange("(n p) -> p n", p=P)))
                small.append((b1_s[0:tail, l, 3 * g + 2:3 * g + 3],
                              b1[l, o + 2 * P:o + HID].rearrange("(p a) -> p a", a=1)))
            for j, s in enumerate((q_scale, k_scale)):
                row = s[l:l + 1, :]
                small.append((rscale[:, l, j * DH:(j + 1) * DH], row.to_broadcast([P, DH])))
                o = (2 + j) * DH
                small.append((rscale[:, l, o:o + DH // 2], row[:, DH // 2:].to_broadcast([P, DH // 2])))
                small.append((rscale[:, l, o + DH // 2:o + DH], row[:, 0:DH // 2].to_broadcast([P, DH // 2])))
        EARLY = 11
        N_EARLY, N_LATE = 16 * EARLY, 16 * (len(small) - EARLY)

        mod_ready, mod_done, sig_ready, silc_ready = count("mod_ready mod_done sig_ready silc_ready")
        xT_ps, xT_done, tr_ps, tr_done = count("xT_ps xT_done tr_ps tr_done")
        fold_ps, fold_done, rot_ready = count("fold_ps fold_done rot_ready")
        cen_ready, sq_ready, var_ready, ln_ready = count("cen_ready sq_ready var_ready ln_ready")
        rstd_ready, nrm_ready, aff_ready = count("rstd_ready nrm_ready aff_ready")
        y_ready, silu_ready, x1_done = count("y_ready silu_ready x1_done")
        h2sq_ready, ms_ready, rmsln_ready, rms_ready, xn_done = count("h2sq_ready ms_ready rmsln_ready rms_ready xn_done")
        xn_ready, sim_ps, sim_ready, hid_ps, gelu_ready = count("xn_ready sim_ps sim_ready hid_ps gelu_ready")
        weight_ready, hidw_ready, eout_ps, x2_done = count("weight_ready hidw_ready eout_ps x2_done")
        sum_ready, kept_ready, kept_used, thr_ready = count("sum_ready kept_ready kept_used thr_ready")
        hc_ready, qk1_ps, v1_ps, qk_ready, v_ready = count("hc_ready qk1_ps v1_ps qk_ready v_ready")
        score_ps, score_ready, ctx_ps, ctx_done, x3_done = count("score_ps score_ready ctx_ps ctx_done x3_done")
        hs_ready, hv_ready, q2_ps, qk2_ps, v2_ps, v2_ready, sq2_ready, ss_ready = count("hs_ready hv_ready q2_ps qk2_ps v2_ps v2_ready sq2_ready ss_ready")
        lnss_ready, r_ready, rot0_ready, sqk_ready, rot1_ready, rotq_ready, rotk_ready = count("lnss_ready r_ready rot0_ready sqk_ready rot1_ready rotq_ready rotk_ready")
        ra_ready, ka_ready, half_ready, sssum_ready, mx_ready, rinv_ready = count("ra_ready ka_ready half_ready sssum_ready mx_ready rinv_ready")
        qT_ps, qkT_ps, qT_ready, kT_ready, sim2_ps, max_ready, p_ready = count("qT_ps qkT_ps qT_ready kT_ready sim2_ps max_ready p_ready")
        pT_ps, pT_ready, pTo_ready, pTw_ready, pv_ps, pn_ready = count("pT_ps pT_ready pTo_ready pTw_ready pv_ps pn_ready")
        kw_ready, v0_ready, vw_ready, oT_ready, wo_ps, zb_done = count("kw_ready v0_ready vw_ready oT_ready wo_ps zb_done")
        zs_ready, up_ps, gate_ready, hh_ready, down_ps, za_done = count("zs_ready up_ps gate_ready hh_ready down_ps za_done")
        fin_ready, finT_ps, fin_out = count("fin_ready finT_ps fin_out")

        scan1, scan2 = carve(0, CH), carve(CH, CH)
        ysum, silu_s = carve(2 * CH, 2, CH), carve(4 * CH, 2, CH)

        rms_s = carve(8 * NE, 2, CH)

        xn = sb("xn", [P, 2, TILE])
        sims = sb("sims", [P, 2, 2 * EH * NK])
        rest = sb("rest", [P, 2 * EH, NK])
        srt = sb("srt", [P, 2 * EH, TOPK])
        cand = sb("cand", [P, EH, CAND])
        cand2 = sb("cand2", [P, EH, CAND])
        top = sb("top", [P, EH, TOPK])
        thr = sb("thr", [P, EH])
        def places(*parts):
            return [v[:, i * NE:(i + 1) * NE] for v, m in parts for i in range(m)]

        tok = x_tok[:, :, :].rearrange("p a b -> p (a b)")
        sums = places((arena[:, 0:4 * NE], 4), (ZA[:, 1:1 + T], T // NE), (ZB[:, 1:1 + T], T // NE))
        kept = places((arena[:, 4 * NE:6 * NE], 2), (flat, 4), (tok, 2))
        gelu_s = carve(6 * NE, 2, NE)
        hidw = carve(8 * NE, NE)

        hc = sb("hc", [P, 2, TILE])
        hv = sb("hv", [P, TILE])
        q1 = sb("q1", [P, 2, TILE])
        k1 = sb("k1", [P, 2, TILE])
        v1 = sb("v1", [P, 2, D])
        sc = sb("sc", [P, 2, TILE + SPAN])

        sq2 = carve(0 * NE, 2 * INNER)
        ss = sb("ss", [P, 2 * H])
        lnss = sb("lnss", [P, 2 * H])
        rr = sb("rr", [P, 2 * H])
        ra = carve(1 * NE, 2 * INNER)
        rb = carve(2 * NE, 2 * INNER)
        qT = sb("qT", [P, H // 2, TILE])
        kT = sb("kT", [P, 2, H // 2, WIN + KEYS])
        v2 = carve(6 * NE + 3 * H * WIN, 2, INNER)
        vw = sb("vw", [WIN, 2, H // 2, DH])
        mx = sb("mx", [P, H])
        nmx = sb("nmx", [P, H])
        pr = carve(6 * NE, H // 2, 2 * KEYS)
        rsum = sb("rsum", [P, H])
        rinv = sb("rinv", [P, H])
        pT = carve(3 * NE, H, TILE)
        pTw = carve(4 * NE, H // 2, TILE)
        oT = carve(5 * NE + INNER, INNER // P, TILE)

        zs = carve(4 * NE + CH, 2, CH)
        gate = carve(0, 3, CH)
        hh = carve(3 * CH, 3, CH)
        fin = carve(4 * NE, 2, CH)

        def turns(eng, base, ahead, step):
            looped = (NT - ahead) // 2
            with eng.Fori(0, looped) as p:
                for u in range(2):
                    step(2 * p + (base + u), u, (2 * p + u) * TILE, NT)
            for t in range(2 * looped, NT):
                step(base + t, t % 2, t * TILE, NT - 1 - t)


        def plain(eng):
            eng.sem_inc(passed, 1)

        def cols_at(buf, off, n, rows=slice(0, P)):
            return buf[rows, bass.ds(off, n)]

        def place(h):
            return (h % 2) * (H // 2) + h // 2

        def scores_of(h):
            o = (place(h) // 2) * CH + (place(h) % 2) * KEYS
            return PS[:, o:o + KEYS]

        def keys_of(row, odd):
            return row[:, 0:KEYS] if odd else row[:, WIN:WIN + KEYS]

        block = ctx.enter_context(nc.Block())

        @block.sync
        def _(sp):
            for s in counted:
                sp.sem_inc(s, START)
            x_v = x[0].rearrange("(n p) d -> p n d", p=P)
            for c in range(NC):
                sp.dma_start(x_tok[:, c * CT:(c + 1) * CT, :], x_v[:, c * CT:(c + 1) * CT, :]).then_inc(ld_x[c], 16)
            sp.dma_start(wmod_s[:, 0, :], wmod0).then_inc(ld_mod, 16)
            sp.dma_start(wmod_s[:, 1, :], wmod1).then_inc(ld_mod, 16)
            sp.dma_start(wq_s[:, :], wq).then_inc(ld_w0, 16)
            sp.dma_start(keys_s[:, :, :],
                         keys.rearrange("h k p d -> (h k p) d").rearrange("(n r) d -> r n d", r=P)).then_inc(ld_w0, 16)
            sp.dma_start(down_s[:, :, :], e_down.rearrange("(n r) d -> r n d", r=P)).then_inc(ld_w0, 16)
            sp.dma_start(up_s[:, :, :], e_up.rearrange("(n r) d -> r n d", r=P)).then_inc(ld_w0, 16)
            sp.dma_start(wqkv1_s[:, :], w_qkv).then_inc(ld_w1, 16)
            sp.dma_start(rot_s[:, :, :], rotary.rearrange("(n p) c -> p n c", p=P)).then_inc(ld_w1, 16)
            sp.dma_start(wqkv_s[:, :, :], wqkv.rearrange("l p n -> p l n")).then_inc(ld_w1, 16)
            for l in range(LAYERS):
                sp.dma_start(wo_s[:, l, :, :], wo[l].rearrange("(n p) d -> p n d", p=P)).then_inc(ld_w1, 16)
                sp.dma_start(w2_s[:, l, 0:2, :], w2[l, 0:2 * P, :].rearrange("(n p) d -> p n d", p=P)).then_inc(ld_w1, 16)
                sp.dma_start(w2_s[0:tail, l, 2, :], w2[l, 2 * P:HID, :]).then_inc(ld_w1, 16)
            sp.dma_start(w1_s[:, :, :], w1.rearrange("l p n -> p l n")).then_inc(ld_w1, 16)
            for dst, src in small[EARLY:]:
                sp.dma_start(dst, src, allow_slow_non_contiguous=True).then_inc(ld_late, 16)
            o_v = out[0].rearrange("(n p) d -> p n d", p=P)
            for c in range(NC):
                sp.wait_ge(fin_out, START + c + 1)
                sp.dma_start(o_v[:, c * CT:(c + 1) * CT, :], x_tok[:, c * CT:(c + 1) * CT, :]).then_inc(stored, 16)
            sp.wait_ge(stored, 16 * NC)
        N_W0 = 16 * 4
        N_W1 = 16 * (4 + 3 * LAYERS)

        @block.gpsimd
        def _(pool):
            n = [0]

            def step(ins):
                n[0] += 1
                ins.then_inc(pool_step, 1)
                pool.wait_ge(pool_step, n[0])

            nc.gpsimd.memset(ident[:, :], 0.0)
            nc.gpsimd.memset(center[:, :], -1.0 / D)
            nc.gpsimd.memset(mean[:, :], 1.0 / D)
            nc.gpsimd.memset(eps_c[:, :], EPS)
            step(nc.gpsimd.memset(ema[:, :], 0.0))
            step(nc.gpsimd.affine_select(out=ident[:, :], in_=ident[:, :], compare_op=ALU.not_equal, fill=1.0,
                                         base=0, pattern=[[-1, P]], channel_multiplier=1))
            nc.gpsimd.tensor_tensor(center[:, :], center[:, :], ident[:, :], ALU.add).then_inc(const_ready, 1)
            nc.gpsimd.memset(band[:, :], 1.0)
            nc.gpsimd.memset(mask_bf[:, :], 0.0)
            nc.gpsimd.memset(k1[:, :, :], 0.0)
            nc.gpsimd.memset(v1[:, :, :], 0.0)
            nc.gpsimd.memset(kT[:, 0, :, 0:WIN], 0.0)
            nc.gpsimd.memset(kT[:, 0, :, KEYS:KEYS + WIN], 0.0)
            nc.gpsimd.memset(vw[:, 0, :, :], 0.0)
            nc.gpsimd.memset(ZA[:, 0:1], 0.0)
            step(nc.gpsimd.memset(ZB[:, 0:1], 0.0))
            own = band[:, 0:P]
            step(nc.gpsimd.affine_select(out=own, in_=own, compare_op=ALU.is_ge, fill=0.0,
                                         base=0, pattern=[[1, P]], channel_multiplier=-1))
            step(nc.gpsimd.affine_select(out=own, in_=own, compare_op=ALU.is_ge, fill=0.0,
                                         base=SPAN - 1, pattern=[[-1, P]], channel_multiplier=1))
            prev = band[:, P:P + SPAN]
            step(nc.gpsimd.affine_select(out=prev, in_=prev, compare_op=ALU.is_ge, fill=0.0,
                                         base=SPAN - 1 - P, pattern=[[-1, SPAN]], channel_multiplier=1))
            m, m0 = mask_bf[:, 0:KEYS], mask0_bf[:, 0:KEYS]
            step(nc.gpsimd.affine_select(out=m, in_=m, compare_op=ALU.is_ge, fill=MASKED,
                                         base=WIN, pattern=[[-1, KEYS]], channel_multiplier=1))
            step(nc.gpsimd.affine_select(out=m, in_=m, compare_op=ALU.is_ge, fill=MASKED,
                                         base=0, pattern=[[1, KEYS]], channel_multiplier=-1))
            step(nc.gpsimd.affine_select(out=m0, in_=m, compare_op=ALU.is_ge, fill=MASKED,
                                         base=-WIN, pattern=[[1, KEYS]], channel_multiplier=0))
            nc.gpsimd.tensor_copy(mask_bf[:, KEYS:KEYS + WIN], mask_bf[:, 0:WIN])
            nc.gpsimd.tensor_copy(mask0_bf[:, KEYS:KEYS + WIN], mask0_bf[:, 0:WIN])
            nc.gpsimd.tensor_copy(ident_bf[:, :], ident[:, :]).then_inc(masks_ready, 1)

            def rotary_table(l):
                ins = nc.gpsimd.tensor_tensor(rotL[:, :, :], rot_s[:, :, :],
                                              rscale[:, l:l + 1, :].to_broadcast([P, NT, 4 * DH]), ALU.mult)
                ins.then_inc(rot_ready, 1)

            def pair_sums(t, u):
                pool.wait_ge(sim_ready, t + (START + 1))
                for h in range(EH):
                    pool.wait_ge(kept_ready, t * EH + (START + h + 1 - EH))
                    a = sims[:, u, h * NK:(h + 1) * NK].unsqueeze(2).to_broadcast([P, NK, NK])
                    b = sims[:, u, (EH + h) * NK:(EH + h + 1) * NK].unsqueeze(1).to_broadcast([P, NK, NK])
                    nc.gpsimd.tensor_tensor(sums[h].rearrange("p (a b) -> p a b", a=NK), a, b, ALU.add).then_inc(sum_ready, 1)

            def hidden_weights(t, u):
                pool.wait_ge(weight_ready, t + (START + 1))
                pool.wait_ge(gelu_ready, t + (START + 1))
                nc.gpsimd.tensor_tensor(hidw[:, :], hidw[:, :], gelu_s[:, u, :], ALU.mult).then_inc(hidw_ready, 1)

            pair_sums(0, 0)

            def peer(t, u, off, left):
                if left >= 1:
                    pair_sums(t + 1, 1 - u)
                hidden_weights(t, u)

            turns(pool, 0, 2, peer)
            pool.wait_ge(ld_late, N_LATE)
            pool.wait_ge(ld_w1, N_W1)
            pool.wait_ge(kept_used, START + EH * NT)
            pool.wait_ge(x2_done, START + NT)
            nc.gpsimd.memset(v2[WIN:P, 1, :], 0.0).then_inc(v0_ready, 1)
            pool.wait_ge(v0_ready, START + 1)

            for l in range(LAYERS):
                if l:
                    pool.wait_ge(rot1_ready, START + NT * l)
                rotary_table(l)

                def add_k(t):
                    pool.wait_ge(rot1_ready, t + (START + 1))
                    v = ra[:, INNER:2 * INNER]
                    nc.gpsimd.tensor_tensor(v, v, rb[:, INNER:2 * INNER], ALU.add).then_inc(ka_ready, 1)

                def halve_squares(t):
                    pool.wait_ge(sq2_ready, t + (START + 1))
                    v = sq2[:, :].rearrange("p (g d) -> p g d", d=DH)
                    for i, n in enumerate((DH // 2, DH // 4)):
                        if i:
                            pool.wait_ge(half_ready, 2 * t + (START + 1))
                        nc.gpsimd.tensor_tensor(v[:, :, 0:n], v[:, :, 0:n], v[:, :, n:2 * n], ALU.add).then_inc(half_ready, 1)

                def scale_k(t):
                    pool.wait_ge(ka_ready, t + (START + 1))
                    pool.wait_ge(r_ready, t + (START + 1))
                    v = ra[:, INNER:2 * INNER].rearrange("p (g d) -> p g d", d=DH)
                    nc.gpsimd.tensor_tensor(v, v, rr[:, H:2 * H].unsqueeze(2).to_broadcast([P, H, DH]),
                                            ALU.mult).then_inc(rotk_ready, 1)

                def keep_window(t, u):
                    pool.wait_ge(rotk_ready, t + (START + 1))
                    pool.wait_ge(kT_ready, t + (START + 1))
                    plain(pool)
                    nc.gpsimd.tensor_copy(kT[0:DH, 1 - u, :, KEYS:KEYS + WIN], kT[0:DH, u, :, TILE:KEYS])
                    nc.gpsimd.tensor_copy(kT[DH:P, 1 - u, :, 0:WIN], kT[DH:P, u, :, TILE:KEYS]).then_inc(kw_ready, 1)
                    pool.wait_ge(kw_ready, t + (START + 1))

                def keep_values(t, u, last=False):
                    if not last:
                        pool.wait_ge(rotk_ready, t + (START + 2))
                    pool.wait_ge(v2_ready, t + (START + 1))
                    plain(pool)
                    even = v2[WIN:P, u, :].rearrange("p (g e d) -> p g e d", e=2, d=DH)[:, :, 0, :]
                    nc.gpsimd.tensor_copy(vw[:, 1 - u, :, :], even).then_inc(vw_ready, 1)
                    pool.wait_ge(vw_ready, t + (START + 1))

                base = NT * l
                halve_squares(base)
                add_k(base)
                scale_k(base)
                keep_window(base, 0)
                halve_squares(base + 1)
                add_k(base + 1)
                scale_k(base + 1)
                keep_values(base, 0)

                def attend(t, u, off, left):
                    if left >= 1:
                        keep_window(t + 1, 1 - u)
                    if left >= 2:
                        halve_squares(t + 2)
                        add_k(t + 2)
                        scale_k(t + 2)
                    if left >= 1:
                        keep_values(t + 1, 1 - u, left == 1)

                turns(pool, base, 2, attend)

        @block.scalar
        def _(act):
            A = nc.scalar
            for dst, src in small[0:EARLY]:
                act.dma_start(dst, src, allow_slow_non_contiguous=True).then_inc(ld_early, 16)
            for c in range(NC):
                act.wait_ge(xT_ps, START + c + 1)
                A.copy(XT[:, c * CH:(c + 1) * CH], bank(c)).then_inc(xT_done, 1)
            act.wait_ge(ld_early, N_EARLY)
            A.activation(silc[:, :], cols[:, CC:CC + 2], ACT.Silu).then_inc(silc_ready, 1)
            A.activation(sig[:, :], cols[:, CD:CD + 4], ACT.Sigmoid).then_inc(sig_ready, 1)
            act.wait_ge(const_ready, 1)

            def exp_and_ln():
                A.preload_act_table_set("natural_log_exp_and_others")

            def squares_of(k):
                for c in k:
                    act.wait_ge(cen_ready, START + c + 1)
                    A.activation(sq_s[:, c % 2, :], bank(c % NC), ACT.Square).then_inc(sq_ready, 1)

            def inv_stds(k):
                for c in k:
                    act.wait_ge(var_ready, START + c + 1)
                    act.wait_ge(nrm_ready, START + c - 1)
                    A.activation(rstd[:, c % 2, :], bank(4 + c % 2), ACT.Ln, bias=eps_c[:, 0:1]).then_inc(ln_ready, 1)
                for c in k:
                    act.wait_ge(ln_ready, START + c + 1)
                    A.activation(rstd[:, c % 2, :], rstd[:, c % 2, :], ACT.Exp, scale=-0.5).then_inc(rstd_ready, 1)

            def scaled(k, dst, scale, bias):
                if k[0] == 0:
                    act.wait_ge(mod_done, START + 1)
                for c in k:
                    act.wait_ge(nrm_ready, START + c + 1)
                    A.activation(dst(c % NC), nrm[:, c % 2, :], ACT.Identity, scale=scale, bias=bias).then_inc(aff_ready, 1)

            def norm(n, dst, scale, bias, free=None, between=None, begun=False):
                first, second = range(n * NC, n * NC + 2), range(n * NC + 2, n * NC + 4)
                if not begun:
                    squares_of(first)
                inv_stds(first)
                squares_of(second)
                scaled(first, dst, scale, bias)
                inv_stds(second)
                if between is not None:
                    between()
                if free is not None:
                    act.wait_ge(*free)
                scaled(second, dst, scale, bias)

            def chunk_of(buf, c, shift=0):
                return buf[:, c * CH + shift:(c + 1) * CH + shift]

            exp_and_ln()
            norm(0, lambda c: chunk_of(HT, c), mod[:, 1:2], mod[:, 0:1])
            def silu(c):
                act.wait_ge(y_ready, START + c + 1)
                act.wait_ge(x1_done, START + c - 1)
                A.activation(silu_s[:, c % 2, :], ysum[:, c % 2, :], ACT.Silu).then_inc(silu_ready, 1)

            def copy_turned(g):
                act.wait_ge(tr_ps, START + g + 1)
                dst = (wqT[:, 4 * g:4 * g + 4, :] if g < 4 else
                       (keysT[:, :] if g == 4 else downT[:, (g - 5) * CH:(g - 4) * CH]).rearrange("p (a b) -> p a b", a=4))
                A.copy(dst, bank(6 + g % 2).rearrange("p (a b) -> p a b", a=4)).then_inc(tr_done, 1)

            for c in range(NC):
                for g in range(2 * c, min(2 * c + 2, 7)):
                    copy_turned(g)
                silu(c)
            act.wait_ge(fold_ps, START + 1)
            A.copy(fold[:, :], bank(4)).then_inc(fold_done, 1)

            def h2_squares(pair):
                for c in pair:
                    act.wait_ge(aff_ready, START + NC + c + 1)
                    act.wait_ge(var_ready, START + 2 * NC)
                    act.wait_ge(ms_ready, START + c - 1)
                    A.activation(sq_s[:, c % 2, :], h2[:, c % 2, :], ACT.Square).then_inc(h2sq_ready, 1)

            def inv_rms(pair):
                for c in pair:
                    act.wait_ge(ms_ready, START + c + 1)
                    act.wait_ge(xn_done, START + c - 1)
                    A.activation(rms_s[:, c % 2, :], bank(6 + c % 2), ACT.Ln, bias=eps_c[:, 0:1]).then_inc(rmsln_ready, 1)
                for c in pair:
                    act.wait_ge(rmsln_ready, START + c + 1)
                    A.activation(rms_s[:, c % 2, :], rms_s[:, c % 2, :], ACT.Exp, scale=-0.5).then_inc(rms_ready, 1)

            exp_and_ln()
            squares_of(range(NC, NC + 2))
            inv_stds(range(NC, NC + 2))
            squares_of(range(NC + 2, NC + 4))
            scaled(range(NC, NC + 2), lambda c: h2[:, c % 2, :], mod[:, 4:5], mod[:, 3:4])
            inv_stds(range(NC + 2, NC + 4))
            h2_squares(range(2))
            inv_rms(range(2))
            act.wait_ge(xn_done, START + 2)
            A.copy(xn[:, 0, :], HT[:, 0:TILE]).then_inc(xn_ready, 1)
            scaled(range(NC + 2, NC + 4), lambda c: h2[:, c % 2, :], mod[:, 4:5], mod[:, 3:4])
            act.wait_ge(sim_ps, START + 1)
            A.copy(sims[:, 0, :], bank(0)).then_inc(sim_ready, 1)
            h2_squares(range(2, 4))
            inv_rms(range(2, 4))
            act.wait_ge(xn_done, START + NC)

            def copy_xn(t, u, off):
                act.wait_ge(hid_ps, t + (START - 1))
                plain(act)
                A.copy(xn[:, u, :], cols_at(HT, off, TILE)).then_inc(xn_ready, 1)

            def copy_sim(t, u):
                act.wait_ge(sim_ps, t + (START + 1))
                act.wait_ge(kept_ready, t * EH + (START - EH))
                A.copy(sims[:, u, :], bank(u)).then_inc(sim_ready, 1)

            def gelu(t, u):
                act.wait_ge(hid_ps, t + (START + 1))
                act.wait_ge(hidw_ready, t + (START - 1))
                A.activation(gelu_s[:, u, :], PS[:, 2 * CH:4 * CH], ACT.Gelu).then_inc(gelu_ready, 1)

            A.copy(xn[:, 1, :], HT[:, TILE:2 * TILE]).then_inc(xn_ready, 1)
            gelu(0, 0)

            def copy_weights(t):
                act.wait_ge(kept_used, t * EH + (START + EH))
                act.wait_ge(eout_ps, t + START)
                A.copy(hidw[:, :], PS[:, 4 * CH:6 * CH]).then_inc(weight_ready, 1)

            def peer(t, u, off, left):
                if left >= 1:
                    copy_sim(t + 1, 1 - u)
                if left >= 2:
                    copy_xn(t + 2, u, off + 2 * TILE)
                copy_weights(t)
                if left >= 1:
                    gelu(t + 1, 1 - u)

            turns(act, 0, 2, peer)

            exp_and_ln()

            def first_columns():
                act.wait_ge(aff_ready, START + 2 * NC + 1)
                for u in range(2):
                    A.copy(hc[:, u, :], HT[:, u * TILE:(u + 1) * TILE]).then_inc(hc_ready, 1)

            norm(2, lambda c: chunk_of(HT, c), mod[:, 7:8], mod[:, 6:7], between=first_columns)

            def copy_hc(t, u, off):
                act.wait_ge(v1_ps, t + (START - 1))
                plain(act)
                A.copy(hc[:, u, :], cols_at(HT, off, TILE)).then_inc(hc_ready, 1)

            def bias_qk(t, u):
                act.wait_ge(qk1_ps, t + (START + 1))
                act.wait_ge(score_ps, t + START)
                A.activation(q1[:, u, :], bank(u)[:, 0:TILE], ACT.Identity, bias=cols[:, CBQ:CBQ + 1])
                A.activation(k1[:, u, :], bank(u)[:, TILE:2 * TILE], ACT.Identity,
                             bias=cols[:, CBK:CBK + 1]).then_inc(qk_ready, 1)

            bias_qk(0, 0)
            bias_qk(1, 1)
            act.wait_ge(aff_ready, START + 3 * NC)
            copy_hc(2, 0, 2 * TILE)

            def band_attend(t, u, off, left):
                if left >= 2:
                    bias_qk(t + 2, u)
                if left >= 3:
                    copy_hc(t + 3, 1 - u, off + 3 * TILE)
                act.wait_ge(ctx_ps, t + (START + 1))
                plain(act)
                A.copy(cols_at(HT, off, TILE), bank(4 + u, TILE)).then_inc(ctx_done, 1)

            turns(act, 0, 3, band_attend)

            def shift_into(dst, off, ready):
                plain(act)
                A.copy(dst[0:DH, :], cols_at(ZA, off + 1, TILE, slice(0, DH)))
                A.copy(dst[DH:P, :], cols_at(ZA, off, TILE, slice(DH, P))).then_inc(ready, 1)

            def shifted(t, u, off):
                act.wait_ge(qk2_ps, t + (START - 1))
                shift_into(hc[:, u, :], off, hs_ready)

            def shifted_v(t, off):
                act.wait_ge(v2_ps, t + START)
                shift_into(hv[:, :], off, hv_ready)

            def first_two(l, chunks):
                act.wait_ge(*chunks)
                shifted(NT * l, 0, 0)
                shifted(NT * l + 1, 1, TILE)
                shifted_v(NT * l, 0)

            norm(3, lambda c: h2[:, c % 2, :], cols[:, CLW:CLW + 1], cols[:, CLB:CLB + 1], (x3_done, START + 2),
                 between=lambda: squares_of(range(4 * NC, 4 * NC + 2)))
            norm(4, lambda c: chunk_of(ZA, c, 1), mod[:, 10:11], mod[:, 9:10],
                 between=lambda: first_two(0, (aff_ready, START + 4 * NC + 1)), begun=True)

            for l in range(LAYERS):
                base = NT * l
                act.wait_ge(*((za_done, START + NC * l) if l else (aff_ready, START + 5 * NC)))

                def squares(t):
                    act.wait_ge(qk2_ps, t + (START + 1))
                    act.wait_ge(sssum_ready, t + START)
                    A.activation(sq2[:, INNER:2 * INNER], bank(5), ACT.Square).then_inc(sqk_ready, 1)
                    act.wait_ge(rot0_ready, t + (START + 1))
                    A.activation(sq2[:, 0:INNER], bank(4), ACT.Square).then_inc(sq2_ready, 1)

                def copy_v(t, u):
                    act.wait_ge(v2_ps, t + (START + 1))
                    act.wait_ge(vw_ready, t + (START - 1))
                    A.copy(v2[:, u, :], bank(7)).then_inc(v2_ready, 1)

                def inv_norms(t):
                    act.wait_ge(ss_ready, t + (START + 1))
                    A.activation(lnss[:, :], ss[:, :], ACT.Ln).then_inc(lnss_ready, 1)
                    act.wait_ge(lnss_ready, t + (START + 1))
                    act.wait_ge(rotq_ready, t + START)
                    act.wait_ge(rotk_ready, t + START)
                    A.activation(rr[:, :], lnss[:, :], ACT.Exp, scale=-0.5).then_inc(r_ready, 1)

                def copy_kT(t, u):
                    act.wait_ge(qkT_ps, t + (START + 1))
                    A.copy(kT[:, u, :, WIN:KEYS], bank(7).rearrange("p (a b) -> p a b", a=H // 2)).then_inc(kT_ready, 1)

                def exps(t, j):
                    act.wait_ge(max_ready, 2 * t + (START + j + 1))
                    for h in range(j, H, 2):
                        ins = A.activation(pr[:, h // 2, j * KEYS:(j + 1) * KEYS], scores_of(h), ACT.Exp, scale=QK_SCALE,
                                           bias=nmx[:, place(h):place(h) + 1], accum_out=rsum[:, place(h):place(h) + 1])
                    ins.then_inc(p_ready, 1)

                def copy_pT(t):
                    act.wait_ge(pT_ps, 3 * t + (START + 1))
                    A.copy(pT[:, 0:H // 2, :], bank(0).rearrange("p (a b) -> p a b", b=TILE)).then_inc(pT_ready, 1)
                    act.wait_ge(pT_ps, 3 * t + (START + 3))
                    A.copy(pTw[:, :, :], bank(2).rearrange("p (a b) -> p a b", b=TILE)).then_inc(pTw_ready, 1)

                def copy_oT(t):
                    act.wait_ge(pv_ps, t + (START + 1))
                    A.copy(oT[:, :, :], bank(6).rearrange("p (a b) -> p a b", a=INNER // P)).then_inc(oT_ready, 1)

                squares(base)
                shifted(base + 2, 0, 2 * TILE)
                inv_norms(base)
                copy_kT(base, 0)
                squares(base + 1)
                shifted(base + 3, 1, 3 * TILE)
                exps(base, 0)
                exps(base, 1)
                copy_v(base, 0)
                inv_norms(base + 1)

                def attend(t, u, off, left):
                    copy_pT(t)
                    if left >= 1:
                        copy_kT(t + 1, 1 - u)
                    if left >= 2:
                        squares(t + 2)
                    if left >= 1:
                        shifted_v(t + 1, off + TILE)
                        exps(t + 1, 0)
                        exps(t + 1, 1)
                    copy_oT(t)
                    if left >= 1:
                        copy_v(t + 1, 1 - u)
                    if left >= 2:
                        inv_norms(t + 2)
                    if left >= 4:
                        shifted(t + 4, u, off + 4 * TILE)

                turns(act, base, 4, attend)

                norm(5 + l, lambda c: chunk_of(HT, c), cols[:, CLG + l:CLG + l + 1], cols[:, CLBB + l:CLBB + l + 1])

                def rows_out(c):
                    act.wait_ge(finT_ps, START + c + 1)
                    A.copy(x_tok[:, c * CT:(c + 1) * CT, :],
                           bank(2 + c % 2).rearrange("p (a b) -> p a b", a=CT)).then_inc(fin_out, 1)

                for i in range(3 * NC):
                    k, b, m = 3 * NC * l + i, i % 3, HB[i % 3][1]
                    if l == LAYERS - 1 and b == 2 and i > 6:
                        rows_out(i // 3 - 2)
                    if l < LAYERS - 1 and i == 3 * NC - 2:
                        first_two(l + 1, (za_done, START + NC * l + 1))
                    act.wait_ge(up_ps, START + k + 1)
                    act.wait_ge(hh_ready, START + k - 2)
                    A.activation(gate[0:m, b, :], PS[0:m, (6 + i % 2) * CH:(7 + i % 2) * CH], ACT.Gelu,
                                 bias=b1_s[0:m, l, 3 + b:4 + b]).then_inc(gate_ready, 1)
                if l < LAYERS - 1:
                    exp_and_ln()
                else:
                    rows_out(NC - 2)
                    rows_out(NC - 1)


        @block.tensor
        def _(pe):
            def mm(o, w, m, start=True, stop=True):
                return nc.tensor.matmul(o, w, m, start=start, stop=stop)

            def add(o, w, m, start=False):
                return nc.tensor.matmul(o, w, m, start=start, stop=True, skip_group_check=True)

            pe.wait_ge(const_ready, 1)
            for c in range(NC):
                pe.wait_ge(ld_x[c], 16)
                for j in range(CT):
                    ins = nc.tensor.transpose(bank(c)[:, j * TILE:(j + 1) * TILE], x_tok[:, c * CT + j, :], ident[:, :])
                ins.then_inc(xT_ps, 1)
            def deviations(n, two, src, ready=None):
                for c in two:
                    pe.wait_ge(nrm_ready, START + (n - 1) * NC + c + 1)
                    if ready is not None:
                        pe.wait_ge(ready[0], ready[1] + START + c + 1)
                    mm(bank(c), center[:, :], src(c)).then_inc(cen_ready, 1)

            def norm(n, src, ready=None, between=None, begun=False):
                if not begun:
                    deviations(n, range(0, 2), src, ready)
                if between is not None:
                    between()
                mean_squares(n, range(0, 2))
                deviations(n, range(2, 4), src, ready)
                mean_squares(n, range(2, 4))

            def mean_squares(n, two):
                for c in two:
                    pe.wait_ge(sq_ready, START + n * NC + c + 1)
                    pe.wait_ge(ln_ready, START + n * NC + c - 1)
                    mm(bank(4 + c % 2), mean[:, :], sq_s[:, c % 2, :]).then_inc(var_ready, 1)

            def chunk_of(buf, c):
                return buf[:, c * CH:(c + 1) * CH]

            def modulation():
                pe.wait_ge(ld_mod, 32)
                pe.wait_ge(silc_ready, START + 1)
                for l in range(2):
                    for j in range(6):
                        ins = mm(bank(7)[:, 6 * l + j:6 * l + j + 1], wmod_s[:, l, j * D:(j + 1) * D], silc[:, l:l + 1])
                ins.then_inc(mod_ready, 1)

            norm(0, lambda c: chunk_of(XT, c), (xT_done, 0), modulation)
            pe.wait_ge(ld_w0, N_W0)
            pe.wait_ge(mod_done, START + 1)
            for g in range(7):
                if g >= 2:
                    pe.wait_ge(tr_done, START + g - 1)
                for j in range(4):
                    src = (wq_s[:, (4 * g + j) * D:(4 * g + j + 1) * D] if g < 4 else
                           keys_s[:, j, :] if g == 4 else down_s[:, 4 * (g - 5) + j, :])
                    ins = nc.tensor.transpose(bank(6 + g % 2)[:, j * P:(j + 1) * P], src, ident[:, :])
                ins.then_inc(tr_ps, 1)
            pe.wait_ge(tr_done, START + 5)
            pe.wait_ge(ln_ready, START + NC)
            kv = keysT[:, :].rearrange("p (h k a) -> p h a k", h=EH, a=2)
            for a in range(2):
                for h in range(EH):
                    o = (a * EH + h) * NK
                    ins = mm(bank(4)[:, o:o + NK], wqT[:, 2 * h + a, :], kv[:, h, a, :])
            ins.then_inc(fold_ps, 1)
            pe.wait_ge(tr_done, START + 7)
            pe.wait_ge(x1_done, START + NC)

            norm(1, lambda c: chunk_of(XT, c))

            def key_scores(t, u):
                pe.wait_ge(xn_ready, t + (START + 1))
                pe.wait_ge(sim_ready, t + (START - 1))
                mm(bank(u), xn[:, u, :], fold[:, :]).then_inc(sim_ps, 1)

            for c in range(NC):
                if c == 2:
                    pe.wait_ge(fold_done, START + 1)
                    pe.wait_ge(nrm_ready, START + 2 * NC)
                    key_scores(0, 0)
                pe.wait_ge(h2sq_ready, START + c + 1)
                pe.wait_ge(rmsln_ready, START + c - 1)
                mm(bank(6 + c % 2), mean[:, :], sq_s[:, c % 2, :]).then_inc(ms_ready, 1)

            def hidden(t, u):
                pe.wait_ge(gelu_ready, t + START)
                for e in range(EB):
                    ins = mm(PS[:, 2 * CH + e * P:2 * CH + (e + 1) * P], downT[:, e * P:(e + 1) * P], xn[:, u, :])
                ins.then_inc(hid_ps, 1)

            def weights(t, heads):
                pe.wait_ge(weight_ready, t + START)
                for h in heads:
                    pe.wait_ge(kept_ready, t * EH + (START + h + 1))
                    for e in range(EB):
                        ins = add(PS[:, 4 * CH + e * P:4 * CH + (e + 1) * P], kept[h][:, e * P:(e + 1) * P],
                                  ident[:, :], start=(h == 0 and e % 4 == 0))
                    ins.then_inc(kept_used, 1)

            def experts_out(t, u):
                pe.wait_ge(hidw_ready, t + (START + 1))
                pe.wait_ge(x2_done, t + (START - 1))
                for e in range(EB):
                    ins = mm(bank(6 + u, TILE), up_s[:, e, :], hidw[:, e * P:(e + 1) * P], e == 0, e == EB - 1)
                ins.then_inc(eout_ps, 1)

            hidden(0, 0)
            key_scores(1, 1)
            weights(0, range(EH))
            hidden(1, 1)

            def peer(t, u, off, left):
                if left >= 2:
                    key_scores(t + 2, u)
                if left >= 1:
                    weights(t + 1, range(0, 2))
                if left == 0:
                    deviations(2, range(0, 2), lambda c: chunk_of(XT, c))
                experts_out(t, u)
                if left >= 1:
                    weights(t + 1, range(2, EH))
                if left >= 2:
                    hidden(t + 2, u)

            turns(pe, 0, 2, peer)

            mean_squares(2, range(0, 2))
            pe.wait_ge(x2_done, START + NT)
            deviations(2, range(2, 4), lambda c: chunk_of(XT, c))
            mean_squares(2, range(2, 4))
            pe.wait_ge(ld_w1, N_W1)
            pe.wait_ge(nrm_ready, START + 2 * NC + 2)

            def project_qk(t, u):
                pe.wait_ge(hc_ready, t + (START + 1))
                pe.wait_ge(qk_ready, t + (START - 1))
                mm(bank(u)[:, 0:TILE], wqkv1_s[:, 0:D], hc[:, u, :])
                mm(bank(u)[:, TILE:2 * TILE], wqkv1_s[:, D:2 * D], hc[:, u, :]).then_inc(qk1_ps, 1)

            def project_v(t, u):
                pe.wait_ge(v_ready, t + (START - 1))
                mm(bank(6 + u, TILE), hc[:, u, :], wqkv1_s[:, 2 * D:3 * D]).then_inc(v1_ps, 1)

            def scores(t, u):
                pe.wait_ge(qk_ready, t + (START + 1))
                pe.wait_ge(score_ready, t + (START - 1))
                mm(bank(2 + u)[:, 0:TILE], k1[:, u, :], q1[:, u, :])
                mm(bank(2 + u)[:, TILE:TILE + SPAN], k1[:, 1 - u, :], q1[:, u, 0:SPAN]).then_inc(score_ps, 1)

            def context(t, u):
                pe.wait_ge(score_ready, t + (START + 1))
                pe.wait_ge(v_ready, t + (START + 1))
                pe.wait_ge(ctx_done, t + (START - 1))
                o = bank(4 + u, TILE)
                mm(o, v1[:, u, :], sc[:, u, 0:TILE])
                add(o[:, 0:SPAN], v1[:, 1 - u, :], sc[:, u, TILE:TILE + SPAN]).then_inc(ctx_ps, 1)

            project_qk(0, 0)
            project_qk(1, 1)
            project_v(0, 0)
            pe.wait_ge(nrm_ready, START + 3 * NC)
            scores(0, 0)

            def band_attend(t, u, off, left):
                if left >= 1:
                    scores(t + 1, 1 - u)
                if left >= 2:
                    project_qk(t + 2, u)
                if left >= 1:
                    project_v(t + 1, 1 - u)
                context(t, u)

            turns(pe, 0, 2, band_attend)
            pe.wait_ge(ctx_done, START + NT)
            norm(3, lambda c: chunk_of(HT, c))
            norm(4, lambda c: chunk_of(XT, c), (x3_done, 0))
            pe.wait_ge(ln_ready, START + 5 * NC)
            pe.wait_ge(masks_ready, 1)

            for l in range(LAYERS):
                base = NT * l

                def project_qk(t, u):
                    pe.wait_ge(hs_ready, t + (START + 1))
                    pe.wait_ge(sq2_ready, t + START)
                    mm(bank(4), hc[:, u, :], wqkv_s[:, l, 0:INNER]).then_inc(q2_ps, 1)
                    pe.wait_ge(rot1_ready, t + START)
                    mm(bank(5), hc[:, u, :], wqkv_s[:, l, INNER:2 * INNER]).then_inc(qk2_ps, 1)

                def project_v(t, u):
                    pe.wait_ge(hv_ready, t + (START + 1))
                    pe.wait_ge(kT_ready, t + (START + 1))
                    mm(bank(7), hv[:, :], wqkv_s[:, l, 2 * INNER:3 * INNER]).then_inc(v2_ps, 1)

                def turn_qk(t):
                    pe.wait_ge(v2_ready, t + START)
                    for j, (b, ready, done) in enumerate(((3, rotq_ready, qT_ps), (7, rotk_ready, qkT_ps))):
                        pe.wait_ge(ready, t + (START + 1))
                        for g in range(H // 2):
                            o = j * INNER + g * P
                            ins = nc.tensor.transpose(bank(b)[:, g * P:(g + 1) * P], ra[:, o:o + P], ident[:, :])
                        ins.then_inc(done, 1)

                def masks(t, m):
                    pe.wait_ge(pT_ready, t + START)
                    pe.wait_ge(pTo_ready, t + START)
                    pe.wait_ge(pTw_ready, t + START)
                    for j in range(2):
                        if j:
                            pe.wait_ge(qT_ready, t + (START + 1))
                        for h in range(j, H, 2):
                            add(scores_of(h), ident_bf[:, :], keys_of(m, j), start=(place(h) % 2 == 0))

                def scores(t, u):
                    pe.wait_ge(qT_ready, t + (START + 1))
                    pe.wait_ge(kT_ready, t + (START + 1))
                    pe.wait_ge(kw_ready, t + START)
                    for j in range(2):
                        for h in range(j, H, 2):
                            rows = slice(DH * j, DH * j + DH)
                            ins = add(scores_of(h), qT[rows, h // 2, :], keys_of(kT[rows, u, h // 2, :], j))
                        ins.then_inc(sim2_ps, 1)

                def turn_p(t):
                    for j in range(3):
                        if j < 2:
                            pe.wait_ge(pn_ready, 2 * t + (START + j + 1))
                        for g in range(H // 2):
                            o = (0, TILE + 2 * WIN, TILE)[j]
                            ins = nc.tensor.transpose(bank(j)[:, g * P:(g + 1) * P], pr[:, g, o:o + P], ident[:, :])
                        ins.then_inc(pT_ps, 1)

                def weigh_v(t, u):
                    pe.wait_ge(v2_ready, t + (START + 1))
                    pe.wait_ge(vw_ready, t + START)
                    pe.wait_ge(zb_done, t + START)
                    for j in range(2):
                        pe.wait_ge((pT_ready, pTo_ready)[j], t + (START + 1))
                        for g in range(H // 2):
                            h = 2 * g + j
                            add(bank(6)[DH * j:DH * j + DH, g * P:(g + 1) * P], v2[:, u, h * DH:(h + 1) * DH],
                                pT[:, (H // 2) * j + g, :], start=(g == 0))
                    pe.wait_ge(pTw_ready, t + (START + 1))
                    plain(pe)
                    for j in range(2):
                        rows = slice(WIN * j, WIN * j + WIN)
                        for g in range(H // 2):
                            h = 2 * g + j
                            before = v2[rows, 1 - u, h * DH:(h + 1) * DH] if j else vw[:, u, g, :]
                            ins = add(bank(6)[DH * j:DH * j + DH, g * P:(g + 1) * P], before, pTw[rows, g, :])
                    ins.then_inc(pv_ps, 1)

                def project_o(t):
                    pe.wait_ge(oT_ready, t + (START + 1))
                    for g in range(INNER // P):
                        ins = mm(bank(6, TILE), wo_s[:, l, g, :], oT[:, g, :], g == 0, g == INNER // P - 1)
                    ins.then_inc(wo_ps, 1)

                project_qk(base, 0)
                if l:
                    pe.wait_ge(za_done, START + NC * l)
                project_qk(base + 1, 1)
                turn_qk(base)
                masks(base, mask0_bf)
                scores(base, 0)
                project_v(base, 0)
                project_qk(base + 2, 0)

                def attend(t, u, off, left):
                    turn_p(t)
                    if left >= 1:
                        turn_qk(t + 1)
                        masks(t + 1, mask_bf)
                        scores(t + 1, 1 - u)
                    weigh_v(t, u)
                    if left >= 1:
                        project_v(t + 1, 1 - u)
                    else:
                        deviations(5 + l, range(0, 2), lambda c: zs[:, c % 2, :], (zs_ready, NC * l))
                    if left >= 3:
                        project_qk(t + 3, 1 - u)
                    project_o(t)

                turns(pe, base, 3, attend)

                norm(5 + l, lambda c: zs[:, c % 2, :], (zs_ready, NC * l), begun=True)
                pe.wait_ge(ln_ready, START + (6 + l) * NC)

                def up(i):
                    c, b = i // 3, i % 3
                    o, m = HB[b]
                    pe.wait_ge(aff_ready, START + (5 + l) * NC + c + 1)
                    pe.wait_ge(hh_ready, START + 3 * NC * l + i - 1)
                    mm(PS[0:m, (4 + i % 2) * CH:(5 + i % 2) * CH], w1_s[:, l, o:o + m], chunk_of(HT, c))
                    mm(PS[0:m, (6 + i % 2) * CH:(7 + i % 2) * CH], w1_s[:, l, HID + o:HID + o + m],
                       chunk_of(HT, c)).then_inc(up_ps, 1)

                def down(c):
                    pe.wait_ge(nrm_ready, START + (6 + l) * NC)
                    pe.wait_ge(hh_ready, START + 3 * NC * l + 3 * c + 3)
                    pe.wait_ge(za_done, START + NC * l + c - 1)
                    for b, (o, m) in enumerate(HB):
                        ins = mm(bank(c % 2), w2_s[0:m, l, b, :], hh[0:m, b, :], b == 0, b == 2)
                    ins.then_inc(down_ps, 1)

                def turn_out(c):
                    pe.wait_ge(fin_ready, START + c + 1)
                    pe.wait_ge(fin_out, START + c - 1)
                    for j in range(CT):
                        ins = nc.tensor.transpose(bank(2 + c % 2)[:, j * TILE:(j + 1) * TILE],
                                                  fin[:, c % 2, j * TILE:(j + 1) * TILE], ident[:, :])
                    ins.then_inc(finT_ps, 1)

                for i in range(3 * NC):
                    up(i)
                    if i % 3 == 0 and i:
                        down(i // 3 - 1)
                    if l == LAYERS - 1 and i % 3 == 1 and i > 6:
                        turn_out(i // 3 - 2)
                down(NC - 1)
                if l == LAYERS - 1:
                    turn_out(NC - 2)
                    turn_out(NC - 1)


        @block.vector
        def _(dve):
            V = nc.vector
            n = [0]

            def step(ins):
                n[0] += 1
                ins.then_inc(dve_step, 1)
                dve.wait_ge(dve_step, n[0])

            dve.wait_ge(mod_ready, START + 1)
            step(V.tensor_copy(mod_raw[:, :], bank(7, 12)))
            step(V.tensor_copy(mod[:, :], mod_raw[:, :]))
            step(V.tensor_scalar(sgn[:, :], mod_raw[:, :], 0.0, 2.0, ALU.is_ge, ALU.mult))
            for l in range(2):
                for j in (1, 4):
                    V.tensor_scalar(mod[:, 6 * l + j:6 * l + j + 1], mod_raw[:, 6 * l + j:6 * l + j + 1], 1.0, None, ALU.add)
            step(V.tensor_scalar(sgn[:, :], sgn[:, :], -1.0, None, ALU.add))
            for op, s, b in ((ALU.mult, 1, ALU.max), (ALU.mult, 0, None)):
                for l in range(2):
                    for j in (2, 5):
                        o = 6 * l + j
                        if b is not None:
                            ins = V.tensor_scalar(mod[:, o:o + 1], mod_raw[:, o:o + 1], sgn[:, o:o + 1], 0.25, op, b)
                        else:
                            ins = V.tensor_tensor(mod[:, o:o + 1], mod[:, o:o + 1], sgn[:, o:o + 1], op)
                step(ins)
            V.tensor_copy(sgn[:, 0:1], mod[:, 0:1]).then_inc(mod_done, 1)
            dve.wait_ge(sig_ready, START + 1)
            dve.wait_ge(const_ready, 1)
            step(V.tensor_tensor(ema[:, 0:2], sig[:, 0:2], sig[:, 2:4], ALU.mult))
            V.tensor_tensor(ema[:, 2:4], sig[:, 0:2], cols[:, CB:CB + 2], ALU.mult)
            step(V.tensor_scalar(ema[:, 4:6], cols[:, CG:CG + 2], float(np.sqrt(0.5)), None, ALU.mult))
            V.tensor_scalar(ema[:, 0:2], ema[:, 0:2], -1.0, 1.0, ALU.mult, ALU.add)
            step(V.tensor_tensor(ema[:, 2:4], ema[:, 2:4], ema[:, 4:6], ALU.mult))

            def norm(n, pair):
                for c in range(n * NC + 2 * pair, n * NC + 2 * pair + 2):
                    dve.wait_ge(rstd_ready, START + c + 1)
                    dve.wait_ge(aff_ready, START + c - 1)
                    V.tensor_tensor(nrm[:, c % 2, :], bank(c % NC), rstd[:, c % 2, :], ALU.mult).then_inc(nrm_ready, 1)

            def ema_scan(c):
                u = c % 2
                dve.wait_ge(aff_ready, START + c + 1)
                h = HT[:, c * CH:(c + 1) * CH]
                dve.wait_ge(silu_ready, START + c - 1)
                dve.wait_ge(y_ready, START + c)
                V.tensor_tensor_scan(scan1[:, :], ema[:, 0:1].to_broadcast([P, CH]), h, ema[:, 6:7], ALU.mult, ALU.add)
                V.tensor_tensor_scan(scan2[:, :], ema[:, 1:2].to_broadcast([P, CH]), h, ema[:, 7:8], ALU.mult, ALU.add)
                step(V.tensor_scalar(ysum[:, u, :], h, cols[:, CO:CO + 1], None, ALU.mult))
                V.tensor_copy(ema[:, 6:7], scan1[:, CH - 1:CH])
                V.tensor_copy(ema[:, 7:8], scan2[:, CH - 1:CH])
                step(V.scalar_tensor_tensor(out=ysum[:, u, :], in0=scan1[:, :], scalar=ema[:, 2:3], in1=ysum[:, u, :],
                                            op0=ALU.mult, op1=ALU.add))
                V.scalar_tensor_tensor(out=ysum[:, u, :], in0=scan2[:, :], scalar=ema[:, 3:4], in1=ysum[:, u, :],
                                       op0=ALU.mult, op1=ALU.add).then_inc(y_ready, 1)

            def ema_out(c):
                dve.wait_ge(silu_ready, START + c + 1)
                xt = XT[:, c * CH:(c + 1) * CH]
                V.scalar_tensor_tensor(out=xt, in0=silu_s[:, c % 2, :], scalar=mod[:, 2:3], in1=xt,
                                       op0=ALU.mult, op1=ALU.add).then_inc(x1_done, 1)

            for c in range(NC):
                if c < 2:
                    norm(0, c)
                ema_scan(c)
                if c:
                    ema_out(c - 1)
            ema_out(NC - 1)

            norm(1, 0)
            norm(1, 1)

            def rms(pair):
                for c in range(2 * pair, 2 * pair + 2):
                    dve.wait_ge(rms_ready, START + c + 1)
                    V.scalar_tensor_tensor(out=HT[:, c * CH:(c + 1) * CH], in0=h2[:, c % 2, :], scalar=cols[:, CN:CN + 1],
                                           in1=rms_s[:, c % 2, :], op0=ALU.mult, op1=ALU.mult).then_inc(xn_done, 1)

            rms(0)

            before = n[0]
            PER = 13

            def residual(t, u, off):
                dve.wait_ge(eout_ps, t + (START + 1))
                xt = cols_at(XT, off, TILE)
                V.scalar_tensor_tensor(out=xt, in0=bank(6 + u, TILE), scalar=mod[:, 5:6], in1=xt,
                                       op0=ALU.mult, op1=ALU.add).then_inc(x2_done, 1)

            def peer(t, u, first=False, before_last=None):
                done = [0]

                def link(ins):
                    done[0] += 1
                    ins.then_inc(dve_step, 1)
                    dve.wait_ge(dve_step, t * PER + (before + done[0]))
                    if not first:
                        plain(dve)

                dve.wait_ge(sim_ready, t + (START + 1))
                if not first:
                    plain(dve)
                s = sims[:, u, :].rearrange("p (g k) -> p g k", k=NK)

                def stages(n, *ops):
                    due = [None, None]
                    for i, op in enumerate(ops):
                        for lot in range(2):
                            if due[lot] is not None:
                                dve.wait_ge(dve_step, t * PER + (before + due[lot]))
                                if not first:
                                    plain(dve)
                            for g in range(lot * n // 2, (lot + 1) * n // 2):
                                ins = op(g)
                            done[0] += 1
                            ins.then_inc(dve_step, 1)
                            due[lot] = done[0]
                    return due

                stages(2 * EH,
                       lambda g: V.max(srt[:, g, 0:8], s[:, g, :]),
                       lambda g: V.match_replace(out=rest[:, g, :], in_to_replace=srt[:, g, 0:8], in_values=s[:, g, :],
                                                 imm_value=LOWEST),
                       lambda g: V.max(srt[:, g, 8:16], rest[:, g, :]))
                if before_last is not None:
                    before_last()
                dve.wait_ge(dve_step, t * PER + (before + done[0]))
                if not first:
                    plain(dve)
                A, B = srt[:, 0:EH, :], srt[:, EH:2 * EH, :]
                o = 0
                for i in range(5):
                    m = TOPK // (i + 1)
                    V.tensor_tensor(cand[:, :, o:o + m], A[:, :, i:i + 1].to_broadcast([P, EH, m]), B[:, :, 0:m], ALU.add)
                    o += m
                V.tensor_tensor(cand[:, :, o:o + 6].rearrange("p h (i j) -> p h i j", j=2),
                                A[:, :, 5:8].unsqueeze(3).to_broadcast([P, EH, 3, 2]),
                                B[:, :, 0:2].unsqueeze(2).to_broadcast([P, EH, 3, 2]), ALU.add)
                o += 6
                link(V.tensor_tensor(cand[:, :, o:CAND], A[:, :, 8:16], B[:, :, 0:1].to_broadcast([P, EH, 8]), ALU.add))
                due = stages(EH,
                             lambda h: V.max(top[:, h, 0:8], cand[:, h, :]),
                             lambda h: V.match_replace(out=cand2[:, h, :], in_to_replace=top[:, h, 0:8],
                                                       in_values=cand[:, h, :], imm_value=LOWEST),
                             lambda h: V.max(top[:, h, 8:16], cand2[:, h, :]))
                assert done[0] == PER

                def threshold(lot):
                    heads = slice(lot * EH // 2, (lot + 1) * EH // 2)
                    dve.wait_ge(dve_step, t * PER + (before + due[lot]))
                    V.tensor_scalar(thr[:, heads], top[:, heads, TOPK - 1], 0.0, None, ALU.max).then_inc(thr_ready, 1)

                threshold(0)
                for h in range(EH):
                    if h == 1:
                        threshold(1)
                    if h in (0, EH // 2):
                        dve.wait_ge(thr_ready, 2 * t + (START + 1 + (h > 0)))
                    dve.wait_ge(sum_ready, t * EH + (START + h + 1))
                    dve.wait_ge(kept_used, t * EH + (START + h + 1 - EH))
                    V.scalar_tensor_tensor(out=kept[h], in0=sums[h], scalar=thr[:, h:h + 1],
                                           in1=sums[h], op0=ALU.is_ge, op1=ALU.mult).then_inc(kept_ready, 1)

            peer(0, 0, first=True, before_last=lambda: rms(1))
            peer(1, 1)
            with dve.Fori(1, NT // 2) as p:
                for u in range(2):
                    peer(2 * p + u, u,
                         before_last=lambda: residual(2 * p + (u - 2), u, (2 * p + (u - 2)) * TILE))
            residual(NT - 2, 0, (NT - 2) * TILE)
            residual(NT - 1, 1, (NT - 1) * TILE)
            n[0] = before + PER * NT

            norm(2, 0)
            norm(2, 1)
            dve.wait_ge(ld_late, N_LATE)
            dve.wait_ge(masks_ready, 1)

            def bias_v(t, u):
                dve.wait_ge(v1_ps, t + (START + 1))
                dve.wait_ge(ctx_ps, t + START)
                V.tensor_tensor(v1[:, u, :], bank(6 + u, TILE), bv_b[:, :], ALU.add).then_inc(v_ready, 1)

            def weigh_scores(t, u):
                dve.wait_ge(score_ps, t + (START + 1))
                dve.wait_ge(ctx_ps, t + (START - 1))
                V.scalar_tensor_tensor(out=sc[:, u, :], in0=bank(2 + u, TILE + SPAN), scalar=1.0 / float(np.sqrt(D * SPAN)),
                                       in1=band[:, :], op0=ALU.mult, op1=ALU.mult).then_inc(score_ready, 1)

            bias_v(0, 0)
            weigh_scores(0, 0)

            def band_attend(t, u, off, left):
                if left >= 1:
                    weigh_scores(t + 1, 1 - u)
                    bias_v(t + 1, 1 - u)

            turns(dve, 0, 1, band_attend)

            for pair in range(2):
                norm(3, pair)
                for c in range(2 * pair, 2 * pair + 2):
                    dve.wait_ge(aff_ready, START + 3 * NC + c + 1)
                    xt = XT[:, c * CH:(c + 1) * CH]
                    V.scalar_tensor_tensor(out=xt, in0=h2[:, c % 2, :], scalar=mod[:, 8:9], in1=xt,
                                           op0=ALU.mult, op1=ALU.add).then_inc(x3_done, 1)
            norm(4, 0)
            norm(4, 1)

            for l in range(LAYERS):
                base = NT * l
                dve.wait_ge(rot_ready, START + l + 1)
                q4 = PS[:, 4 * CH:6 * CH].rearrange("p (j h d) -> p j h d", j=2, h=H)
                a4 = ra[:, :].rearrange("p (j h d) -> p j h d", j=2, h=H)
                b4 = rb[:, :].rearrange("p (j h d) -> p j h d", j=2, h=H)
                hd = DH // 2

                def rotate(t, nt, halves=(0, 1)):
                    if 0 in halves:
                        dve.wait_ge(q2_ps, t + (START + 1))
                        dve.wait_ge(qT_ps, t + START)
                    tab = rotL[:, bass.ds(nt, 1), :].rearrange("p a (s j d) -> p (a s) j d", s=2, j=2)
                    for j in halves:
                        if j:
                            dve.wait_ge(sqk_ready, t + (START + 1))
                            dve.wait_ge(qkT_ps, t + START)
                        V.tensor_tensor(a4[:, j], q4[:, j], tab[:, 0, j:j + 1, :].to_broadcast([P, H, DH]), ALU.mult)
                        V.tensor_tensor(b4[:, j, :, 0:hd], q4[:, j, :, hd:DH],
                                        tab[:, 1, j:j + 1, 0:hd].to_broadcast([P, H, hd]), ALU.mult)
                        ins = V.tensor_tensor(b4[:, j, :, hd:DH], q4[:, j, :, 0:hd],
                                              tab[:, 1, j:j + 1, hd:DH].to_broadcast([P, H, hd]), ALU.mult)
                        ins.then_inc((rot0_ready, rot1_ready)[j], 1)

                def add_parts(t):
                    dve.wait_ge(rot1_ready, t + (START + 1))
                    V.tensor_tensor(ra[:, 0:INNER], ra[:, 0:INNER], rb[:, 0:INNER], ALU.add).then_inc(ra_ready, 1)

                def guard_squares(t):
                    dve.wait_ge(sssum_ready, t + (START + 1))
                    V.tensor_scalar(ss[:, :], ss[:, :], 1e-24, None, ALU.max).then_inc(ss_ready, 1)

                def sum_squares(t):
                    dve.wait_ge(half_ready, 2 * t + (START + 2))
                    V.tensor_reduce(ss[:, :], sq2[:, :].rearrange("p (g d) -> p g d", d=DH)[:, :, 0:DH // 4], AX_X,
                                    ALU.add).then_inc(sssum_ready, 1)

                def scale_q(t):
                    dve.wait_ge(ra_ready, t + (START + 1))
                    dve.wait_ge(r_ready, t + (START + 1))
                    v = ra[:, 0:INNER].rearrange("p (g d) -> p g d", d=DH)
                    V.tensor_tensor(v, v, rr[:, 0:H].unsqueeze(2).to_broadcast([P, H, DH]), ALU.mult).then_inc(rotq_ready, 1)

                def copy_qT(t):
                    dve.wait_ge(qT_ps, t + (START + 1))
                    V.tensor_copy(qT[:, :, :], bank(3).rearrange("p (a b) -> p a b", a=H // 2)).then_inc(qT_ready, 1)

                def maxima(t, j):
                    dve.wait_ge(sim2_ps, 2 * t + (START + j + 1))
                    s = PS[:, 2 * j * CH:(2 * j + 2) * CH].rearrange("p (b c) -> p b c", c=CH)[:, :, 0:2 * KEYS]
                    V.tensor_reduce(mx[:, 4 * j:4 * j + 4].rearrange("p (b e) -> p b e", e=2),
                                    s.rearrange("p b (e k) -> p b e k", k=KEYS), AX_X, ALU.max).then_inc(mx_ready, 1)
                    dve.wait_ge(mx_ready, 2 * t + (START + j + 1))
                    V.tensor_scalar(nmx[:, 4 * j:4 * j + 4], mx[:, 4 * j:4 * j + 4], -QK_SCALE, None,
                                    ALU.mult).then_inc(max_ready, 1)

                def copy_pT(t):
                    dve.wait_ge(pT_ps, 3 * t + (START + 2))
                    V.tensor_copy(pT[:, H // 2:H, :], bank(1).rearrange("p (a b) -> p a b", b=TILE)).then_inc(pTo_ready, 1)

                def inverses(t, j):
                    dve.wait_ge(p_ready, 2 * t + (START + j + 1))
                    V.reciprocal(rinv[:, 4 * j:4 * j + 4], rsum[:, 4 * j:4 * j + 4]).then_inc(rinv_ready, 1)

                def normalise(t, j):
                    dve.wait_ge(rinv_ready, 2 * t + (START + j + 1))
                    for h in range(j, H, 2):
                        p_h = pr[:, h // 2, j * KEYS:(j + 1) * KEYS]
                        ins = V.tensor_scalar(p_h, p_h, rinv[:, place(h):place(h) + 1], None, ALU.mult)
                    ins.then_inc(pn_ready, 1)

                def residual(t, off):
                    dve.wait_ge(wo_ps, t + (START + 1))
                    V.tensor_tensor(cols_at(ZB, off + 1, TILE), bank(6, TILE), cols_at(ZA, off + 1, TILE), ALU.add).then_inc(zb_done, 1)

                rotate(base, 0)
                add_parts(base)
                sum_squares(base)
                guard_squares(base)
                scale_q(base)
                copy_qT(base)
                rotate(base + 1, 1, (0,))
                maxima(base, 0)
                maxima(base, 1)
                rotate(base + 1, 1, (1,))
                inverses(base, 0)
                sum_squares(base + 1)
                normalise(base, 0)
                guard_squares(base + 1)
                inverses(base, 1)
                add_parts(base + 1)
                normalise(base, 1)
                scale_q(base + 1)

                def shift(c):
                    dve.wait_ge(zb_done, START + NT * l + CT * (c + 1))
                    dve.wait_ge(cen_ready, START + (5 + l) * NC + c - 1)
                    V.tensor_copy(zs[0:DH, c % 2, :], ZB[0:DH, c * CH + 1:(c + 1) * CH + 1])
                    V.tensor_copy(zs[DH:P, c % 2, :], ZB[DH:P, c * CH:(c + 1) * CH]).then_inc(zs_ready, 1)

                def attend(t, u, off, left):
                    copy_pT(t)
                    if left == 0:
                        shift(0)
                        shift(1)
                    if left >= 1:
                        copy_qT(t + 1)
                    if left >= 2:
                        rotate(t + 2, t + (2 - base))
                    if left >= 1:
                        maxima(t + 1, 0)
                        maxima(t + 1, 1)
                    if left >= 2:
                        add_parts(t + 2)
                        sum_squares(t + 2)
                    if left >= 1:
                        inverses(t + 1, 0)
                    if left >= 2:
                        guard_squares(t + 2)
                    if left >= 1:
                        normalise(t + 1, 0)
                        inverses(t + 1, 1)
                        normalise(t + 1, 1)
                    if left >= 2:
                        scale_q(t + 2)
                    residual(t, off)

                turns(dve, base, 2, attend)

                shift(2)
                shift(3)
                norm(5 + l, 0)
                norm(5 + l, 1)

                def add_down(c):
                    dve.wait_ge(down_ps, START + NC * l + c + 1)
                    V.scalar_tensor_tensor(out=ZA[:, c * CH + 1:(c + 1) * CH + 1], in0=bank(c % 2),
                                           scalar=cols[:, CB2 + l:CB2 + l + 1], in1=ZB[:, c * CH + 1:(c + 1) * CH + 1],
                                           op0=ALU.add, op1=ALU.add).then_inc(za_done, 1)
                    if l == LAYERS - 1:
                        dve.wait_ge(za_done, START + NC * l + c + 1)
                        dve.wait_ge(finT_ps, START + c - 1)
                        V.scalar_tensor_tensor(out=fin[:, c % 2, :], in0=ZA[:, c * CH + 1:(c + 1) * CH + 1],
                                               scalar=mod[:, 11:12], in1=XT[:, c * CH:(c + 1) * CH],
                                               op0=ALU.mult, op1=ALU.add).then_inc(fin_ready, 1)

                for i in range(3 * NC):
                    k, b, m = 3 * NC * l + i, i % 3, HB[i % 3][1]
                    if b == 0:
                        dve.wait_ge(down_ps, START + NC * l + i // 3)
                    dve.wait_ge(gate_ready, START + k + 1)
                    V.scalar_tensor_tensor(out=hh[0:m, b, :], in0=PS[0:m, (4 + i % 2) * CH:(5 + i % 2) * CH],
                                           scalar=b1_s[0:m, l, b:b + 1], in1=gate[0:m, b, :],
                                           op0=ALU.add, op1=ALU.mult).then_inc(hh_ready, 1)
                    if b == 0 and i:
                        add_down(i // 3 - 1)
                add_down(NC - 1)



def rotary_tables():
    f = np.float32
    half = np.arange(0, DH, 2, dtype=f)
    inv_freq = (f(1.0) / np.power(f(10000.0), half / f(DH))).astype(f)
    t = np.arange(T, dtype=f)
    freqs = t[:, None] * inv_freq[None, :]
    freqs = np.concatenate([freqs, freqs], -1)
    base = (half + f(0.4 * DH)) / f(1.4 * DH)
    power = (t - f(T // 2)) / f(WIN // 2)
    scale = np.power(base[None, :], power[:, None]).astype(f)
    scale = np.concatenate([scale, scale], -1)
    cos, sin = np.cos(freqs).astype(f), np.sin(freqs).astype(f)
    sin[:, :DH // 2] *= f(-1)
    return np.ascontiguousarray(np.concatenate([cos * scale, cos / scale, sin * scale, sin / scale], -1).astype(f))


_INS = ['L0_attn_x', 'L0_attn_delta', 'L0_attn_alpha', 'L0_attn_beta', 'L0_attn_gamma', 'L0_attn_omega',
        'L0_ffn_norm_w', 'L0_ffn_wq', 'L0_ffn_keys', 'L0_ffn_expert_down', 'L0_ffn_expert_up', 'L0_c', 'L0_wmod',
        'L1_attn_W_qkv', 'L1_attn_b_qkv', 'L1_attn_ln_w', 'L1_attn_ln_b', 'L1_ffn_wqkv', 'L1_ffn_q_scale',
        'L1_ffn_k_scale', 'L1_ffn_wo', 'L1_ffn_ln_g', 'L1_ffn_ln_b', 'L1_ffn_w1', 'L1_ffn_b1', 'L1_ffn_w2',
        'L1_ffn_b2', 'L1_c', 'L1_wmod']


def kernel(**inputs):
    import concourse.bacc as bacc
    from concourse.bass_utils import run_bass_kernel_spmd

    nc = bacc.Bacc("TRN2", target_bir_lowering=False, num_devices=1)
    arrays, args = {}, []
    given = [(name, np.ascontiguousarray(inputs[name])) for name in _INS] + [("rotary", rotary_tables())]
    for name, a in given:
        arrays[f"in_{name}"] = a
        args.append(nc.dram_tensor(f"in_{name}", a.shape, mybir.dt.from_np(a.dtype), kind="ExternalInput").ap())
    args.append(nc.dram_tensor("out_0", (1, T, D), F32, kind="ExternalOutput").ap())
    build(nc, *args)
    r = run_bass_kernel_spmd(nc, [arrays], core_ids=[0])
    return r.results[0]["out_0"]
```
